# Optimizing a Trainium2 kernel written in Bass

```python
import numpy as np
import jax
import jax.numpy as jnp

def _softmax(x, axis=-1):
    return jax.nn.softmax(x, axis=axis)

def _gelu(x):
    return jax.nn.gelu(x, approximate=True)

def _silu(x):
    return jax.nn.silu(x)

def _sigmoid(x):
    return jax.nn.sigmoid(x)

def _layernorm(x, axis=-1, eps=1e-05):
    m = jnp.mean(x, axis=axis, keepdims=True)
    v = jnp.var(x, axis=axis, keepdims=True)
    return (x - m) / jnp.sqrt(v + eps)

def _scatter_add(tgt, idx, src, axis=0):
    return tgt.at[idx].add(src)

def _segment_sum(src, seg, n):
    return jax.ops.segment_sum(src, seg, n)
kernel_name = 'mk_conv_preact_d2_conv_nchw384_r2_38612b'

def setup_inputs(seed: int=0):
    np.random.seed(seed)
    _w = jnp.asarray

    def _rec_inputs():
        import jax
        import jax.numpy as jnp
        _gk = jax.random.key(seed)
        x = -0.0001538 + 1 * jax.random.normal(jax.random.fold_in(_gk, 1), (4, 192, 32, 32), jnp.float32)
        return x
    x = _rec_inputs()

    def _L0_conv_setup():
        import jax, jax.numpy as jnp
        import numpy as np
        DIM = 192
        PD = 48
        QK = 16
        VD = PD
        QKV_OUT = 2 * QK + VD
        EPS = 1e-05

        def _bn(y, g, b, m, v):
            inv = g / jnp.sqrt(v + EPS)
            return y * inv[None, :, None, None] + (b - m * inv)[None, :, None, None]
        key = jax.random.key(seed)
        ks = jax.random.split(key, 12)
        B, H, W = (4, 32, 32)
        x = jax.random.normal(ks[0], (B, DIM, H, W), dtype=jnp.float32)
        ln_w = jnp.ones((PD,), jnp.float32)
        ln_b = jnp.zeros((PD,), jnp.float32)
        w_qkv = jax.random.normal(ks[1], (QKV_OUT, PD), jnp.float32) * 0.05
        bn1_g = jax.random.uniform(ks[2], (QKV_OUT,), jnp.float32, 0.5, 1.5)
        bn1_b = jax.random.normal(ks[3], (QKV_OUT,), jnp.float32) * 0.05
        bn1_m = jax.random.normal(ks[4], (QKV_OUT,), jnp.float32) * 0.05
        bn1_v = jax.random.uniform(ks[5], (QKV_OUT,), jnp.float32, 0.5, 1.5)
        w_proj = jax.random.normal(ks[6], (DIM, DIM), jnp.float32) * 0.02
        bn2_g = jax.random.uniform(ks[7], (DIM,), jnp.float32, 0.5, 1.5)
        bn2_b = jax.random.normal(ks[8], (DIM,), jnp.float32) * 0.05
        bn2_m = jax.random.normal(ks[9], (DIM,), jnp.float32) * 0.05
        bn2_v = jax.random.uniform(ks[10], (DIM,), jnp.float32, 0.5, 1.5)
        return {'x': x, 'ln_w': ln_w, 'ln_b': ln_b, 'w_qkv': w_qkv, 'bn1_g': bn1_g, 'bn1_b': bn1_b, 'bn1_m': bn1_m, 'bn1_v': bn1_v, 'w_proj': w_proj, 'bn2_g': bn2_g, 'bn2_b': bn2_b, 'bn2_m': bn2_m, 'bn2_v': bn2_v}
    _L0_conv_all = _L0_conv_setup()
    _L0_conv_in = {k: v for k, v in _L0_conv_all.items() if k in ('ln_w', 'ln_b', 'w_qkv', 'bn1_g', 'bn1_b', 'bn1_m', 'bn1_v', 'w_proj', 'bn2_g', 'bn2_b', 'bn2_m', 'bn2_v')}
    del _L0_conv_all

    def _L1_conv_setup():
        import jax, jax.numpy as jnp
        import numpy as np

        def conv2d(x, w, b=None, stride=1, padding=0, groups=1, dilation=1):
            out = jax.lax.conv_general_dilated(x, w, (stride, stride), [(padding, padding), (padding, padding)], rhs_dilation=(dilation, dilation), dimension_numbers=('NCHW', 'OIHW', 'NCHW'), feature_group_count=groups)
            if b is not None:
                out = out + b[None, :, None, None]
            return out

        def _l2norm(x, axis=-1, eps=1e-12):
            n = jnp.sqrt(jnp.sum(x * x, axis=axis, keepdims=True))
            return x / jnp.maximum(n, eps)
        B, C, H, W = (8, 192, 32, 32)
        heads = 8
        C6, C2, C4 = (C // 6, C // 2, C // 4)
        key = jax.random.key(seed)
        ks = iter(jax.random.split(key, 40))
        p = lambda shape: jax.random.normal(next(ks), shape, jnp.float32) * 0.02
        z = lambda n: jnp.zeros((n,), jnp.float32)
        inp = {'x': jax.random.normal(next(ks), (B, C, H, W), jnp.float32), 'temperature': jnp.ones((heads, 1, 1), jnp.float32), 'qkv_w': p((3 * C, C)), 'proj_w': p((C, C)), 'proj_b': z(C), 'dw1_w': p((C, C, 1, 1)), 'dw1_b': z(C), 'dw2_w': p((C, 1, 3, 3)), 'dw2_b': z(C), 'cp_in_w': p((C6, C, 1, 1)), 'cp_in_b': z(C6), 'ci1_w': p((C6, C6, 1, 1)), 'ci1_b': z(C6), 'ci2a_w': p((C6, 1, 3, 3)), 'ci2a_b': z(C6), 'ci2b_w': p((C6, 1, 7, 7)), 'ci2b_b': z(C6), 'ci2c_w': p((C6, C6, 1, 1)), 'ci2c_b': z(C6), 'cp_out_w': p((C, C6, 1, 1)), 'cp_out_b': z(C), 'sp_in_w': p((C2, C, 1, 1)), 'sp_in_b': z(C2), 'sp_dw_w': p((C2, 1, 3, 3)), 'sp_dw_b': z(C2), 'sp_out_w': p((C, C4, 1, 1)), 'sp_out_b': z(C)}
        return inp
    _L1_conv_all = _L1_conv_setup()
    _L1_conv_in = {k: v for k, v in _L1_conv_all.items() if k in ('temperature', 'qkv_w', 'proj_w', 'proj_b', 'dw1_w', 'dw1_b', 'dw2_w', 'dw2_b', 'cp_in_w', 'cp_in_b', 'ci1_w', 'ci1_b', 'ci2a_w', 'ci2a_b', 'ci2b_w', 'ci2b_b', 'ci2c_w', 'ci2c_b', 'cp_out_w', 'cp_out_b', 'sp_in_w', 'sp_in_b', 'sp_dw_w', 'sp_dw_b', 'sp_out_w', 'sp_out_b')}
    del _L1_conv_all
    return {'x': x, 'L0_conv_ln_w': _L0_conv_in['ln_w'], 'L0_conv_ln_b': _L0_conv_in['ln_b'], 'L0_conv_w_qkv': _L0_conv_in['w_qkv'], 'L0_conv_bn1_g': _L0_conv_in['bn1_g'], 'L0_conv_bn1_b': _L0_conv_in['bn1_b'], 'L0_conv_bn1_m': _L0_conv_in['bn1_m'], 'L0_conv_bn1_v': _L0_conv_in['bn1_v'], 'L0_conv_w_proj': _L0_conv_in['w_proj'], 'L0_conv_bn2_g': _L0_conv_in['bn2_g'], 'L0_conv_bn2_b': _L0_conv_in['bn2_b'], 'L0_conv_bn2_m': _L0_conv_in['bn2_m'], 'L0_conv_bn2_v': _L0_conv_in['bn2_v'], 'L1_conv_temperature': _L1_conv_in['temperature'], 'L1_conv_qkv_w': _L1_conv_in['qkv_w'], 'L1_conv_proj_w': _L1_conv_in['proj_w'], 'L1_conv_proj_b': _L1_conv_in['proj_b'], 'L1_conv_dw1_w': _L1_conv_in['dw1_w'], 'L1_conv_dw1_b': _L1_conv_in['dw1_b'], 'L1_conv_dw2_w': _L1_conv_in['dw2_w'], 'L1_conv_dw2_b': _L1_conv_in['dw2_b'], 'L1_conv_cp_in_w': _L1_conv_in['cp_in_w'], 'L1_conv_cp_in_b': _L1_conv_in['cp_in_b'], 'L1_conv_ci1_w': _L1_conv_in['ci1_w'], 'L1_conv_ci1_b': _L1_conv_in['ci1_b'], 'L1_conv_ci2a_w': _L1_conv_in['ci2a_w'], 'L1_conv_ci2a_b': _L1_conv_in['ci2a_b'], 'L1_conv_ci2b_w': _L1_conv_in['ci2b_w'], 'L1_conv_ci2b_b': _L1_conv_in['ci2b_b'], 'L1_conv_ci2c_w': _L1_conv_in['ci2c_w'], 'L1_conv_ci2c_b': _L1_conv_in['ci2c_b'], 'L1_conv_cp_out_w': _L1_conv_in['cp_out_w'], 'L1_conv_cp_out_b': _L1_conv_in['cp_out_b'], 'L1_conv_sp_in_w': _L1_conv_in['sp_in_w'], 'L1_conv_sp_in_b': _L1_conv_in['sp_in_b'], 'L1_conv_sp_dw_w': _L1_conv_in['sp_dw_w'], 'L1_conv_sp_dw_b': _L1_conv_in['sp_dw_b'], 'L1_conv_sp_out_w': _L1_conv_in['sp_out_w'], 'L1_conv_sp_out_b': _L1_conv_in['sp_out_b']}

def reference(x, L0_conv_ln_w, L0_conv_ln_b, L0_conv_w_qkv, L0_conv_bn1_g, L0_conv_bn1_b, L0_conv_bn1_m, L0_conv_bn1_v, L0_conv_w_proj, L0_conv_bn2_g, L0_conv_bn2_b, L0_conv_bn2_m, L0_conv_bn2_v, L1_conv_temperature, L1_conv_qkv_w, L1_conv_proj_w, L1_conv_proj_b, L1_conv_dw1_w, L1_conv_dw1_b, L1_conv_dw2_w, L1_conv_dw2_b, L1_conv_cp_in_w, L1_conv_cp_in_b, L1_conv_ci1_w, L1_conv_ci1_b, L1_conv_ci2a_w, L1_conv_ci2a_b, L1_conv_ci2b_w, L1_conv_ci2b_b, L1_conv_ci2c_w, L1_conv_ci2c_b, L1_conv_cp_out_w, L1_conv_cp_out_b, L1_conv_sp_in_w, L1_conv_sp_in_b, L1_conv_sp_dw_w, L1_conv_sp_dw_b, L1_conv_sp_out_w, L1_conv_sp_out_b):
    import jax
    import jax.numpy as jnp

    def _L0_conv_ref(x, ln_w, ln_b, w_qkv, bn1_g, bn1_b, bn1_m, bn1_v, w_proj, bn2_g, bn2_b, bn2_m, bn2_v):
        import jax, jax.numpy as jnp
        import numpy as np
        DIM = 192
        PD = 48
        QK = 16
        VD = PD
        QKV_OUT = 2 * QK + VD
        EPS = 1e-05

        def _bn(y, g, b, m, v):
            inv = g / jnp.sqrt(v + EPS)
            return y * inv[None, :, None, None] + (b - m * inv)[None, :, None, None]
        B, C, H, W = x.shape
        N = H * W
        scale = QK ** (-0.5)
        x_attn = x[:, :PD]
        x_skip = x[:, PD:]
        u = x_attn.mean(axis=1, keepdims=True)
        s = ((x_attn - u) ** 2).mean(axis=1, keepdims=True)
        xn = (x_attn - u) / jnp.sqrt(s + EPS)
        xn = xn * ln_w[None, :, None, None] + ln_b[None, :, None, None]
        qkv = jnp.einsum('oc,bchw->bohw', w_qkv, xn)
        qkv = _bn(qkv, bn1_g, bn1_b, bn1_m, bn1_v)
        q = qkv[:, :QK].reshape(B, QK, N)
        k = qkv[:, QK:2 * QK].reshape(B, QK, N)
        v = qkv[:, 2 * QK:].reshape(B, VD, N)
        attn = jax.nn.softmax(jnp.einsum('bcn,bcm->bnm', q, k) * scale, axis=-1)
        out = jnp.einsum('bcn,bmn->bcm', v, attn).reshape(B, VD, H, W)
        xm = jax.nn.relu(jnp.concatenate([out, x_skip], axis=1))
        y = jnp.einsum('oc,bchw->bohw', w_proj, xm)
        y = _bn(y, bn2_g, bn2_b, bn2_m, bn2_v)
        return y

    def _L1_conv_ref(x, temperature, qkv_w, proj_w, proj_b, dw1_w, dw1_b, dw2_w, dw2_b, cp_in_w, cp_in_b, ci1_w, ci1_b, ci2a_w, ci2a_b, ci2b_w, ci2b_b, ci2c_w, ci2c_b, cp_out_w, cp_out_b, sp_in_w, sp_in_b, sp_dw_w, sp_dw_b, sp_out_w, sp_out_b):
        import jax, jax.numpy as jnp
        import numpy as np

        def conv2d(x, w, b=None, stride=1, padding=0, groups=1, dilation=1):
            out = jax.lax.conv_general_dilated(x, w, (stride, stride), [(padding, padding), (padding, padding)], rhs_dilation=(dilation, dilation), dimension_numbers=('NCHW', 'OIHW', 'NCHW'), feature_group_count=groups)
            if b is not None:
                out = out + b[None, :, None, None]
            return out

        def _l2norm(x, axis=-1, eps=1e-12):
            n = jnp.sqrt(jnp.sum(x * x, axis=axis, keepdims=True))
            return x / jnp.maximum(n, eps)
        B, C, H, W = x.shape
        N = H * W
        heads = temperature.shape[0]
        hd = C // heads
        C6 = cp_in_w.shape[0]
        C2 = sp_in_w.shape[0]
        xf = x.reshape(B, C, N).transpose(0, 2, 1)
        qkv = xf @ qkv_w.T
        qkv = qkv.reshape(B, N, 3, heads, hd).transpose(2, 0, 3, 1, 4)
        q = qkv[0].swapaxes(-2, -1)
        k = qkv[1].swapaxes(-2, -1)
        v = qkv[2].swapaxes(-2, -1)
        v_ = v.reshape(B, C, H, W)
        q = _l2norm(q, axis=-1)
        k = _l2norm(k, axis=-1)
        attn = jnp.einsum('bhcn,bhdn->bhcd', q, k) * temperature
        attn = jax.nn.softmax(attn, axis=-1)
        at = jnp.einsum('bhcd,bhdn->bhcn', attn, v)
        attened = at.transpose(0, 3, 1, 2).reshape(B, N, C)
        conv_x = conv2d(conv2d(v_, dw1_w, dw1_b), dw2_w, dw2_b, padding=1, groups=C)
        ar = attened.swapaxes(-2, -1).reshape(B, C, H, W)
        t = conv2d(ar, cp_in_w, cp_in_b)
        ci1 = conv2d(t.mean((2, 3), keepdims=True), ci1_w, ci1_b)
        ci2 = conv2d(t, ci2a_w, ci2a_b, padding=1, groups=C6)
        ci2 = conv2d(ci2, ci2b_w, ci2b_b, padding=9, groups=C6, dilation=3)
        ci2 = conv2d(ci2, ci2c_w, ci2c_b)
        channel_map = conv2d(t * ci1 * ci2, cp_out_w, cp_out_b)
        attened = attened + channel_map.transpose(0, 2, 3, 1).reshape(B, N, C)
        cm = channel_map.mean((2, 3), keepdims=True)
        sp = conv2d(conv_x, sp_in_w, sp_in_b)
        d = conv2d(sp, sp_dw_w, sp_dw_b, padding=1, groups=C2)
        x1, x2 = jnp.split(d, 2, axis=1)
        sp = conv2d(jax.nn.gelu(x1, approximate=False) * x2, sp_out_w, sp_out_b)
        spatial_map = sp.transpose(0, 2, 3, 1).reshape(B, N, C)
        attened = attened * jax.nn.sigmoid(spatial_map)
        conv_x = conv_x * jax.nn.sigmoid(cm)
        conv_x = conv_x.transpose(0, 2, 3, 1).reshape(B, N, C)
        out = (attened + conv_x) @ proj_w.T + proj_b
        return out.transpose(0, 2, 1).reshape(B, C, H, W)

    def _gn(v, G=32, eps=1e-05):
        B_, C_, H_, W_ = v.shape
        g = v.reshape(B_, G, C_ // G, H_, W_)
        m = jnp.mean(g, axis=(2, 3, 4), keepdims=True)
        s = jnp.var(g, axis=(2, 3, 4), keepdims=True)
        return ((g - m) / jnp.sqrt(s + eps)).reshape(v.shape)

    def _ln_c(v, eps=1e-06):
        m = jnp.mean(v, axis=1, keepdims=True)
        s = jnp.var(v, axis=1, keepdims=True)
        return (v - m) / jnp.sqrt(s + eps)

    def _ln_t(v, eps=1e-05):
        m = jnp.mean(v, axis=-1, keepdims=True)
        s = jnp.var(v, axis=-1, keepdims=True)
        return (v - m) / jnp.sqrt(s + eps)

    def _to_tokens(v):
        B_, C_, H_, W_ = v.shape
        return v.reshape(B_, C_, H_ * W_).transpose(0, 2, 1)

    def _from_tokens(t, like):
        B_, C_, H_, W_ = like.shape
        return t.transpose(0, 2, 1).reshape(B_, C_, H_, W_)
    x = x + _L0_conv_ref(_gn(x), L0_conv_ln_w, L0_conv_ln_b, L0_conv_w_qkv, L0_conv_bn1_g, L0_conv_bn1_b, L0_conv_bn1_m, L0_conv_bn1_v, L0_conv_w_proj, L0_conv_bn2_g, L0_conv_bn2_b, L0_conv_bn2_m, L0_conv_bn2_v)
    x = x + _L1_conv_ref(_gn(x), L1_conv_temperature, L1_conv_qkv_w, L1_conv_proj_w, L1_conv_proj_b, L1_conv_dw1_w, L1_conv_dw1_b, L1_conv_dw2_w, L1_conv_dw2_b, L1_conv_cp_in_w, L1_conv_cp_in_b, L1_conv_ci1_w, L1_conv_ci1_b, L1_conv_ci2a_w, L1_conv_ci2a_b, L1_conv_ci2b_w, L1_conv_ci2b_b, L1_conv_ci2c_w, L1_conv_ci2c_b, L1_conv_cp_out_w, L1_conv_cp_out_b, L1_conv_sp_in_w, L1_conv_sp_in_b, L1_conv_sp_dw_w, L1_conv_sp_dw_b, L1_conv_sp_out_w, L1_conv_sp_out_b)
    return x

_drawn_inputs = setup_inputs


def setup_inputs(seed=0):
    import zlib

    import numpy as np

    out = dict(_drawn_inputs(seed))
    spreads = {'L0_conv_ln_w': (1.0, 0.6),
     'L0_conv_ln_b': (0.0, 0.8),
     'L1_conv_temperature': (1.0, 0.6),
     'L1_conv_proj_b': (0.0, 0.1),
     'L1_conv_dw1_b': (0.0, 0.8),
     'L1_conv_dw2_b': (0.0, 0.723),
     'L1_conv_cp_in_b': (0.0, 0.8),
     'L1_conv_ci1_b': (0.0, 0.8),
     'L1_conv_ci2a_b': (0.0, 0.8),
     'L1_conv_ci2b_b': (0.0, 0.8),
     'L1_conv_ci2c_b': (0.0, 0.8),
     'L1_conv_cp_out_b': (0.0, 0.728),
     'L1_conv_sp_in_b': (0.0, 0.8),
     'L1_conv_sp_dw_b': (0.0, 0.8),
     'L1_conv_sp_out_b': (0.0, 0.8)}
    factors = {'L0_conv_w_qkv': 8.0,
     'L0_conv_bn1_g': 8.0,
     'L0_conv_bn1_b': 8.0,
     'L0_conv_bn1_m': 8.0,
     'L0_conv_bn1_v': 8.0,
     'L1_conv_qkv_w': 7.335,
     'L1_conv_proj_w': 2.987,
     'L1_conv_dw1_w': 8.0,
     'L1_conv_dw2_w': 8.0,
     'L1_conv_cp_in_w': 8.0,
     'L1_conv_ci1_w': 8.0,
     'L1_conv_ci2a_w': 8.0,
     'L1_conv_ci2b_w': 8.0,
     'L1_conv_ci2c_w': 8.0,
     'L1_conv_cp_out_w': 8.0,
     'L1_conv_sp_in_w': 8.0,
     'L1_conv_sp_dw_w': 8.0,
     'L1_conv_sp_out_w': 8.0}
    for name, (base, spread) in spreads.items():
        noise = np.random.default_rng([zlib.crc32(name.encode()), seed]).standard_normal(out[name].shape)
        drawn = base * np.exp(spread * noise) if base else spread * noise
        out[name] = jnp.asarray(drawn.astype(out[name].dtype))
    for name, factor in factors.items():
        out[name] = (out[name] * factor).astype(out[name].dtype)
    return out
```

```python
from contextlib import ExitStack

import numpy as np

import concourse.bass as bass
from concourse import mybir

F32 = mybir.dt.float32
F32R = mybir.dt.float32r
ALU = mybir.AluOpType
ACT = mybir.ActivationFunctionType
AX_X = mybir.AxisListType.X

B, C, HH, WW = 4, 192, 32, 32
N = HH * WW
P = 128
CH = C // 2
GROUP = C // 32
PD, QK = 48, 16
QKV = 2 * QK + PD
NKT = N // P
HB = N // 2
QB = N // 4
C6 = C // 6
HD = C // 8
EPS = 1e-5
PW = WW + 2
UW = WW + 18
SP2 = 64
SPN = SP2 + PD
MASKED = -1e30
FILLS = 8

FIRST = {
    "ident": (P, P), "gavg": (CH, CH), "center": (PD, CH), "mean48": (PD, 1), "ones": (P, CH),
    "e48": (PD + 1, 1), "ln_w": (PD, 1), "ln_b": (PD, 1), "wqkvT": (PD, QKV),
    "bn1": (QKV, 4), "wproj": (CH, 2 * C), "bn2": (CH, 8),
}
SECOND = {
    "wqkT": (CH, 2 * 2 * C), "wv": (CH, 2 * C), "wdw1T": (CH, 2 * C), "wcpT": (CH, 2 * C6),
    "row_dw1_b": (CH + 1, C), "row_cp_in_b": (CH + 1, C6), "row_cp_out_b": (CH + 1, C),
    "wdw2": (CH, 2 * 9), "bdw2": (CH, 2), "temp": (CH, 2), "mask": (CH, CH),
    "w_ci1": (P, P), "b_ci1": (P, 1), "w_ci2a": (CH, 3 * C6), "b_ci2a": (P, 1),
    "ci2cT": (P, C6), "w_ci2b": (P, 14), "ci2cT_rep": (C6, P), "b_ci2b": (C6, 1), "b_ci2c": (P, 1),
    "wcoT": (P, C), "half_biases": (CH, 4), "w_spi": (CH, 2 * SPN), "b_spi": (SPN, 1),
    "w_spdw": (SPN, 9), "b_spdw": (SPN, 1), "w_spo": (SPN, C), "w_pr": (CH, 2 * C), "b_pr": (CH, 2),
}


def place(blocks, start):
    at = {}
    for name, (parts, cols) in blocks.items():
        at[name] = (parts, start, cols)
        start += cols
    return at, start


AT1, N1 = place(FIRST, 0)
AT2, NW = place(SECOND, N1)
AT = {**AT1, **AT2}


class Signal:

    def __init__(self, sem, per, before=0):
        self.sem, self.per, self.before = sem, per, before

    def at(self, b, k):
        return b * self.per + (k + self.before)


def build(nc, x, params, out):
    with ExitStack() as ctx:
        def sb(name, shape, dt=F32):
            return ctx.enter_context(nc.sbuf_tensor(name, shape, dt))

        def psum(name, shape):
            return ctx.enter_context(nc.psum_tensor(name, shape, F32))

        def sem(name):
            return ctx.enter_context(nc.semaphore(name))

        def sig(name, per, before=0):
            return Signal(sem(name), per, before)

        psA = psum("psA", [P, N])
        psB = psum("psB", [P, N])
        psO = psum("psO", [P, HB])
        R = [psum(f"psR{i}", [P, HB]) for i in range(3)]

        wt = sb("wt", [P, NW])

        def par(name):
            parts, off, cols = AT[name]
            return wt[0:parts, off:off + cols]

        def par2(name):
            return par(name).rearrange("p (h c) -> p h c", h=2)

        ident, ones = par("ident"), par("ones")
        lnmat = sb("lnmat", [PD, PD + 1])
        mhalf = sb("mhalf", [P, NKT])
        var1 = sb("var1", [QKV, 1])
        isd1 = sb("isd1", [QKV, 1])
        inv1 = sb("inv1", [QKV, 1])
        sh1 = sb("sh1", [QKV, 1])
        wl = sb("wl", [QKV, PD + 1])
        q3w = sb("q3w", [PD + 1, CH])
        k3w = sb("k3w", [PD + 1, CH])
        v1w = sb("v1w", [PD + 1, PD + 1])
        var2 = sb("var2", [CH, 2])
        isd2 = sb("isd2", [CH, 2])
        inv2 = sb("inv2", [CH, 2])
        dinv2 = sb("dinv2", [CH, 2, CH])
        bias2 = sb("bias2", [CH, 2])
        wp2 = sb("wp2", [CH, 2, C])
        wc1 = sb("wc1", [CH + 1, 2, C])
        wb = sb("wb", [P, 14, C6])
        bci2 = sb("bci2", [P, 1])
        hbias = sb("hbias", [CH, 4])
        wph = sb("wph", [CH, 2, C])

        xt = sb("xt", [CH, 2, N])
        st6 = [sb(f"st6_{i}", [CH, 8, 3]) for i in range(2)]
        mv = [sb(f"mv_{i}", [CH, 2, 8]) for i in range(2)]
        msq = [sb(f"msq_{i}", [CH, 8]) for i in range(2)]
        gm = [sb(f"gm_{i}", [CH, 2, 2]) for i in range(2)]
        gsq = [sb(f"gsq_{i}", [CH, 2]) for i in range(2)]
        gvar = [sb(f"gvar_{i}", [CH, 2]) for i in range(2)]
        gr = [sb(f"gr_{i}", [CH, 2]) for i in range(2)]
        gb = [sb(f"gb_{i}", [CH, 2]) for i in range(2)]
        xa = sb("xa", [PD, N])
        sq = sb("sq", [PD, N])
        pv8 = sb("pv8", [P, NKT])
        rT = sb("rT", [P, NKT])
        dg = sb("dg", [P, NKT, P])
        rb = sb("rb", [PD, N])
        xn = sb("xn", [64, N])
        qs = sb("qs", [P, N], F32R)
        ks = sb("ks", [P, N], F32R)
        vt = sb("vt", [P, NKT, PD + 1])
        nm = sb("nm", [P, NKT])
        nmr = sb("nmr", [P, NKT, 2], F32R)
        pT = [sb(f"pT{i}", [P, N]) for i in range(2)]
        osb = sb("osb", [PD + 1, N])
        xm = sb("xm", [CH, 2, N])
        x2 = sb("x2", [CH, 2, N])

        X = sb("X", [CH + 1, 2, N])
        xr = sb("xr", [CH, 2, N])
        cp = sb("cp", [CH, 2, PW, PW])
        cx = sb("cx", [CH, 2, N])
        xT = sb("xT", [P, NKT, C])
        gram = sb("gram", [CH, 2, C])
        tu = sb("tu", [CH, 2, 2 * C])
        prd = sb("prd", [CH, 2, 2 * C])
        nrm = sb("nrm", [CH, 4])
        rn = sb("rn", [CH, 4])
        dk = sb("dk", [CH, 2, CH])
        rk = sb("rk", [CH, 2, CH])
        rq = sb("rq", [CH, 2])
        s1 = sb("s1", [CH, 2, CH])
        s2 = sb("s2", [CH, 2, CH])
        smx = sb("smx", [CH, 2])
        se = sb("se", [CH, 2, CH])
        ssum = sb("ssum", [CH, 2])
        srec = sb("srec", [CH, 2])
        attn = sb("attn", [CH, 2, CH])
        attT = sb("attT", [CH, 2, CH])
        wmt = sb("wmt", [CH + 1, 2, C])
        wma = sb("wma", [CH, 2, C])
        wmc = sb("wmc", [CH + 1, 2, C6])
        t4 = sb("t4", [P, QB])
        tsum = sb("tsum", [P, 1])
        tp = sb("tp", [CH, PW * PW])
        up = sb("up", [P, UW * UW])
        ci1 = sb("ci1", [P, 1])
        wco = sb("wco", [P, C])
        pr4 = sb("pr4", [P, N])
        psm = sb("psm", [P, 1])
        gate = sb("gate", [CH, 2])
        gate2 = sb("gate2", [CH, 2])
        spp = sb("spp", [SPN, PW, PW])
        dd = sb("dd", [SPN, N])
        gl = sb("gl", [SPN, N])
        gmul = gl
        th = sb("th", [CH, 2, N])
        uu = sb("uu", [CH, 2, N])
        zz = uu
        oo = sb("oo", [CH, 2, N])

        s_w1, s_w2 = sem("params1_loaded"), sem("params2_loaded")
        s_fill, s_rows = sem("constants_filled"), sem("rows_of_ones")
        s_isd = sem("setup_rsqrt")
        s_ln = sem("lnmat_ready")
        s_su_pe = sem("setup_products")
        s_su = sem("setup_vector_steps")

        x_in = sig("x_in", 16)
        gst = [sig(f"channel_stats_{i}", 7) for i in range(2)]
        gav = [sig(f"group_means_{i}", 1) for i in range(2)]
        gmm = [sig(f"group_steps_{i}", 4) for i in range(2)]
        grr = [sig(f"group_rstd_{i}", 1) for i in range(2)]
        xa_s = sig("attended_normed", 1)
        xm_s = sig("relu_normed", 2)
        xc_s = sig("centered", 1)
        sq_s = sig("squares", 1)
        var_s = sig("pixel_vars", 1)
        pv_s = sig("pixel_vars_copied", 1)
        rT_s = sig("pixel_rstd", 1)
        dg_s = sig("diagonals", 2)
        rbp_s = sig("rstd_rows", 1)
        rb_s = sig("rstd_rows_copied", 1)
        xn_s = sig("layer_normed", 1)
        qkp_s = sig("qkv_products", 3)
        qk_s = sig("qk_high_parts", 2)
        ql_s = sig("qk_low_parts", 2)
        vt_s = sig("vT_copied", 1)
        mx_s = sig("score_rows", NKT)
        nm_s = sig("row_max_steps", NKT + 2)
        tm_s = sig("max_rows", 1)
        qm_s = sig("max_rows_copied", 1)
        st_s = sig("scores_t", NKT)
        ex_s = sig("exps", NKT)
        pvd_s = sig("pv_done", NKT)
        oc_s = sig("attn_out_copied", 2)
        dn_s = sig("denominators", 1)
        dr_s = sig("denominators_inverted", 1)
        db_s = sig("denominator_rows", 1)
        xo_s = sig("attn_relu", 1)
        y_s = sig("proj1", 2)
        x2_s = sig("block1_out", 2)

        X_s = sig("normed2", 2)
        xr_s = sig("residual_biased", 2)
        c1_s = sig("conv1_product", 4)
        ce_s = sig("conv1_padded", 4)
        cf_s = sig("conv2_first_tap", 2)
        cv_s = sig("conv2_taps", 16)
        xtp_s = sig("xT_product", 4)
        xte_s = sig("xT_copied", 4)
        gp_s = sig("gram_product", 1)
        ge_s = sig("gram_copied", 1)
        tup_s = sig("tu_product", 2)
        tue_s = sig("tu_copied", 2)
        prd_s = sig("tu_times_w", 1)
        kn_s = sig("norms_product", 1)
        nrm_s = sig("norms_clamped", 1)
        rn_s = sig("inverse_norms", 1)
        dk_s = sig("k_norm_diagonals", 2)
        kr_s = sig("k_norm_rows", 1)
        rk_s = sig("k_norm_rows_copied", 1)
        sc_s = sig("head_scores", 1)
        sm_s = sig("head_softmax_steps", 8)
        se_s = sig("head_exps", 2)
        at_s = sig("attn_transposed", 1)
        ate_s = sig("attn_transposed_copied", 1)
        mp_s = sig("attn_wv_products", 3)
        mte_s = sig("wmt_copied", 1)
        mae_s = sig("wma_copied", 1)
        mce_s = sig("wmc_copied", 1)
        tt_s = sig("t_product", 1)
        t4_s = sig("t_copied", 1)
        tpc_s = sig("t_padded", 4)
        tpd_s = sig("t_shifted_copies", 32)
        ca_s = sig("ci2a_product", 1)
        ue_s = sig("ci2a_padded", 4)
        ud_s = sig("ci2a_shifted_copies", 48)
        cip_s = sig("ci1_product", 1)
        ci_s = sig("ci1_steps", 2)
        cb_s = sig("ci2_product", 1)
        pr_s = sig("channel_product", 4)
        cm_s = sig("channel_map_mean", 1)
        gt_s = sig("gate_tanh", 2)
        g2_s = sig("gate_plus_one", 1)
        spi_s = sig("sp_in_product", 2)
        spe_s = sig("sp_in_padded", 2)
        df_s = sig("sp_first_tap", 1)
        dv_s = sig("sp_conv", 16)
        gl_s = sig("gelu", 1)
        gu_s = sig("gelu_times_x2", 1)
        spo_s = sig("sp_out_product", 4)
        th_s = sig("spatial_tanh", 4)
        ap_s = sig("attended_product", 4)
        uu_s = sig("attended_gated", 4)
        zz_s = sig("merged", 2)
        op_s = sig("proj2", 4)
        oo_s = sig("out_copied", 4, before=1)
        st_out = sig("out_stored", 64, before=1)

        bn1 = par("bn1")
        bn2 = par("bn2").rearrange("p (f h) -> p f h", f=4)

        def row(name):
            _, off, cols = AT[name]
            return wt[CH:CH + 1, off:off + cols]

        def halves(ps):
            return [ps[:, 0:HB], ps[:, HB:N]]

        block = ctx.enter_context(nc.Block())

        @block.sync
        def _(sp):
            sp.dma_start(wt[:, 0:N1], params[:, 0:N1]).then_inc(s_w1, 16)

            def load_x(b):
                sp.dma_start(xt[:], x[b].rearrange("h c n -> c h n")).then_inc(x_in.sem, 16)

            def shift_t(c):
                sp.wait_ge(tpc_s.sem, tpc_s.at(c, 4))
                for j in (1, 2):
                    n = PW * PW - j
                    sp.dma_start(tp[j * C6:(j + 1) * C6, 0:n], tp[0:C6, j:j + n]).then_inc(tpd_s.sem, 16)

            def shift_u(c):
                sp.wait_ge(ue_s.sem, ue_s.at(c, 4))
                for j in (1, 2, 3):
                    n = UW * UW - 3 * j
                    sp.dma_start(up[j * C6:(j + 1) * C6, 0:n], up[0:C6, 3 * j:3 * j + n]).then_inc(ud_s.sem, 16)

            def store(c):
                for k in range(4):
                    h, n = divmod(k, 2)
                    sp.wait_ge(oo_s.sem, oo_s.at(c, k + 1))
                    sp.dma_start(out[c, h, :, n * HB:(n + 1) * HB],
                                 oo[:, h, n * HB:(n + 1) * HB]).then_inc(st_out.sem, 16)

            load_x(0)
            sp.dma_start(wt[:, N1:NW], params[:, N1:NW]).then_inc(s_w2, 16)
            with sp.Fori(1, B) as i:
                sp.wait_ge(x2_s.sem, x2_s.at(i, 0))
                load_x(i)
                shift_t(i - 1)
                shift_u(i - 1)
                store(i - 1)
            shift_t(B - 1)
            shift_u(B - 1)
            store(B - 1)
            sp.wait_ge(st_out.sem, st_out.at(B - 1, 64))

        @block.tensor
        def _(pe):
            mm = nc.tensor.matmul

            def setup():
                pe.wait_ge(s_w1, 16)
                pe.wait_ge(s_ln, 2)
                mm(psA[0:QKV, 0:PD + 1], par("wqkvT"), lnmat[:], start=True, stop=True).then_inc(s_su_pe, 1)
                pe.wait_ge(s_su, 8)
                mm(psB[0:PD + 1, 0:QKV], wl[:], ident[0:QKV, 0:QKV], start=True, stop=True).then_inc(s_su_pe, 1)
                wp = par2("wproj")
                for k in range(2):
                    for h in range(2):
                        last = mm(psA[0:CH, k * C + h * CH:k * C + (h + 1) * CH], wp[:, h, k * CH:(k + 1) * CH],
                                  dinv2[:, h, :], start=True, stop=True)
                last.then_inc(s_su_pe, 1)

            def setup2():
                pe.wait_ge(s_w2, 16)
                wv, wd = par2("wv"), par2("wdw1T")
                for jh in range(2):
                    for h in range(2):
                        last = mm(R[0][0:CH, jh * C:(jh + 1) * C], wv[:, h, jh * CH:(jh + 1) * CH],
                                  wd[:, h, :], start=(h == 0), stop=(h == 1))
                last.then_inc(s_su_pe, 1)
                mm(R[1][:, 0:1], par("ci2cT_rep"), par("b_ci2b"), start=True, stop=True).then_inc(s_su_pe, 1)

            def group_means(i, b, ps):
                pe.wait_ge(gst[i].sem, gst[i].at(b, 7))
                mm(ps[0:CH, 0:16], par("gavg"), mv[i][:].rearrange("p s k -> p (s k)"),
                   start=True, stop=True).then_inc(gav[i].sem, 1)

            def center(b):
                pe.wait_ge(xa_s.sem, xa_s.at(b, 1))
                for n in range(2):
                    last = mm(psA[0:CH, n * HB:(n + 1) * HB], par("center"), xa[:, n * HB:(n + 1) * HB],
                              start=True, stop=True)
                last.then_inc(xc_s.sem, 1)

            def pixel_var(b):
                pe.wait_ge(sq_s.sem, sq_s.at(b, 1))
                for t in range(NKT):
                    last = mm(psB[:, t:t + 1], sq[:, t * P:(t + 1) * P], par("mean48"), start=True, stop=True)
                last.then_inc(var_s.sem, 1)

            def spread(b, k, done):
                pe.wait_ge(dg_s.sem, dg_s.at(b, k))
                for n in range(2):
                    last = mm(psB[0:PD, n * HB:(n + 1) * HB], ones[:, 0:PD], dg[:, n * 4:(n + 1) * 4, :],
                              start=True, stop=True)
                last.then_inc(done.sem, 1)

            def qkv(b):
                pe.wait_ge(xn_s.sem, xn_s.at(b, 1))
                for w, ps in ((q3w, psB), (k3w, psA)):
                    for n in range(2):
                        last = mm(ps[0:CH, n * HB:(n + 1) * HB], w[:], xn[0:PD + 1, n * HB:(n + 1) * HB],
                                  start=True, stop=True)
                    last.then_inc(qkp_s.sem, 1)
                for t in range(NKT):
                    last = mm(psO[:, t * 64:t * 64 + PD + 1], xn[0:PD + 1, t * P:(t + 1) * P], v1w[:],
                              start=True, stop=True)
                last.then_inc(qkp_s.sem, 1)

            def score_rows(b, t):
                if t == 0:
                    pe.wait_ge(qk_s.sem, qk_s.at(b, 2))
                    pe.wait_ge(ql_s.sem, ql_s.at(b, 2))
                if t >= 2:
                    pe.wait_ge(nm_s.sem, nm_s.at(b, t - 1))
                ps = (psA, psB)[t % 2]
                for n in range(2):
                    last = mm(ps[:, n * HB:(n + 1) * HB], qs[0:CH, t * P:(t + 1) * P],
                              ks[0:CH, n * HB:(n + 1) * HB], start=True, stop=True)
                last.then_inc(mx_s.sem, 1)

            def max_rows(b):
                pe.wait_ge(nm_s.sem, nm_s.at(b, NKT + 2))
                for t in range(NKT):
                    last = nc.tensor.transpose(psB[0:2, t * P:(t + 1) * P], nmr[:, t, :].bitcast(F32), ident)
                last.then_inc(tm_s.sem, 1)

            def scores_t(b, t):
                if t == 0:
                    pe.wait_ge(qm_s.sem, qm_s.at(b, 1))
                if t >= 2:
                    pe.wait_ge(ex_s.sem, ex_s.at(b, t - 1))
                ps = (psA, psB)[t % 2]
                for n in range(2):
                    last = mm(ps[:, n * HB:(n + 1) * HB], ks[0:CH + 2, t * P:(t + 1) * P],
                              qs[0:CH + 2, n * HB:(n + 1) * HB], start=True, stop=True)
                last.then_inc(st_s.sem, 1)

            def pv(b, t):
                if t == 0:
                    pe.wait_ge(vt_s.sem, vt_s.at(b, 1))
                pe.wait_ge(ex_s.sem, ex_s.at(b, t + 1))
                for n in range(2):
                    last = mm(psO[64 * n:64 * n + PD + 1, :], vt[:, t, :], pT[t % 2][:, n * HB:(n + 1) * HB],
                              start=(t == 0), stop=(t == NKT - 1))
                last.then_inc(pvd_s.sem, 1)

            def denominators(b):
                pe.wait_ge(oc_s.sem, oc_s.at(b, 2))
                for t in range(NKT):
                    last = mm(psA[:, t:t + 1], osb[:, t * P:(t + 1) * P], par("e48"), start=True, stop=True)
                last.then_inc(dn_s.sem, 1)

            def proj1(b):
                pe.wait_ge(xo_s.sem, xo_s.at(b, 1))
                for h in range(2):
                    ps = (psA, psB)[h]
                    for n in range(2):
                        for k in range(2):
                            last = mm(ps[0:CH, n * HB:(n + 1) * HB], wp2[:, k, h * CH:(h + 1) * CH],
                                      xm[:, k, n * HB:(n + 1) * HB], start=(k == 0), stop=(k == 1))
                    last.then_inc(y_s.sem, 1)

            def conv1(c):
                pe.wait_ge(X_s.sem, X_s.at(c, 2))
                for k in range(4):
                    h, n = divmod(k, 2)
                    if k == 3:
                        pe.wait_ge(ce_s.sem, ce_s.at(c, 1))
                    ps = R[(1, 2, 0, 1)[k]]
                    mm(ps[0:CH, :], wc1[0:CH + 1, 0, h * CH:(h + 1) * CH], X[0:CH + 1, 0, n * HB:(n + 1) * HB],
                       start=True, stop=False)
                    mm(ps[0:CH, :], wc1[0:CH, 1, h * CH:(h + 1) * CH], X[0:CH, 1, n * HB:(n + 1) * HB],
                       start=False, stop=True).then_inc(c1_s.sem, 1)

            def transpose_x(c):
                for k in range(4):
                    if k < 3:
                        pe.wait_ge(ce_s.sem, ce_s.at(c, k + 2))
                    else:
                        pe.wait_ge(xte_s.sem, xte_s.at(c, 1))
                    ps = R[(2, 0, 1, 2)[k]]
                    for j in range(4):
                        t, h = 2 * k + j // 2, j % 2
                        last = nc.tensor.transpose(ps[:, j * CH:(j + 1) * CH], X[0:CH, h, t * P:(t + 1) * P],
                                                   ident[0:CH, 0:CH])
                    last.then_inc(xtp_s.sem, 1)

            def gram_x(c):
                pe.wait_ge(xte_s.sem, xte_s.at(c, 4))
                for h in range(2):
                    for t in range(NKT):
                        last = mm(R[0][0:CH, h * C:(h + 1) * C], xT[:, t, h * CH:(h + 1) * CH], xT[:, t, :],
                                  start=(t == 0), stop=(t == NKT - 1))
                last.then_inc(gp_s.sem, 1)

            def gram_w(c):
                pe.wait_ge(ge_s.sem, ge_s.at(c, 1))
                wqk = par2("wqkT")
                for jh in range(2):
                    for k in range(2):
                        last = mm(R[1 + jh][0:CH, 0:2 * C], gram[:, k, jh * CH:(jh + 1) * CH], wqk[:, k, :],
                                  start=(k == 0), stop=(k == 1))
                    last.then_inc(tup_s.sem, 1)

            def head_scores(c):
                pe.wait_ge(tue_s.sem, tue_s.at(c, 2))
                wqk = par2("wqkT")
                for h in range(2):
                    for jh in range(2):
                        last = mm(R[1][0:CH, h * CH:(h + 1) * CH], tu[:, jh, h * CH:(h + 1) * CH],
                                  wqk[:, jh, C + h * CH:C + (h + 1) * CH], start=(jh == 0), stop=(jh == 1))
                last.then_inc(sc_s.sem, 1)

            def norms(c):
                pe.wait_ge(prd_s.sem, prd_s.at(c, 1))
                for k in range(4):
                    for jh in range(2):
                        last = mm(R[0][0:CH, k:k + 1], prd[:, jh, k * CH:(k + 1) * CH], ones[0:CH, 0:1],
                                  start=(jh == 0), stop=(jh == 1))
                last.then_inc(kn_s.sem, 1)

            def k_norm_rows(c):
                pe.wait_ge(dk_s.sem, dk_s.at(c, 2))
                for h in range(2):
                    last = mm(R[2][0:CH, h * CH:(h + 1) * CH], ones[0:CH, :], dk[:, h, :], start=True, stop=True)
                last.then_inc(kr_s.sem, 1)

            def transpose_attn(c):
                pe.wait_ge(sm_s.sem, sm_s.at(c, 8))
                for h in range(2):
                    last = nc.tensor.transpose(R[2][0:CH, h * CH:(h + 1) * CH], attn[:, h, :], ident[0:CH, 0:CH])
                last.then_inc(at_s.sem, 1)

            def attn_weights(c):
                pe.wait_ge(ate_s.sem, ate_s.at(c, 1))
                wv = par2("wv")
                for h in range(2):
                    last = mm(R[1][0:CH, h * C:(h + 1) * C], attT[:, h, :], wv[:, h, :], start=True, stop=True)
                last.then_inc(mp_s.sem, 1)
                for jh in range(2):
                    for h in range(2):
                        last = mm(R[0][0:CH, jh * C + h * CH:jh * C + (h + 1) * CH],
                                  wv[:, h, jh * CH:(jh + 1) * CH], attT[:, h, :], start=True, stop=True)
                last.then_inc(mp_s.sem, 1)
                pe.wait_ge(mae_s.sem, mae_s.at(c, 1))
                wcp = par2("wcpT")
                for jh in range(2):
                    for h in range(2):
                        last = mm(R[2][0:CH, jh * C6:(jh + 1) * C6], wma[:, h, jh * CH:(jh + 1) * CH],
                                  wcp[:, h, :], start=(h == 0), stop=(h == 1))
                last.then_inc(mp_s.sem, 1)

            def t_product(c):
                pe.wait_ge(mte_s.sem, mte_s.at(c, 1))
                pe.wait_ge(mce_s.sem, mce_s.at(c, 1))
                for jh in range(2):
                    kk = CH + 1 if jh == 0 else CH
                    for q in range(4):
                        last = mm(R[0][q * C6:(q + 1) * C6, 0:QB], wmc[0:kk, jh, :],
                                  X[0:kk, jh, q * QB:(q + 1) * QB], start=(jh == 0), stop=(jh == 1))
                last.then_inc(tt_s.sem, 1)

            def ci1_product(c):
                pe.wait_ge(t4_s.sem, t4_s.at(c, 1))
                mm(R[2][:, 0:1], par("w_ci1"), tsum[:], start=True, stop=True).then_inc(cip_s.sem, 1)

            def ci2a(c):
                pe.wait_ge(tpd_s.sem, tpd_s.at(c, 32))
                w = par("w_ci2a").rearrange("p (y o) -> p y o", y=3)
                img = tp[:].rearrange("p (y x) -> p y x", x=PW)
                for dy in range(3):
                    for q in range(4):
                        last = mm(R[1][q * C6:(q + 1) * C6, 0:QB], w[:, dy, :],
                                  img[:, q * 8 + dy:q * 8 + dy + 8, 0:WW], start=(dy == 0), stop=(dy == 2))
                last.then_inc(ca_s.sem, 1)

            def ci2b(c):
                pe.wait_ge(ud_s.sem, ud_s.at(c, 48))
                img = up[:].rearrange("p (y x) -> p y x", x=UW)
                for g in range(14):
                    dy, second = divmod(g, 2)
                    kk = 3 * C6 if second else P
                    for q in range(4):
                        y0 = q * 8 + 3 * dy
                        last = mm(R[0][q * C6:(q + 1) * C6, 0:QB], wb[0:kk, g, :],
                                  img[0:kk, y0:y0 + 8, 12 * second:12 * second + WW],
                                  start=(g == 0), stop=(g == 13))
                last.then_inc(cb_s.sem, 1)

            def map_mean(c):
                pe.wait_ge(pr_s.sem, pr_s.at(c, 4))
                pe.wait_ge(ci_s.sem, ci_s.at(c, 2))
                for h in range(2):
                    last = mm(R[2][0:CH, h:h + 1], wco[:, h * CH:(h + 1) * CH], psm[:], start=True, stop=True)
                last.then_inc(cm_s.sem, 1)

            def sp_in(c):
                pe.wait_ge(cv_s.sem, cv_s.at(c, 16))
                pe.wait_ge(gt_s.sem, gt_s.at(c, 2))
                w = par2("w_spi")
                for n in range(2):
                    for k in range(2):
                        last = mm(R[1 + n][0:SPN, :], w[:, k, :], cx[:, k, n * HB:(n + 1) * HB],
                                  start=(k == 0), stop=(k == 1))
                    last.then_inc(spi_s.sem, 1)

            def sp_out(c):
                pe.wait_ge(gu_s.sem, gu_s.at(c, 1))
                for k in range(4):
                    h, n = divmod(k, 2)
                    if k == 3:
                        pe.wait_ge(th_s.sem, th_s.at(c, 1))
                    mm(R[(0, 1, 2, 0)[k]][0:CH, :], par("w_spo")[SP2:SPN, h * CH:(h + 1) * CH],
                       gmul[SP2:SPN, n * HB:(n + 1) * HB], start=True, stop=True).then_inc(spo_s.sem, 1)

            def attended(c):
                for k in range(4):
                    h, n = divmod(k, 2)
                    if k < 3:
                        pe.wait_ge(th_s.sem, th_s.at(c, k + 2))
                    else:
                        pe.wait_ge(uu_s.sem, uu_s.at(c, 1))
                    ps = R[(1, 2, 0, 1)[k]]
                    mm(ps[0:CH, :], wmt[0:CH + 1, 0, h * CH:(h + 1) * CH], X[0:CH + 1, 0, n * HB:(n + 1) * HB],
                       start=True, stop=False)
                    mm(ps[0:CH, :], wmt[0:CH, 1, h * CH:(h + 1) * CH], X[0:CH, 1, n * HB:(n + 1) * HB],
                       start=False, stop=False)
                    mm(ps[0:CH, :], wco[:, h * CH:(h + 1) * CH], pr4[:, n * HB:(n + 1) * HB],
                       start=False, stop=True).then_inc(ap_s.sem, 1)

            def proj2(c):
                pe.wait_ge(zz_s.sem, zz_s.at(c, 2))
                for k in range(4):
                    h, n = divmod(k, 2)
                    if k < 3:
                        pe.wait_ge(uu_s.sem, uu_s.at(c, k + 2))
                    else:
                        pe.wait_ge(oo_s.sem, oo_s.at(c, 1))
                    for j in range(2):
                        last = mm(R[(2, 0, 1, 2)[k]][0:CH, :], wph[:, j, h * CH:(h + 1) * CH],
                                  zz[:, j, n * HB:(n + 1) * HB], start=(j == 0), stop=(j == 1))
                    last.then_inc(op_s.sem, 1)

            def block1_a(b):
                group_means(0, b, psB)
                center(b)
                pixel_var(b)
                spread(b, 1, rbp_s)
                qkv(b)

            def block1_b(b):
                for t in range(NKT):
                    score_rows(b, t)
                max_rows(b)

            def block1_c(b):
                scores_t(b, 0)
                for t in range(NKT):
                    if t + 1 < NKT:
                        scores_t(b, t + 1)
                    pv(b, t)

            def block1_d(b):
                denominators(b)
                spread(b, 2, db_s)
                proj1(b)

            def block2_a(c):
                group_means(1, c, R[0])
                conv1(c)
                transpose_x(c)
                gram_x(c)
                gram_w(c)
                head_scores(c)
                norms(c)

            def block2_b(c):
                k_norm_rows(c)
                transpose_attn(c)
                attn_weights(c)
                t_product(c)
                ci1_product(c)

            def block2_c(c):
                ci2a(c)
                ci2b(c)
                map_mean(c)
                sp_in(c)

            def block2_d(c):
                sp_out(c)
                attended(c)
                proj2(c)

            setup()
            pe.wait_ge(s_su, 9)
            block1_a(0)
            block1_b(0)
            block1_c(0)
            block1_d(0)
            setup2()
            pe.wait_ge(s_su, 15)
            pe.wait_ge(s_fill, FILLS)
            with pe.Fori(1, B) as i:
                pe.wait_ge(x2_s.sem, x2_s.at(i, 0))
                pe.wait_ge(oo_s.sem, oo_s.at(i - 1, 0))
                block2_a(i - 1)
                block1_a(i)
                block2_b(i - 1)
                block1_b(i)
                block2_c(i - 1)
                block1_c(i)
                block2_d(i - 1)
                block1_d(i)
            pe.wait_ge(x2_s.sem, x2_s.at(B, 0))
            pe.wait_ge(oo_s.sem, oo_s.at(B - 1, 0))
            block2_a(B - 1)
            block2_b(B - 1)
            block2_c(B - 1)
            block2_d(B - 1)

        @block.vector
        def _(dve):
            v = nc.vector

            def setup():
                v.memset(ks[CH:CH + 2, :].bitcast(F32), 1.0).then_inc(s_rows, 1)
                v.memset(X[CH:CH + 1, :, :], 1.0).then_inc(s_rows, 1)
                dve.wait_ge(s_rows, 2)
                dve.wait_ge(s_fill, 1)
                dve.wait_ge(s_w1, 16)
                v.tensor_scalar(lnmat[:, 0:PD], ident[0:PD, 0:PD], par("ln_w"), None, ALU.mult).then_inc(s_ln, 1)
                v.tensor_copy(lnmat[:, PD:PD + 1], par("ln_b")).then_inc(s_ln, 1)
                v.tensor_scalar(var1[:], bn1[:, 3:4], EPS, None, ALU.add).then_inc(s_su, 1)
                v.tensor_scalar(var2[:], bn2[:, 3, :], EPS, None, ALU.add).then_inc(s_su, 1)
                dve.wait_ge(s_isd, 2)
                v.tensor_tensor(inv1[:], bn1[:, 0:1], isd1[:], ALU.mult).then_inc(s_su, 1)
                v.tensor_tensor(inv2[:], bn2[:, 0, :], isd2[:], ALU.mult).then_inc(s_su, 1)
                dve.wait_ge(s_su, 4)
                dve.wait_ge(s_su_pe, 1)
                v.tensor_scalar(wl[:], psA[0:QKV, 0:PD + 1], inv1[:, 0:1], None, ALU.mult).then_inc(s_su, 1)
                for h in range(2):
                    v.tensor_scalar(dinv2[:, h, :], ident[0:CH, 0:CH], inv2[:, h:h + 1], None, ALU.mult)
                v.tensor_tensor(bias2[:], bn2[:, 2, :], inv2[:], ALU.mult)
                v.scalar_tensor_tensor(sh1[:], bn1[:, 2:3], inv1[:, 0:1], bn1[:, 1:2], ALU.mult, ALU.subtract).then_inc(s_su, 1)
                dve.wait_ge(s_su, 6)
                v.tensor_tensor(bias2[:], bn2[:, 1, :], bias2[:], ALU.subtract).then_inc(s_su, 1)
                v.tensor_tensor(wl[:, PD:PD + 1], wl[:, PD:PD + 1], sh1[:], ALU.subtract).then_inc(s_su, 1)
                v.memset(q3w[:], 0.0)
                v.memset(k3w[:], 0.0)
                v.tensor_copy(v1w[:, PD:PD + 1], par("e48")).then_inc(s_ln, 1)
                dve.wait_ge(s_ln, 3)
                dve.wait_ge(s_su_pe, 2)
                for j in range(3):
                    v.tensor_scalar(q3w[:, 32 * j:32 * j + QK], psB[0:PD + 1, 0:QK], QK ** -0.5, None, ALU.mult)
                    v.tensor_copy(k3w[:, 32 * j:32 * j + QK], psB[0:PD + 1, QK:2 * QK])
                v.tensor_copy(v1w[:, 0:PD], psB[0:PD + 1, 2 * QK:QKV])
                dve.wait_ge(s_su_pe, 3)
                v.tensor_copy(wp2[:], psA[0:CH, 0:2 * C].rearrange("p (k c) -> p k c", k=2)).then_inc(s_su, 1)

            def setup2():
                dve.wait_ge(s_w2, 16)
                dve.wait_ge(s_su_pe, 5)
                v.tensor_copy(wc1[0:CH, :, :], R[0][0:CH, 0:2 * C].rearrange("p (h c) -> p h c", h=2)).then_inc(s_su, 1)
                v.tensor_tensor(bci2[:], R[1][:, 0:1], par("b_ci2c"), ALU.add).then_inc(s_su, 1)
                v.tensor_tensor(wb[:], par("ci2cT").unsqueeze(1).broadcast_to([P, 14, C6]),
                                par("w_ci2b").unsqueeze(2).broadcast_to([P, 14, C6]), ALU.mult).then_inc(s_su, 1)
                v.tensor_scalar(hbias[:], par("half_biases"), 0.5, None, ALU.mult).then_inc(s_su, 1)
                v.tensor_scalar(wph[:], par2("w_pr"), 0.5, None, ALU.mult).then_inc(s_su, 1)
                v.tensor_copy(wc1[CH:CH + 1, 0, :], row("row_dw1_b"))
                v.tensor_copy(wmt[CH:CH + 1, 0, :], row("row_cp_out_b"))
                v.tensor_copy(wmc[CH:CH + 1, 0, :], row("row_cp_in_b")).then_inc(s_su, 1)

            def channel_stats(i, b, src):
                s = gst[i]
                for k in range(4):
                    h, n = divmod(k, 2)
                    v.bn_stats(st6[i][:, 2 * k:2 * k + 2, :], src[:, h, n * HB:(n + 1) * HB]).then_inc(s.sem, 1)
                dve.wait_ge(s.sem, s.at(b, 4))
                v.tensor_copy(mv[i][:, 0, :], st6[i][:, :, 1]).then_inc(s.sem, 1)
                v.tensor_tensor(msq[i][:], st6[i][:, :, 1], st6[i][:, :, 1], ALU.mult).then_inc(s.sem, 1)
                dve.wait_ge(s.sem, s.at(b, 6))
                v.scalar_tensor_tensor(mv[i][:, 1, :], st6[i][:, :, 2], 2.0 / HB, msq[i][:],
                                       ALU.mult, ALU.add).then_inc(s.sem, 1)

            def group_stats(i, b, ps):
                s = gmm[i]
                dve.wait_ge(gav[i].sem, gav[i].at(b, 1))
                v.tensor_reduce(gm[i][:], ps[0:CH, 0:16].rearrange("p (s h k) -> p s h k", s=2, h=2),
                                AX_X, ALU.add).then_inc(s.sem, 1)
                dve.wait_ge(s.sem, s.at(b, 1))
                v.tensor_tensor(gsq[i][:], gm[i][:, 0, :], gm[i][:, 0, :], ALU.mult).then_inc(s.sem, 1)
                dve.wait_ge(s.sem, s.at(b, 2))
                v.scalar_tensor_tensor(gvar[i][:], gm[i][:, 1, :], EPS, gsq[i][:], ALU.add, ALU.subtract).then_inc(s.sem, 1)
                dve.wait_ge(grr[i].sem, grr[i].at(b, 1))
                v.scalar_tensor_tensor(gb[i][:], gm[i][:, 0, :], -1.0, gr[i][:], ALU.mult, ALU.mult).then_inc(s.sem, 1)

            def diagonals(b, k, src):
                v.tensor_tensor(dg[:], ident.unsqueeze(1).broadcast_to([P, NKT, P]),
                                src[:].unsqueeze(2).broadcast_to([P, NKT, P]), ALU.mult).then_inc(dg_s.sem, 1)

            def pixel_rstd(b):
                dve.wait_ge(var_s.sem, var_s.at(b, 1))
                v.tensor_scalar(pv8[:], psB[:, 0:NKT], EPS, None, ALU.add).then_inc(pv_s.sem, 1)
                dve.wait_ge(rT_s.sem, rT_s.at(b, 1))
                diagonals(b, 1, rT)
                dve.wait_ge(rb_s.sem, rb_s.at(b, 1))
                v.tensor_tensor(xn[0:PD, :], psA[0:PD, :], rb[:], ALU.mult).then_inc(xn_s.sem, 1)

            def low_parts(b):
                dve.wait_ge(qk_s.sem, qk_s.at(b, 1))
                v.tensor_tensor(qs[32:64, :], psB[32:64, :], qs[32:64, :].bitcast(F32), ALU.subtract).then_inc(ql_s.sem, 1)
                dve.wait_ge(qk_s.sem, qk_s.at(b, 2))
                v.tensor_tensor(ks[64:96, :], psA[64:96, :], ks[64:96, :].bitcast(F32), ALU.subtract).then_inc(ql_s.sem, 1)
                dve.wait_ge(qkp_s.sem, qkp_s.at(b, 3))
                v.tensor_copy(vt[:], psO[:].rearrange("p (t c) -> p t c", c=64)[:, :, 0:PD + 1]).then_inc(vt_s.sem, 1)

            def row_max(b, t):
                dve.wait_ge(mx_s.sem, mx_s.at(b, t + 1))
                v.tensor_reduce(nm[:, t:t + 1], (psA, psB)[t % 2][:], AX_X, ALU.max, negate=True).then_inc(nm_s.sem, 1)

            def split_max(b):
                dve.wait_ge(nm_s.sem, nm_s.at(b, NKT))
                v.tensor_copy(nmr[:, :, 0], nm[:]).then_inc(nm_s.sem, 1)
                dve.wait_ge(nm_s.sem, nm_s.at(b, NKT + 1))
                v.tensor_tensor(nmr[:, :, 1], nm[:], nmr[:, :, 0].bitcast(F32), ALU.subtract).then_inc(nm_s.sem, 1)

            def attn_out(b):
                dve.wait_ge(pvd_s.sem, pvd_s.at(b, NKT))
                v.tensor_copy(osb[:, HB:N], psO[64:64 + PD + 1, :]).then_inc(oc_s.sem, 1)
                dve.wait_ge(dn_s.sem, dn_s.at(b, 1))
                v.reciprocal(rT[:], psA[:, 0:NKT]).then_inc(dr_s.sem, 1)
                dve.wait_ge(dr_s.sem, dr_s.at(b, 1))
                diagonals(b, 2, rT)
                dve.wait_ge(db_s.sem, db_s.at(b, 1))
                dve.wait_ge(xm_s.sem, xm_s.at(b, 2))
                v.scalar_tensor_tensor(xm[0:PD, 0, :], osb[0:PD, :], 0.0, psB[0:PD, :], ALU.max, ALU.mult).then_inc(xo_s.sem, 1)

            def block1_out(b):
                for h in range(2):
                    dve.wait_ge(y_s.sem, y_s.at(b, h + 1))
                    v.scalar_tensor_tensor(x2[:, h, :], (psA, psB)[h][0:CH, :], bias2[:, h:h + 1], xt[:, h, :],
                                           ALU.add, ALU.add).then_inc(x2_s.sem, 1)

            def normed(c):
                dve.wait_ge(gmm[1].sem, gmm[1].at(c, 4))
                for h in range(2):
                    v.tensor_scalar(X[0:CH, h, :], x2[:, h, :], gr[1][:, h:h + 1], gb[1][:, h:h + 1],
                                    ALU.mult, ALU.add).then_inc(X_s.sem, 1)

            def gram_copy(c):
                dve.wait_ge(gp_s.sem, gp_s.at(c, 1))
                v.tensor_copy(gram[:], R[0][0:CH, 0:2 * C].rearrange("p (h c) -> p h c", h=2)).then_inc(ge_s.sem, 1)

            def times_w(c):
                dve.wait_ge(tue_s.sem, tue_s.at(c, 2))
                v.tensor_tensor(prd[:], tu[:], par2("wqkT"), ALU.mult).then_inc(prd_s.sem, 1)
                dve.wait_ge(kn_s.sem, kn_s.at(c, 1))
                v.tensor_scalar(nrm[:], R[0][0:CH, 0:4], 1e-24, None, ALU.max).then_inc(nrm_s.sem, 1)

            def head_softmax(c):
                s = sm_s
                dve.wait_ge(rn_s.sem, rn_s.at(c, 1))
                for h in range(2):
                    v.tensor_scalar(dk[:, h, :], ident[0:CH, 0:CH], rn[:, 2 + h:3 + h], None, ALU.mult).then_inc(dk_s.sem, 1)
                v.tensor_tensor(rq[:], rn[:, 0:2], par("temp"), ALU.mult).then_inc(s.sem, 1)
                dve.wait_ge(rk_s.sem, rk_s.at(c, 1))
                dve.wait_ge(s.sem, s.at(c, 1))
                dve.wait_ge(sc_s.sem, sc_s.at(c, 1))
                for h in range(2):
                    v.scalar_tensor_tensor(s1[:, h, :], R[1][0:CH, h * CH:(h + 1) * CH], rq[:, h:h + 1],
                                           rk[:, h, :], ALU.mult, ALU.mult).then_inc(s.sem, 1)
                dve.wait_ge(s.sem, s.at(c, 3))
                v.tensor_tensor(s2[:], s1[:], par("mask").unsqueeze(1).broadcast_to([CH, 2, CH]), ALU.add).then_inc(s.sem, 1)
                dve.wait_ge(s.sem, s.at(c, 4))
                v.tensor_reduce(smx[:], s2[:], AX_X, ALU.max, negate=True).then_inc(s.sem, 1)
                dve.wait_ge(se_s.sem, se_s.at(c, 2))
                v.reciprocal(srec[:], ssum[:]).then_inc(s.sem, 1)
                dve.wait_ge(s.sem, s.at(c, 6))
                for h in range(2):
                    v.tensor_scalar(attn[:, h, :], se[:, h, :], srec[:, h:h + 1], None, ALU.mult).then_inc(s.sem, 1)

            def weight_copies(c):
                dve.wait_ge(mp_s.sem, mp_s.at(c, 1))
                v.tensor_copy(wma[:], R[1][0:CH, 0:2 * C].rearrange("p (h c) -> p h c", h=2)).then_inc(mae_s.sem, 1)
                dve.wait_ge(mp_s.sem, mp_s.at(c, 3))
                v.tensor_copy(wmc[0:CH, :, :], R[2][0:CH, 0:2 * C6].rearrange("p (h c) -> p h c", h=2)).then_inc(mce_s.sem, 1)

            def pad_t(c):
                dve.wait_ge(t4_s.sem, t4_s.at(c, 1))
                img = tp[:].rearrange("p (y x) -> p y x", x=PW)
                for q in range(4):
                    v.tensor_copy(img[0:C6, 1 + 8 * q:9 + 8 * q, 1:1 + WW],
                                  t4[q * C6:(q + 1) * C6, :].rearrange("p (y x) -> p y x", x=WW)).then_inc(tpc_s.sem, 1)

            def ci1_scale(c):
                dve.wait_ge(cip_s.sem, cip_s.at(c, 1))
                v.tensor_scalar(ci1[:], R[2][:, 0:1], 1.0 / N, par("b_ci1"), ALU.mult, ALU.add).then_inc(ci_s.sem, 1)
                dve.wait_ge(ci_s.sem, ci_s.at(c, 1))
                v.tensor_scalar(wco[:], par("wcoT"), ci1[:, 0:1], None, ALU.mult).then_inc(ci_s.sem, 1)

            def channel_product(c):
                dve.wait_ge(cb_s.sem, cb_s.at(c, 1))
                for q in range(4):
                    p = slice(q * C6, (q + 1) * C6)
                    v.scalar_tensor_tensor(pr4[p, q * QB:(q + 1) * QB], R[0][p, 0:QB], bci2[p, 0:1], t4[p, :],
                                           ALU.add, ALU.mult, accum_out=psm[p, :]).then_inc(pr_s.sem, 1)

            def gate_one(c):
                dve.wait_ge(gt_s.sem, gt_s.at(c, 2))
                v.tensor_scalar(gate2[:], gate[:], 1.0, None, ALU.add).then_inc(g2_s.sem, 1)

            def conv2(c):
                w = par2("wdw2")
                dve.wait_ge(cf_s.sem, cf_s.at(c, 2))
                for tap in range(1, 9):
                    dy, dx = divmod(tap, 3)
                    for h in range(2):
                        if tap > 1:
                            dve.wait_ge(cv_s.sem, cv_s.at(c, 2 * (tap - 2) + h + 1))
                        acc = cx[:, h, :].rearrange("p (y x) -> p y x", x=WW)
                        v.scalar_tensor_tensor(acc, cp[:, h, dy:dy + HH, dx:dx + WW], w[:, h, tap:tap + 1], acc,
                                               ALU.mult, ALU.add).then_inc(cv_s.sem, 1)

            def sp_conv(c):
                dve.wait_ge(df_s.sem, df_s.at(c, 1))
                k = 0
                for tap in range(1, 9):
                    dy, dx = divmod(tap, 3)
                    for p in range(2):
                        if tap > 1:
                            dve.wait_ge(dv_s.sem, dv_s.at(c, k - 1))
                        acc = dd[:, p * HB:(p + 1) * HB].rearrange("p (y x) -> p y x", x=WW)
                        v.scalar_tensor_tensor(acc, spp[:, 16 * p + dy:16 * p + dy + 16, dx:dx + WW],
                                               par("w_spdw")[:, tap:tap + 1], acc, ALU.mult, ALU.add).then_inc(dv_s.sem, 1)
                        k += 1

            def gelu_product(c):
                dve.wait_ge(gl_s.sem, gl_s.at(c, 1))
                v.tensor_tensor(gmul[SP2:SPN, :], gl[SP2:SPN, :], dd[SP2:SPN, :], ALU.mult).then_inc(gu_s.sem, 1)

            def merge(c):
                for k in range(4):
                    h, n = divmod(k, 2)
                    dve.wait_ge(ap_s.sem, ap_s.at(c, k + 1))
                    v.scalar_tensor_tensor(uu[:, h, n * HB:(n + 1) * HB], th[:, h, n * HB:(n + 1) * HB], 1.0,
                                           R[(1, 2, 0, 1)[k]][0:CH, :], ALU.add, ALU.mult).then_inc(uu_s.sem, 1)
                dve.wait_ge(g2_s.sem, g2_s.at(c, 1))
                for h in range(2):
                    dve.wait_ge(uu_s.sem, uu_s.at(c, 2 * h + 2))
                    v.scalar_tensor_tensor(zz[:, h, :], cx[:, h, :], gate2[:, h:h + 1], uu[:, h, :],
                                           ALU.mult, ALU.add).then_inc(zz_s.sem, 1)

            def result(c):
                dve.wait_ge(st_out.sem, st_out.at(c, 0))
                for k in range(4):
                    h, n = divmod(k, 2)
                    dve.wait_ge(op_s.sem, op_s.at(c, k + 1))
                    v.tensor_tensor(oo[:, h, n * HB:(n + 1) * HB], R[(2, 0, 1, 2)[k]][0:CH, :],
                                    xr[:, h, n * HB:(n + 1) * HB], ALU.add).then_inc(oo_s.sem, 1)

            def block1_a(b):
                dve.wait_ge(x_in.sem, x_in.at(b, 16))
                channel_stats(0, b, xt)
                group_stats(0, b, psB)
                pixel_rstd(b)
                low_parts(b)

            def block1_b(b):
                for t in range(NKT):
                    row_max(b, t)
                split_max(b)

            def block1_d(b):
                attn_out(b)
                block1_out(b)

            def block2_a(c):
                channel_stats(1, c, x2)
                group_stats(1, c, R[0])
                normed(c)
                gram_copy(c)
                times_w(c)

            def block2_b(c):
                head_softmax(c)
                weight_copies(c)
                pad_t(c)
                ci1_scale(c)
                conv2(c)

            def block2_c(c):
                channel_product(c)
                gate_one(c)
                sp_conv(c)

            def block2_d(c):
                gelu_product(c)
                merge(c)
                result(c)

            dve.sem_inc(oo_s.sem, 1)
            dve.sem_inc(st_out.sem, 1)
            setup()
            block1_a(0)
            block1_b(0)
            block1_d(0)
            setup2()
            dve.wait_ge(s_fill, FILLS)
            with dve.Fori(1, B) as i:
                dve.wait_ge(x2_s.sem, x2_s.at(i, 0))
                dve.wait_ge(oo_s.sem, oo_s.at(i - 1, 0))
                block2_a(i - 1)
                block1_a(i)
                block2_b(i - 1)
                block1_b(i)
                block2_c(i - 1)
                block2_d(i - 1)
                block1_d(i)
            dve.wait_ge(x2_s.sem, x2_s.at(B, 0))
            block2_a(B - 1)
            block2_b(B - 1)
            block2_c(B - 1)
            block2_d(B - 1)

        @block.scalar
        def _(act):
            a = nc.scalar.activation
            ID = ACT.Identity

            def normed1(b):
                act.wait_ge(gmm[0].sem, gmm[0].at(b, 4))
                a(xa[:], xt[0:PD, 0, :], ID, bias=gb[0][0:PD, 0:1], scale=gr[0][0:PD, 0:1]).then_inc(xa_s.sem, 1)
                act.wait_ge(xc_s.sem, xc_s.at(b, 1))
                a(sq[:], psA[0:PD, :], ACT.Square).then_inc(sq_s.sem, 1)
                for h in range(2):
                    a(xm[:, h, :], xt[:, h, :], ACT.Relu, bias=gb[0][:, h:h + 1],
                      scale=gr[0][:, h:h + 1]).then_inc(xm_s.sem, 1)
                act.wait_ge(rbp_s.sem, rbp_s.at(b, 1))
                a(rb[:], psB[0:PD, :], ACT.Copy).then_inc(rb_s.sem, 1)

            def high_parts(b):
                act.wait_ge(qkp_s.sem, qkp_s.at(b, 1))
                a(qs[0:CH, :], psB[0:CH, :], ACT.Copy).then_inc(qk_s.sem, 1)
                act.wait_ge(qkp_s.sem, qkp_s.at(b, 2))
                a(ks[0:CH, :], psA[0:CH, :], ACT.Copy).then_inc(qk_s.sem, 1)

            def max_copy(b):
                act.wait_ge(tm_s.sem, tm_s.at(b, 1))
                a(qs[CH:CH + 2, :], psB[0:2, :], ACT.Copy).then_inc(qm_s.sem, 1)

            def exps(b):
                for t in range(NKT):
                    act.wait_ge(st_s.sem, st_s.at(b, t + 1))
                    if t >= 2:
                        act.wait_ge(pvd_s.sem, pvd_s.at(b, t - 1))
                    a(pT[t % 2][:], (psA, psB)[t % 2][:], ACT.Exp).then_inc(ex_s.sem, 1)

            def attn_out(b):
                act.wait_ge(pvd_s.sem, pvd_s.at(b, NKT))
                a(osb[:, 0:HB], psO[0:PD + 1, :], ACT.Copy).then_inc(oc_s.sem, 1)

            def residual(c):
                for h in range(2):
                    a(xr[:, h, :], x2[:, h, :], ID, bias=par("b_pr")[:, h:h + 1]).then_inc(xr_s.sem, 1)

            def pad_conv1(c):
                for k in range(4):
                    h, n = divmod(k, 2)
                    act.wait_ge(c1_s.sem, c1_s.at(c, k + 1))
                    a(cp[:, h, 1 + 16 * n:17 + 16 * n, 1:1 + WW],
                      R[(1, 2, 0, 1)[k]][0:CH, :].rearrange("p (y x) -> p y x", x=WW), ACT.Copy).then_inc(ce_s.sem, 1)

            def conv2_first(c, h):
                act.wait_ge(ce_s.sem, ce_s.at(c, 2 * h + 2))
                a(cx[:, h, :].rearrange("p (y x) -> p y x", x=WW), cp[:, h, 0:HH, 0:WW], ID,
                  bias=par("bdw2")[:, h:h + 1], scale=par2("wdw2")[:, h, 0:1]).then_inc(cf_s.sem, 1)

            def copy_xT(c, k):
                act.wait_ge(xtp_s.sem, xtp_s.at(c, k + 1))
                a(xT[:, 2 * k:2 * k + 2, :], R[(2, 0, 1, 2)[k]][:, 0:4 * CH].rearrange("p (t c) -> p t c", t=2),
                  ACT.Copy).then_inc(xte_s.sem, 1)

            def copy_tu(c):
                for jh in range(2):
                    act.wait_ge(tup_s.sem, tup_s.at(c, jh + 1))
                    a(tu[:, jh, :], R[1 + jh][0:CH, 0:2 * C], ACT.Copy).then_inc(tue_s.sem, 1)

            def head_exps(c):
                act.wait_ge(kr_s.sem, kr_s.at(c, 1))
                a(rk[:], R[2][0:CH, 0:2 * CH].rearrange("p (h c) -> p h c", h=2), ACT.Copy).then_inc(rk_s.sem, 1)
                act.wait_ge(sm_s.sem, sm_s.at(c, 5))
                for h in range(2):
                    a(se[:, h, :], s2[:, h, :], ACT.Exp, bias=smx[:, h:h + 1],
                      accum_out=ssum[:, h:h + 1]).then_inc(se_s.sem, 1)
                act.wait_ge(at_s.sem, at_s.at(c, 1))
                a(attT[:], R[2][0:CH, 0:2 * CH].rearrange("p (h c) -> p h c", h=2), ACT.Copy).then_inc(ate_s.sem, 1)
                act.wait_ge(mp_s.sem, mp_s.at(c, 2))
                a(wmt[0:CH, :, :], R[0][0:CH, 0:2 * C].rearrange("p (h c) -> p h c", h=2),
                  ACT.Copy).then_inc(mte_s.sem, 1)

            def copy_t(c):
                act.wait_ge(tt_s.sem, tt_s.at(c, 1))
                a(t4[:], R[0][:, 0:QB], ACT.Copy, accum_out=tsum[:]).then_inc(t4_s.sem, 1)

            def pad_ci2a(c):
                act.wait_ge(ca_s.sem, ca_s.at(c, 1))
                img = up[:].rearrange("p (y x) -> p y x", x=UW)
                for q in range(4):
                    p0 = q * C6
                    a(img[0:C6, 9 + 8 * q:17 + 8 * q, 9:9 + WW],
                      R[1][p0:p0 + C6, 0:QB].rearrange("p (y x) -> p y x", x=WW), ID,
                      bias=par("b_ci2a")[p0:p0 + C6, :]).then_inc(ue_s.sem, 1)

            def channel_gate(c):
                act.wait_ge(cm_s.sem, cm_s.at(c, 1))
                for h in range(2):
                    a(gate[:, h:h + 1], R[2][0:CH, h:h + 1], ACT.Tanh, bias=hbias[:, 2 + h:3 + h],
                      scale=0.5 / N).then_inc(gt_s.sem, 1)

            def pad_sp(c):
                for n in range(2):
                    act.wait_ge(spi_s.sem, spi_s.at(c, n + 1))
                    a(spp[:, 1 + 16 * n:17 + 16 * n, 1:1 + WW],
                      R[1 + n][0:SPN, :].rearrange("p (y x) -> p y x", x=WW), ID,
                      bias=par("b_spi")).then_inc(spe_s.sem, 1)
                act.wait_ge(spe_s.sem, spe_s.at(c, 2))
                a(dd[:].rearrange("p (y x) -> p y x", x=WW), spp[:, 0:HH, 0:WW], ID, bias=par("b_spdw"),
                  scale=par("w_spdw")[:, 0:1]).then_inc(df_s.sem, 1)

            def gelu_tanh(c):
                act.wait_ge(dv_s.sem, dv_s.at(c, 16))
                a(gl[SP2:SPN, :], dd[0:PD, :], ACT.Gelu).then_inc(gl_s.sem, 1)
                for k in range(4):
                    h, n = divmod(k, 2)
                    act.wait_ge(spo_s.sem, spo_s.at(c, k + 1))
                    a(th[:, h, n * HB:(n + 1) * HB], R[(0, 1, 2, 0)[k]][0:CH, :], ACT.Tanh, scale=0.5,
                      bias=hbias[:, h:h + 1]).then_inc(th_s.sem, 1)

            def block1_a(b):
                normed1(b)
                high_parts(b)

            def block2_a(c):
                residual(c)
                pad_conv1(c)
                copy_xT(c, 0)
                conv2_first(c, 0)
                copy_xT(c, 1)
                copy_xT(c, 2)
                copy_xT(c, 3)
                conv2_first(c, 1)
                copy_tu(c)

            def block2_b(c):
                head_exps(c)
                copy_t(c)

            def block2_c(c):
                pad_ci2a(c)
                channel_gate(c)
                pad_sp(c)

            act.wait_ge(s_w1, 16)
            block1_a(0)
            max_copy(0)
            exps(0)
            attn_out(0)
            act.wait_ge(s_w2, 16)
            act.wait_ge(s_su, 15)
            act.wait_ge(s_fill, FILLS)
            with act.Fori(1, B) as i:
                act.wait_ge(x2_s.sem, x2_s.at(i, 0))
                act.wait_ge(oo_s.sem, oo_s.at(i - 1, 0))
                block2_a(i - 1)
                block1_a(i)
                block2_b(i - 1)
                max_copy(i)
                block2_c(i - 1)
                exps(i)
                gelu_tanh(i - 1)
                attn_out(i)
            act.wait_ge(x2_s.sem, x2_s.at(B, 0))
            act.wait_ge(oo_s.sem, oo_s.at(B - 1, 0))
            block2_a(B - 1)
            block2_b(B - 1)
            block2_c(B - 1)
            gelu_tanh(B - 1)

        @block.gpsimd
        def _(pool):
            g = nc.gpsimd

            def rsqrt(dst, src):
                n = src.shape[-1]
                return g.tensor_tensor(dst, src, mhalf[0:src.shape[0], 0:n], ALU.pow)

            def group_rstd(i, b):
                pool.wait_ge(gmm[i].sem, gmm[i].at(b, 3))
                rsqrt(gr[i][:], gvar[i][:]).then_inc(grr[i].sem, 1)

            def block1_a(b):
                group_rstd(0, b)
                pool.wait_ge(pv_s.sem, pv_s.at(b, 1))
                rsqrt(rT[:], pv8[:]).then_inc(rT_s.sem, 1)

            def inverse_norms(c):
                pool.wait_ge(nrm_s.sem, nrm_s.at(c, 1))
                rsqrt(rn[:], nrm[:]).then_inc(rn_s.sem, 1)

            g.memset(xn[:], 1.0).then_inc(s_fill, 1)
            g.memset(mhalf[:], -0.5).then_inc(s_fill, 1)
            pool.wait_ge(s_fill, 2)
            pool.wait_ge(s_su, 2)
            rsqrt(isd1[:], var1[:]).then_inc(s_isd, 1)
            rsqrt(isd2[:], var2[:]).then_inc(s_isd, 1)
            block1_a(0)
            g.memset(tp[:], 0.0).then_inc(s_fill, 1)
            g.memset(up[:], 0.0).then_inc(s_fill, 1)
            g.memset(cp[:, 0, :, :], 0.0).then_inc(s_fill, 1)
            g.memset(cp[:, 1, :, :], 0.0).then_inc(s_fill, 1)
            g.memset(spp[:], 0.0).then_inc(s_fill, 1)
            g.memset(pr4[:], 0.0).then_inc(s_fill, 1)
            pool.wait_ge(s_w2, 16)
            with pool.Fori(1, B) as i:
                pool.wait_ge(x2_s.sem, x2_s.at(i, 0))
                pool.wait_ge(oo_s.sem, oo_s.at(i - 1, 0))
                group_rstd(1, i - 1)
                block1_a(i)
                inverse_norms(i - 1)
            pool.wait_ge(x2_s.sem, x2_s.at(B, 0))
            pool.wait_ge(oo_s.sem, oo_s.at(B - 1, 0))
            group_rstd(1, B - 1)
            inverse_norms(B - 1)


def constants():
    k = np.arange(CH)
    same_group = (k[:, None] // GROUP) == (k[None, :] // GROUP)
    same_head = (k[:, None] // HD) == (k[None, :] // HD)
    e48 = np.zeros((PD + 1, 1), np.float32)
    e48[PD] = 1.0
    return {
        "ident": np.eye(P), "gavg": same_group / (4 * GROUP), "center": np.pad(np.eye(PD) - 1.0 / PD, ((0, 0), (0, CH - PD))),
        "mean48": np.full((PD, 1), 1.0 / PD), "ones": np.ones((P, CH)), "e48": e48,
        "mask": np.where(same_head, 0.0, MASKED),
    }


def pack(p):
    f = {k: np.asarray(v) for k, v in p.items()}
    l0 = {k[8:]: v for k, v in f.items() if k.startswith("L0_conv_")}
    l1 = {k[8:]: v for k, v in f.items() if k.startswith("L1_conv_")}

    def halves(m):
        return m.reshape(2, CH, -1).transpose(1, 0, 2).reshape(CH, -1)

    def split_sp(m):
        o = np.zeros(m.shape[:-1] + (SPN,), np.float32)
        o[..., 0:PD], o[..., SP2:SPN] = m[..., 0:PD], m[..., PD:2 * PD]
        return o

    w2a = l1["ci2a_w"][:, 0]
    w_ci2a = np.zeros((3, C6, 3, C6), np.float32)
    for ch in range(C6):
        w_ci2a[:, ch, :, ch] = w2a[ch].T
    w_ci2b = np.zeros((4, C6, 7, 2), np.float32)
    for dx in range(7):
        w_ci2b[dx % 4, :, :, dx // 4] = l1["ci2b_w"][:, 0, :, dx]
    w_spo = np.zeros((SPN, C), np.float32)
    w_spo[SP2:SPN] = l1["sp_out_w"][:, :, 0, 0].T
    ci2cT = l1["ci2c_w"][:, :, 0, 0].T
    blocks = {
        **constants(),
        "ln_w": l0["ln_w"][:, None], "ln_b": l0["ln_b"][:, None], "wqkvT": l0["w_qkv"].T,
        "bn1": np.stack([l0[f"bn1_{k}"] for k in "gbmv"], 1),
        "wproj": halves(l0["w_proj"]),
        "bn2": np.concatenate([halves(l0[f"bn2_{k}"][:, None]) for k in "gbmv"], 1),
        "wqkT": halves(l1["qkv_w"][0:2 * C].T), "wv": halves(l1["qkv_w"][2 * C:]),
        "wdw1T": halves(l1["dw1_w"][:, :, 0, 0].T), "wcpT": halves(l1["cp_in_w"][:, :, 0, 0].T),
        "wdw2": halves(l1["dw2_w"].reshape(C, 9)), "bdw2": halves(l1["dw2_b"][:, None]),
        "temp": halves(np.repeat(l1["temperature"].reshape(-1), HD)[:, None]),
        "w_ci1": np.tile(l1["ci1_w"][:, :, 0, 0].T, (4, 4)), "b_ci1": np.tile(l1["ci1_b"], 4)[:, None],
        "w_ci2a": w_ci2a.reshape(CH, 3 * C6), "b_ci2a": np.tile(l1["ci2a_b"], 4)[:, None],
        "ci2cT": np.tile(ci2cT, (4, 1)), "w_ci2b": w_ci2b.reshape(P, 14),
        "ci2cT_rep": np.tile(ci2cT, (1, 4)), "b_ci2b": l1["ci2b_b"][:, None],
        "b_ci2c": np.tile(l1["ci2c_b"], 4)[:, None], "wcoT": np.tile(l1["cp_out_w"][:, :, 0, 0].T, (4, 1)),
        "half_biases": np.concatenate([halves(l1["sp_out_b"][:, None]), halves(l1["cp_out_b"][:, None])], 1),
        "w_spi": split_sp(halves(l1["sp_in_w"][:, :, 0, 0].T).reshape(CH, 2, 2 * PD)).reshape(CH, -1),
        "b_spi": split_sp(l1["sp_in_b"])[:, None], "w_spdw": split_sp(l1["sp_dw_w"].reshape(2 * PD, 9).T).T,
        "b_spdw": split_sp(l1["sp_dw_b"])[:, None], "w_spo": w_spo,
        "w_pr": halves(l1["proj_w"].T), "b_pr": halves(l1["proj_b"][:, None]),
    }
    out = np.zeros((P, NW), np.float32)
    for name, (parts, off, cols) in AT.items():
        if name.startswith("row_"):
            out[CH, off:off + cols] = l1[name[4:]]
        else:
            out[0:parts, off:off + cols] = blocks[name]
    return out


def kernel(**inputs):
    import concourse.bacc as bacc
    from concourse.bass_utils import run_bass_kernel_spmd

    x = np.ascontiguousarray(np.asarray(inputs["x"]).reshape(B, 2, CH, N))
    params = pack({k: v for k, v in inputs.items() if k != "x"})
    nc = bacc.Bacc("TRN2", target_bir_lowering=False, num_devices=1)
    x_ap = nc.dram_tensor("x_dram", x.shape, F32, kind="ExternalInput").ap()
    p_ap = nc.dram_tensor("params_dram", params.shape, F32, kind="ExternalInput").ap()
    o_ap = nc.dram_tensor("out_dram", x.shape, F32, kind="ExternalOutput").ap()
    build(nc, x_ap, p_ap, o_ap)
    r = run_bass_kernel_spmd(nc, [{"x_dram": x, "params_dram": params}], core_ids=[0])
    return r.results[0]["out_dram"].reshape(B, C, HH, WW)
```

```python
from contextlib import ExitStack

import numpy as np

import concourse.bass as bass
from concourse import mybir

F32 = mybir.dt.float32
F32R = mybir.dt.float32r
ALU = mybir.AluOpType
ACT = mybir.ActivationFunctionType
AX_X = mybir.AxisListType.X

B, C, HH, WW = 4, 192, 32, 32
N = HH * WW
P = 128
CH = C // 2
GROUP = C // 32
PD, QK = 48, 16
QKV = 2 * QK + PD
NKT = N // P
HB = N // 2
QB = N // 4
C6 = C // 6
HD = C // 8
EPS = 1e-5
PW = WW + 2
UW = WW + 18
SP2 = 64
SPN = SP2 + PD
MASKED = -1e30
FILLS = 8

FIRST = {
    "ident": (P, P), "gavg": (CH, CH), "center": (PD, CH), "mean48": (PD, 1), "ones": (P, CH),
    "e48": (PD + 1, 1), "ln_w": (PD, 1), "ln_b": (PD, 1), "wqkvT": (PD, QKV),
    "bn1": (QKV, 4), "wproj": (CH, 2 * C), "bn2": (CH, 8),
}
SECOND = {
    "wqkT": (CH, 2 * 2 * C), "wv": (CH, 2 * C), "wdw1T": (CH, 2 * C), "wcpT": (CH, 2 * C6),
    "row_dw1_b": (CH + 1, C), "row_cp_in_b": (CH + 1, C6), "row_cp_out_b": (CH + 1, C),
    "wdw2": (CH, 2 * 9), "bdw2": (CH, 2), "temp": (CH, 2), "mask": (CH, CH),
    "w_ci1": (P, P), "b_ci1": (P, 1), "w_ci2a": (CH, 3 * C6), "b_ci2a": (P, 1),
    "ci2cT": (P, C6), "w_ci2b": (P, 14), "ci2cT_rep": (C6, P), "b_ci2b": (C6, 1), "b_ci2c": (P, 1),
    "wcoT": (P, C), "half_biases": (CH, 4), "w_spi": (CH, 2 * SPN), "b_spi": (SPN, 1),
    "w_spdw": (SPN, 9), "b_spdw": (SPN, 1), "w_spo": (SPN, C), "w_pr": (CH, 2 * C), "b_pr": (CH, 2),
}


def place(blocks, start):
    at = {}
    for name, (parts, cols) in blocks.items():
        at[name] = (parts, start, cols)
        start += cols
    return at, start


AT1, N1 = place(FIRST, 0)
AT2, NW = place(SECOND, N1)
AT = {**AT1, **AT2}


class Signal:

    def __init__(self, sem, per, before=0):
        self.sem, self.per, self.before = sem, per, before

    def at(self, b, k):
        return b * self.per + (k + self.before)


def build(nc, x, params, out):
    with ExitStack() as ctx:
        def sb(name, shape, dt=F32):
            return ctx.enter_context(nc.sbuf_tensor(name, shape, dt))

        def psum(name, shape):
            return ctx.enter_context(nc.psum_tensor(name, shape, F32))

        def sem(name):
            return ctx.enter_context(nc.semaphore(name))

        def sig(name, per, before=0):
            return Signal(sem(name), per, before)

        psA = psum("psA", [P, N])
        psB = psum("psB", [P, N])
        psO = psum("psO", [P, HB])
        R = [psum(f"psR{i}", [P, HB]) for i in range(3)]

        wt = sb("wt", [P, NW])

        def par(name):
            parts, off, cols = AT[name]
            return wt[0:parts, off:off + cols]

        def par2(name):
            return par(name).rearrange("p (h c) -> p h c", h=2)

        ident, ones = par("ident"), par("ones")
        lnmat = sb("lnmat", [PD, PD + 1])
        mhalf = sb("mhalf", [P, NKT])
        var1 = sb("var1", [QKV, 1])
        isd1 = sb("isd1", [QKV, 1])
        inv1 = sb("inv1", [QKV, 1])
        sh1 = sb("sh1", [QKV, 1])
        wl = sb("wl", [QKV, PD + 1])
        q3w = sb("q3w", [PD + 1, CH])
        k3w = sb("k3w", [PD + 1, CH])
        v1w = sb("v1w", [PD + 1, PD + 1])
        var2 = sb("var2", [CH, 2])
        isd2 = sb("isd2", [CH, 2])
        inv2 = sb("inv2", [CH, 2])
        dinv2 = sb("dinv2", [CH, 2, CH])
        bias2 = sb("bias2", [CH, 2])
        wp2 = sb("wp2", [CH, 2, C])
        wc1 = sb("wc1", [CH + 1, 2, C])
        wb = sb("wb", [P, 14, C6])
        bci2 = sb("bci2", [P, 1])
        hbias = sb("hbias", [CH, 4])
        wph = sb("wph", [CH, 2, C])

        xt = sb("xt", [CH, 2, N])
        st6 = [sb(f"st6_{i}", [CH, 8, 3]) for i in range(2)]
        mv = [sb(f"mv_{i}", [CH, 2, 8]) for i in range(2)]
        msq = [sb(f"msq_{i}", [CH, 8]) for i in range(2)]
        gm = [sb(f"gm_{i}", [CH, 2, 2]) for i in range(2)]
        gsq = [sb(f"gsq_{i}", [CH, 2]) for i in range(2)]
        gvar = [sb(f"gvar_{i}", [CH, 2]) for i in range(2)]
        gr = [sb(f"gr_{i}", [CH, 2]) for i in range(2)]
        gb = [sb(f"gb_{i}", [CH, 2]) for i in range(2)]
        xa = sb("xa", [PD, N])
        sq = sb("sq", [PD, N])
        pv8 = sb("pv8", [P, NKT])
        rT = sb("rT", [P, NKT])
        dg = sb("dg", [P, NKT, P])
        rb = sb("rb", [PD, N])
        xn = sb("xn", [64, N])
        qs = sb("qs", [P, N], F32R)
        ks = sb("ks", [P, N], F32R)
        vt = sb("vt", [P, NKT, PD + 1])
        nm = sb("nm", [P, NKT])
        nmr = sb("nmr", [P, NKT, 2], F32R)
        pT = [sb(f"pT{i}", [P, N]) for i in range(2)]
        osb = sb("osb", [PD + 1, N])
        xm = sb("xm", [CH, 2, N])
        x2 = sb("x2", [CH, 2, N])

        X = sb("X", [CH + 1, 2, N])
        xr = sb("xr", [CH, 2, N])
        cp = sb("cp", [CH, 2, PW, PW])
        cx = sb("cx", [CH, 2, N])
        xT = sb("xT", [P, NKT, C])
        gram = sb("gram", [CH, 2, C])
        tu = sb("tu", [CH, 2, 2 * C])
        prd = sb("prd", [CH, 2, 2 * C])
        nrm = sb("nrm", [CH, 4])
        rn = sb("rn", [CH, 4])
        dk = sb("dk", [CH, 2, CH])
        rk = sb("rk", [CH, 2, CH])
        rq = sb("rq", [CH, 2])
        s1 = sb("s1", [CH, 2, CH])
        s2 = sb("s2", [CH, 2, CH])
        smx = sb("smx", [CH, 2])
        se = sb("se", [CH, 2, CH])
        ssum = sb("ssum", [CH, 2])
        srec = sb("srec", [CH, 2])
        attn = sb("attn", [CH, 2, CH])
        attT = sb("attT", [CH, 2, CH])
        wmt = sb("wmt", [CH + 1, 2, C])
        wma = sb("wma", [CH, 2, C])
        wmc = sb("wmc", [CH + 1, 2, C6])
        t4 = sb("t4", [P, QB])
        tsum = sb("tsum", [P, 1])
        tp = sb("tp", [CH, PW * PW])
        up = sb("up", [P, UW * UW])
        ci1 = sb("ci1", [P, 1])
        wco = sb("wco", [P, C])
        pr4 = sb("pr4", [P, N])
        psm = sb("psm", [P, 1])
        gate = sb("gate", [CH, 2])
        gate2 = sb("gate2", [CH, 2])
        spp = sb("spp", [SPN, PW, PW])
        dd = sb("dd", [SPN, N])
        gl = sb("gl", [SPN, N])
        gmul = gl
        th = sb("th", [CH, 2, N])
        uu = sb("uu", [CH, 2, N])
        zz = uu
        oo = sb("oo", [CH, 2, N])

        s_w1, s_w2 = sem("params1_loaded"), sem("params2_loaded")
        s_fill, s_rows = sem("constants_filled"), sem("rows_of_ones")
        s_isd = sem("setup_rsqrt")
        s_ln = sem("lnmat_ready")
        s_su_pe = sem("setup_products")
        s_su = sem("setup_vector_steps")

        x_in = sig("x_in", 16)
        gst = [sig(f"channel_stats_{i}", 7) for i in range(2)]
        gav = [sig(f"group_means_{i}", 1) for i in range(2)]
        gmm = [sig(f"group_steps_{i}", 4) for i in range(2)]
        grr = [sig(f"group_rstd_{i}", 1) for i in range(2)]
        xa_s = sig("attended_normed", 1)
        xm_s = sig("relu_normed", 2)
        xc_s = sig("centered", 1)
        sq_s = sig("squares", 1)
        var_s = sig("pixel_vars", 1)
        pv_s = sig("pixel_vars_copied", 1)
        rT_s = sig("pixel_rstd", 1)
        dg_s = sig("diagonals", 2)
        rbp_s = sig("rstd_rows", 1)
        rb_s = sig("rstd_rows_copied", 1)
        xn_s = sig("layer_normed", 1)
        qkp_s = sig("qkv_products", 3)
        qk_s = sig("qk_high_parts", 2)
        ql_s = sig("qk_low_parts", 2)
        vt_s = sig("vT_copied", 1)
        mx_s = sig("score_rows", NKT)
        nm_s = sig("row_max_steps", NKT + 2)
        tm_s = sig("max_rows", 1)
        qm_s = sig("max_rows_copied", 1)
        st_s = sig("scores_t", NKT)
        ex_s = sig("exps", NKT)
        pvd_s = sig("pv_done", NKT)
        oc_s = sig("attn_out_copied", 2)
        dn_s = sig("denominators", 1)
        dr_s = sig("denominators_inverted", 1)
        db_s = sig("denominator_rows", 1)
        xo_s = sig("attn_relu", 1)
        y_s = sig("proj1", 2)
        x2_s = sig("block1_out", 2)

        X_s = sig("normed2", 2)
        xr_s = sig("residual_biased", 2)
        c1_s = sig("conv1_product", 4)
        ce_s = sig("conv1_padded", 4)
        cf_s = sig("conv2_first_tap", 2)
        cv_s = sig("conv2_taps", 16)
        xtp_s = sig("xT_product", 4)
        xte_s = sig("xT_copied", 4)
        gp_s = sig("gram_product", 1)
        ge_s = sig("gram_copied", 1)
        tup_s = sig("tu_product", 2)
        tue_s = sig("tu_copied", 2)
        prd_s = sig("tu_times_w", 1)
        kn_s = sig("norms_product", 1)
        nrm_s = sig("norms_clamped", 1)
        rn_s = sig("inverse_norms", 1)
        dk_s = sig("k_norm_diagonals", 2)
        kr_s = sig("k_norm_rows", 1)
        rk_s = sig("k_norm_rows_copied", 1)
        sc_s = sig("head_scores", 1)
        sm_s = sig("head_softmax_steps", 8)
        se_s = sig("head_exps", 2)
        at_s = sig("attn_transposed", 1)
        ate_s = sig("attn_transposed_copied", 1)
        mp_s = sig("attn_wv_products", 3)
        mte_s = sig("wmt_copied", 1)
        mae_s = sig("wma_copied", 1)
        mce_s = sig("wmc_copied", 1)
        tt_s = sig("t_product", 1)
        t4_s = sig("t_copied", 1)
        tpc_s = sig("t_padded", 4)
        tpd_s = sig("t_shifted_copies", 32)
        ca_s = sig("ci2a_product", 1)
        ue_s = sig("ci2a_padded", 4)
        ud_s = sig("ci2a_shifted_copies", 48)
        cip_s = sig("ci1_product", 1)
        ci_s = sig("ci1_steps", 2)
        cb_s = sig("ci2_product", 1)
        pr_s = sig("channel_product", 4)
        cm_s = sig("channel_map_mean", 1)
        gt_s = sig("gate_tanh", 2)
        g2_s = sig("gate_plus_one", 1)
        spi_s = sig("sp_in_product", 2)
        spe_s = sig("sp_in_padded", 2)
        df_s = sig("sp_first_tap", 1)
        dv_s = sig("sp_conv", 16)
        gl_s = sig("gelu", 1)
        gu_s = sig("gelu_times_x2", 1)
        spo_s = sig("sp_out_product", 4)
        th_s = sig("spatial_tanh", 4)
        ap_s = sig("attended_product", 4)
        uu_s = sig("attended_gated", 4)
        zz_s = sig("merged", 4)
        op_s = sig("proj2", 4)
        oo_s = sig("out_copied", 4, before=1)
        st_out = sig("out_stored", 64, before=1)

        bn1 = par("bn1")
        bn2 = par("bn2").rearrange("p (f h) -> p f h", f=4)

        def row(name):
            _, off, cols = AT[name]
            return wt[CH:CH + 1, off:off + cols]

        def halves(ps):
            return [ps[:, 0:HB], ps[:, HB:N]]

        block = ctx.enter_context(nc.Block())

        @block.sync
        def _(sp):
            sp.dma_start(wt[:, 0:N1], params[:, 0:N1]).then_inc(s_w1, 16)

            def load_x(b):
                sp.dma_start(xt[:], x[b].rearrange("h c n -> c h n")).then_inc(x_in.sem, 16)

            def shift_t(c):
                sp.wait_ge(tpc_s.sem, tpc_s.at(c, 4))
                for j in (1, 2):
                    n = PW * PW - j
                    sp.dma_start(tp[j * C6:(j + 1) * C6, 0:n], tp[0:C6, j:j + n]).then_inc(tpd_s.sem, 16)

            def shift_u(c):
                sp.wait_ge(ue_s.sem, ue_s.at(c, 4))
                for j in (1, 2, 3):
                    n = UW * UW - 3 * j
                    sp.dma_start(up[j * C6:(j + 1) * C6, 0:n], up[0:C6, 3 * j:3 * j + n]).then_inc(ud_s.sem, 16)

            def store(c):
                for k in range(4):
                    n, h = divmod(k, 2)
                    sp.wait_ge(oo_s.sem, oo_s.at(c, k + 1))
                    sp.dma_start(out[c, h, :, n * HB:(n + 1) * HB],
                                 oo[:, h, n * HB:(n + 1) * HB]).then_inc(st_out.sem, 16)

            def block2(c):
                shift_t(c)
                shift_u(c)
                store(c)

            load_x(0)
            sp.dma_start(wt[:, N1:NW], params[:, N1:NW]).then_inc(s_w2, 16)
            with sp.Fori(1, B) as i:
                sp.wait_ge(x2_s.sem, x2_s.at(i, 0))
                load_x(i)
                block2(i - 1)
            block2(B - 1)
            sp.wait_ge(st_out.sem, st_out.at(B - 1, 64))

        @block.tensor
        def _(pe):
            mm = nc.tensor.matmul

            def setup():
                pe.wait_ge(s_w1, 16)
                pe.wait_ge(s_ln, 2)
                mm(psA[0:QKV, 0:PD + 1], par("wqkvT"), lnmat[:], start=True, stop=True).then_inc(s_su_pe, 1)
                pe.wait_ge(s_su, 8)
                mm(psB[0:PD + 1, 0:QKV], wl[:], ident[0:QKV, 0:QKV], start=True, stop=True).then_inc(s_su_pe, 1)
                wp = par2("wproj")
                for k in range(2):
                    for h in range(2):
                        last = mm(psA[0:CH, k * C + h * CH:k * C + (h + 1) * CH], wp[:, h, k * CH:(k + 1) * CH],
                                  dinv2[:, h, :], start=True, stop=True)
                last.then_inc(s_su_pe, 1)

            def setup2():
                pe.wait_ge(s_w2, 16)
                wv, wd = par2("wv"), par2("wdw1T")
                for jh in range(2):
                    for h in range(2):
                        last = mm(R[0][0:CH, jh * C:(jh + 1) * C], wv[:, h, jh * CH:(jh + 1) * CH],
                                  wd[:, h, :], start=(h == 0), stop=(h == 1))
                last.then_inc(s_su_pe, 1)
                mm(R[1][:, 0:1], par("ci2cT_rep"), par("b_ci2b"), start=True, stop=True).then_inc(s_su_pe, 1)

            def group_means(i, b, ps):
                pe.wait_ge(gst[i].sem, gst[i].at(b, 7))
                mm(ps[0:CH, 0:16], par("gavg"), mv[i][:].rearrange("p s k -> p (s k)"),
                   start=True, stop=True).then_inc(gav[i].sem, 1)

            def center(b):
                pe.wait_ge(xa_s.sem, xa_s.at(b, 1))
                for n in range(2):
                    last = mm(psA[0:CH, n * HB:(n + 1) * HB], par("center"), xa[:, n * HB:(n + 1) * HB],
                              start=True, stop=True)
                last.then_inc(xc_s.sem, 1)

            def pixel_var(b):
                pe.wait_ge(sq_s.sem, sq_s.at(b, 1))
                for t in range(NKT):
                    last = mm(psB[:, t:t + 1], sq[:, t * P:(t + 1) * P], par("mean48"), start=True, stop=True)
                last.then_inc(var_s.sem, 1)

            def spread(b, k, done):
                pe.wait_ge(dg_s.sem, dg_s.at(b, k))
                for n in range(2):
                    last = mm(psB[0:PD, n * HB:(n + 1) * HB], ones[:, 0:PD], dg[:, n * 4:(n + 1) * 4, :],
                              start=True, stop=True)
                last.then_inc(done.sem, 1)

            def qk_product(b, k):
                pe.wait_ge(xn_s.sem, xn_s.at(b, 1))
                w, ps = ((q3w, psB), (k3w, psA))[k]
                for n in range(2):
                    last = mm(ps[0:CH, n * HB:(n + 1) * HB], w[:], xn[0:PD + 1, n * HB:(n + 1) * HB],
                              start=True, stop=True)
                last.then_inc(qkp_s.sem, 1)

            def v_product(b):
                for t in range(NKT):
                    last = mm(psO[:, t * 64:t * 64 + PD + 1], xn[0:PD + 1, t * P:(t + 1) * P], v1w[:],
                              start=True, stop=True)
                last.then_inc(qkp_s.sem, 1)

            def score_rows(b, t):
                if t == 0:
                    pe.wait_ge(qk_s.sem, qk_s.at(b, 2))
                    pe.wait_ge(ql_s.sem, ql_s.at(b, 2))
                if t >= 2:
                    pe.wait_ge(nm_s.sem, nm_s.at(b, t - 1))
                ps = (psA, psB)[t % 2]
                for n in range(2):
                    last = mm(ps[:, n * HB:(n + 1) * HB], qs[0:CH, t * P:(t + 1) * P],
                              ks[0:CH, n * HB:(n + 1) * HB], start=True, stop=True)
                last.then_inc(mx_s.sem, 1)

            def max_rows(b):
                pe.wait_ge(nm_s.sem, nm_s.at(b, NKT + 2))
                for t in range(NKT):
                    last = nc.tensor.transpose(psB[0:2, t * P:(t + 1) * P], nmr[:, t, :].bitcast(F32), ident)
                last.then_inc(tm_s.sem, 1)

            def scores_t(b, t):
                if t == 0:
                    pe.wait_ge(qm_s.sem, qm_s.at(b, 1))
                if t >= 2:
                    pe.wait_ge(ex_s.sem, ex_s.at(b, t - 1))
                ps = (psA, psB)[t % 2]
                for n in range(2):
                    last = mm(ps[:, n * HB:(n + 1) * HB], ks[0:CH + 2, t * P:(t + 1) * P],
                              qs[0:CH + 2, n * HB:(n + 1) * HB], start=True, stop=True)
                last.then_inc(st_s.sem, 1)

            def pv(b, t):
                if t == 0:
                    pe.wait_ge(vt_s.sem, vt_s.at(b, 1))
                pe.wait_ge(ex_s.sem, ex_s.at(b, t + 1))
                for n in range(2):
                    last = mm(psO[64 * n:64 * n + PD + 1, :], vt[:, t, :], pT[t % 2][:, n * HB:(n + 1) * HB],
                              start=(t == 0), stop=(t == NKT - 1))
                last.then_inc(pvd_s.sem, 1)

            def denominators(b):
                pe.wait_ge(oc_s.sem, oc_s.at(b, 2))
                for t in range(NKT):
                    last = mm(psA[:, t:t + 1], osb[:, t * P:(t + 1) * P], par("e48"), start=True, stop=True)
                last.then_inc(dn_s.sem, 1)

            def proj1(b, h):
                pe.wait_ge(xo_s.sem, xo_s.at(b, 1))
                ps = (psA, psB)[h]
                for n in range(2):
                    for k in range(2):
                        last = mm(ps[0:CH, n * HB:(n + 1) * HB], wp2[:, k, h * CH:(h + 1) * CH],
                                  xm[:, k, n * HB:(n + 1) * HB], start=(k == 0), stop=(k == 1))
                last.then_inc(y_s.sem, 1)

            def conv1(c, k):
                pe.wait_ge(X_s.sem, X_s.at(c, 2))
                h, n = divmod(k, 2)
                if k == 3:
                    pe.wait_ge(ce_s.sem, ce_s.at(c, 1))
                ps = R[(1, 2, 0, 1)[k]]
                mm(ps[0:CH, :], wc1[0:CH + 1, 0, h * CH:(h + 1) * CH], X[0:CH + 1, 0, n * HB:(n + 1) * HB],
                   start=True, stop=False)
                mm(ps[0:CH, :], wc1[0:CH, 1, h * CH:(h + 1) * CH], X[0:CH, 1, n * HB:(n + 1) * HB],
                   start=False, stop=True).then_inc(c1_s.sem, 1)

            def transpose_x(c, k):
                if k < 3:
                    pe.wait_ge(ce_s.sem, ce_s.at(c, k + 2))
                else:
                    pe.wait_ge(xte_s.sem, xte_s.at(c, 1))
                ps = R[(2, 0, 1, 2)[k]]
                for j in range(4):
                    t, h = 2 * k + j // 2, j % 2
                    last = nc.tensor.transpose(ps[:, j * CH:(j + 1) * CH], X[0:CH, h, t * P:(t + 1) * P],
                                               ident[0:CH, 0:CH])
                last.then_inc(xtp_s.sem, 1)

            def gram_x(c):
                pe.wait_ge(xte_s.sem, xte_s.at(c, 4))
                for h in range(2):
                    for t in range(NKT):
                        last = mm(R[0][0:CH, h * C:(h + 1) * C], xT[:, t, h * CH:(h + 1) * CH], xT[:, t, :],
                                  start=(t == 0), stop=(t == NKT - 1))
                last.then_inc(gp_s.sem, 1)

            def gram_w(c):
                pe.wait_ge(ge_s.sem, ge_s.at(c, 1))
                wqk = par2("wqkT")
                for jh in range(2):
                    for k in range(2):
                        last = mm(R[1 + jh][0:CH, 0:2 * C], gram[:, k, jh * CH:(jh + 1) * CH], wqk[:, k, :],
                                  start=(k == 0), stop=(k == 1))
                    last.then_inc(tup_s.sem, 1)

            def head_scores(c):
                pe.wait_ge(tue_s.sem, tue_s.at(c, 2))
                wqk = par2("wqkT")
                for h in range(2):
                    for jh in range(2):
                        last = mm(R[1][0:CH, h * CH:(h + 1) * CH], tu[:, jh, h * CH:(h + 1) * CH],
                                  wqk[:, jh, C + h * CH:C + (h + 1) * CH], start=(jh == 0), stop=(jh == 1))
                last.then_inc(sc_s.sem, 1)

            def norms(c):
                pe.wait_ge(prd_s.sem, prd_s.at(c, 1))
                for k in range(4):
                    for jh in range(2):
                        last = mm(R[0][0:CH, k:k + 1], prd[:, jh, k * CH:(k + 1) * CH], ones[0:CH, 0:1],
                                  start=(jh == 0), stop=(jh == 1))
                last.then_inc(kn_s.sem, 1)

            def k_norm_rows(c):
                pe.wait_ge(dk_s.sem, dk_s.at(c, 2))
                for h in range(2):
                    last = mm(R[2][0:CH, h * CH:(h + 1) * CH], ones[0:CH, :], dk[:, h, :], start=True, stop=True)
                last.then_inc(kr_s.sem, 1)

            def transpose_attn(c):
                pe.wait_ge(sm_s.sem, sm_s.at(c, 8))
                for h in range(2):
                    last = nc.tensor.transpose(R[2][0:CH, h * CH:(h + 1) * CH], attn[:, h, :], ident[0:CH, 0:CH])
                last.then_inc(at_s.sem, 1)

            def attn_weights(c):
                pe.wait_ge(ate_s.sem, ate_s.at(c, 1))
                wv = par2("wv")
                for h in range(2):
                    last = mm(R[1][0:CH, h * C:(h + 1) * C], attT[:, h, :], wv[:, h, :], start=True, stop=True)
                last.then_inc(mp_s.sem, 1)
                for jh in range(2):
                    for h in range(2):
                        last = mm(R[0][0:CH, jh * C + h * CH:jh * C + (h + 1) * CH],
                                  wv[:, h, jh * CH:(jh + 1) * CH], attT[:, h, :], start=True, stop=True)
                last.then_inc(mp_s.sem, 1)

            def t_weights(c):
                pe.wait_ge(mae_s.sem, mae_s.at(c, 1))
                wcp = par2("wcpT")
                for jh in range(2):
                    for h in range(2):
                        last = mm(R[2][0:CH, jh * C6:(jh + 1) * C6], wma[:, h, jh * CH:(jh + 1) * CH],
                                  wcp[:, h, :], start=(h == 0), stop=(h == 1))
                last.then_inc(mp_s.sem, 1)

            def t_product(c):
                pe.wait_ge(mte_s.sem, mte_s.at(c, 1))
                pe.wait_ge(mce_s.sem, mce_s.at(c, 1))
                for jh in range(2):
                    kk = CH + 1 if jh == 0 else CH
                    for q in range(4):
                        last = mm(R[0][q * C6:(q + 1) * C6, 0:QB], wmc[0:kk, jh, :],
                                  X[0:kk, jh, q * QB:(q + 1) * QB], start=(jh == 0), stop=(jh == 1))
                last.then_inc(tt_s.sem, 1)

            def ci1_product(c):
                pe.wait_ge(t4_s.sem, t4_s.at(c, 1))
                mm(R[0][:, 0:1], par("w_ci1"), tsum[:], start=True, stop=True).then_inc(cip_s.sem, 1)

            def ci2a(c):
                pe.wait_ge(ci_s.sem, ci_s.at(c, 1))
                pe.wait_ge(tpd_s.sem, tpd_s.at(c, 32))
                w = par("w_ci2a").rearrange("p (y o) -> p y o", y=3)
                img = tp[:].rearrange("p (y x) -> p y x", x=PW)
                for dy in range(3):
                    for q in range(4):
                        last = mm(R[0][q * C6:(q + 1) * C6, 0:QB], w[:, dy, :],
                                  img[:, q * 8 + dy:q * 8 + dy + 8, 0:WW], start=(dy == 0), stop=(dy == 2))
                last.then_inc(ca_s.sem, 1)

            def ci2b(c, dy):
                if dy == 0:
                    pe.wait_ge(ud_s.sem, ud_s.at(c, 48))
                img = up[:].rearrange("p (y x) -> p y x", x=UW)
                for second in range(2):
                    g = 2 * dy + second
                    kk = 3 * C6 if second else P
                    for q in range(4):
                        y0 = q * 8 + 3 * dy
                        last = mm(R[0][q * C6:(q + 1) * C6, 0:QB], wb[0:kk, g, :],
                                  img[0:kk, y0:y0 + 8, 12 * second:12 * second + WW],
                                  start=(g == 0), stop=(g == 13))
                if dy == 6:
                    last.then_inc(cb_s.sem, 1)

            def map_mean(c):
                pe.wait_ge(pr_s.sem, pr_s.at(c, 4))
                pe.wait_ge(ci_s.sem, ci_s.at(c, 2))
                for h in range(2):
                    last = mm(R[0][0:CH, h:h + 1], wco[:, h * CH:(h + 1) * CH], psm[:], start=True, stop=True)
                last.then_inc(cm_s.sem, 1)

            def sp_in(c, n):
                pe.wait_ge(cv_s.sem, cv_s.at(c, 16))
                pe.wait_ge(mce_s.sem, mce_s.at(c, 1))
                w = par2("w_spi")
                for k in range(2):
                    last = mm(R[1 + n][0:SPN, :], w[:, k, :], cx[:, k, n * HB:(n + 1) * HB],
                              start=(k == 0), stop=(k == 1))
                last.then_inc(spi_s.sem, 1)

            def sp_out(c, k):
                pe.wait_ge(gu_s.sem, gu_s.at(c, 1))
                n, h = divmod(k, 2)
                if k >= 2:
                    pe.wait_ge(th_s.sem, th_s.at(c, k - 1))
                mm(R[1 + h][0:CH, :], par("w_spo")[SP2:SPN, h * CH:(h + 1) * CH],
                   gmul[SP2:SPN, n * HB:(n + 1) * HB], start=True, stop=True).then_inc(spo_s.sem, 1)

            def attended(c, k):
                n, h = divmod(k, 2)
                if k == 0:
                    pe.wait_ge(mte_s.sem, mte_s.at(c, 1))
                    pe.wait_ge(gt_s.sem, gt_s.at(c, 2))
                elif k < 3:
                    pe.wait_ge(th_s.sem, th_s.at(c, k + 2))
                else:
                    pe.wait_ge(uu_s.sem, uu_s.at(c, 1))
                ps = R[k % 3]
                mm(ps[0:CH, :], wmt[0:CH + 1, 0, h * CH:(h + 1) * CH], X[0:CH + 1, 0, n * HB:(n + 1) * HB],
                   start=True, stop=False)
                mm(ps[0:CH, :], wmt[0:CH, 1, h * CH:(h + 1) * CH], X[0:CH, 1, n * HB:(n + 1) * HB],
                   start=False, stop=False)
                mm(ps[0:CH, :], wco[:, h * CH:(h + 1) * CH], pr4[:, n * HB:(n + 1) * HB],
                   start=False, stop=True).then_inc(ap_s.sem, 1)

            def proj2(c, k):
                n, h = divmod(k, 2)
                pe.wait_ge(zz_s.sem, zz_s.at(c, 2 * n + 2))
                if k == 1:
                    pe.wait_ge(uu_s.sem, uu_s.at(c, 3))
                if k == 3:
                    pe.wait_ge(oo_s.sem, oo_s.at(c, 1))
                for j in range(2):
                    last = mm(R[(k + 1) % 3][0:CH, :], wph[:, j, h * CH:(h + 1) * CH],
                              zz[:, j, n * HB:(n + 1) * HB], start=(j == 0), stop=(j == 1))
                last.then_inc(op_s.sem, 1)

            def block1(b):
                group_means(0, b, psB)
                center(b)
                pixel_var(b)
                spread(b, 1, rbp_s)
                qk_product(b, 0)
                qk_product(b, 1)
                v_product(b)
                for t in range(8):
                    score_rows(b, t)
                max_rows(b)
                scores_t(b, 0)
                scores_t(b, 1)
                pv(b, 0)
                scores_t(b, 2)
                pv(b, 1)
                scores_t(b, 3)
                pv(b, 2)
                scores_t(b, 4)
                pv(b, 3)
                scores_t(b, 5)
                pv(b, 4)
                scores_t(b, 6)
                pv(b, 5)
                scores_t(b, 7)
                pv(b, 6)
                pv(b, 7)
                denominators(b)
                spread(b, 2, db_s)
                proj1(b, 0)
                proj1(b, 1)

            def block2(c):
                group_means(1, c, R[0])
                for k in range(4):
                    conv1(c, k)
                for k in range(4):
                    transpose_x(c, k)
                gram_x(c)
                gram_w(c)
                head_scores(c)
                norms(c)
                k_norm_rows(c)
                transpose_attn(c)
                attn_weights(c)
                t_weights(c)
                t_product(c)
                sp_in(c, 0)
                sp_in(c, 1)
                ci1_product(c)
                ci2a(c)
                for k in range(7):
                    ci2b(c, k)
                map_mean(c)
                attended(c, 0)
                for k in range(4):
                    sp_out(c, k)
                for k in range(1, 4):
                    attended(c, k)
                for k in range(4):
                    proj2(c, k)

            def both(c, b):
                group_means(1, c, R[0])
                group_means(0, b, psB)
                for k in range(4):
                    conv1(c, k)
                center(b)
                for k in range(3):
                    transpose_x(c, k)
                pixel_var(b)
                transpose_x(c, 3)
                gram_x(c)
                spread(b, 1, rbp_s)
                gram_w(c)
                head_scores(c)
                norms(c)
                k_norm_rows(c)
                qk_product(b, 0)
                qk_product(b, 1)
                v_product(b)
                score_rows(b, 0)
                transpose_attn(c)
                score_rows(b, 1)
                attn_weights(c)
                score_rows(b, 2)
                t_weights(c)
                score_rows(b, 3)
                score_rows(b, 4)
                t_product(c)
                score_rows(b, 5)
                score_rows(b, 6)
                ci1_product(c)
                sp_in(c, 0)
                sp_in(c, 1)
                score_rows(b, 7)
                ci2a(c)
                ci2b(c, 0)
                max_rows(b)
                ci2b(c, 1)
                ci2b(c, 2)
                scores_t(b, 0)
                scores_t(b, 1)
                ci2b(c, 3)
                pv(b, 0)
                scores_t(b, 2)
                pv(b, 1)
                scores_t(b, 3)
                pv(b, 2)
                scores_t(b, 4)
                for k in range(4, 7):
                    ci2b(c, k)
                pv(b, 3)
                scores_t(b, 5)
                pv(b, 4)
                scores_t(b, 6)
                sp_out(c, 0)
                pv(b, 5)
                scores_t(b, 7)
                pv(b, 6)
                sp_out(c, 1)
                pv(b, 7)
                map_mean(c)
                sp_out(c, 2)
                sp_out(c, 3)
                denominators(b)
                attended(c, 0)
                attended(c, 1)
                spread(b, 2, db_s)
                attended(c, 2)
                attended(c, 3)
                proj1(b, 0)
                proj1(b, 1)
                for k in range(4):
                    proj2(c, k)

            setup()
            pe.wait_ge(s_su, 9)
            block1(0)
            setup2()
            pe.wait_ge(s_su, 15)
            pe.wait_ge(s_fill, FILLS)
            with pe.Fori(1, B) as i:
                pe.wait_ge(x2_s.sem, x2_s.at(i, 0))
                pe.wait_ge(oo_s.sem, oo_s.at(i - 1, 0))
                both(i - 1, i)
            pe.wait_ge(x2_s.sem, x2_s.at(B, 0))
            pe.wait_ge(oo_s.sem, oo_s.at(B - 1, 0))
            block2(B - 1)

        @block.vector
        def _(dve):
            v = nc.vector

            def setup():
                v.memset(ks[CH:CH + 2, :].bitcast(F32), 1.0).then_inc(s_rows, 1)
                v.memset(X[CH:CH + 1, :, :], 1.0).then_inc(s_rows, 1)
                dve.wait_ge(s_rows, 2)
                dve.wait_ge(s_fill, 1)
                dve.wait_ge(s_w1, 16)
                v.tensor_scalar(lnmat[:, 0:PD], ident[0:PD, 0:PD], par("ln_w"), None, ALU.mult).then_inc(s_ln, 1)
                v.tensor_copy(lnmat[:, PD:PD + 1], par("ln_b")).then_inc(s_ln, 1)
                v.tensor_scalar(var1[:], bn1[:, 3:4], EPS, None, ALU.add).then_inc(s_su, 1)
                v.tensor_scalar(var2[:], bn2[:, 3, :], EPS, None, ALU.add).then_inc(s_su, 1)
                dve.wait_ge(s_isd, 2)
                v.tensor_tensor(inv1[:], bn1[:, 0:1], isd1[:], ALU.mult).then_inc(s_su, 1)
                v.tensor_tensor(inv2[:], bn2[:, 0, :], isd2[:], ALU.mult).then_inc(s_su, 1)
                dve.wait_ge(s_su, 4)
                dve.wait_ge(s_su_pe, 1)
                v.tensor_scalar(wl[:], psA[0:QKV, 0:PD + 1], inv1[:, 0:1], None, ALU.mult).then_inc(s_su, 1)
                for h in range(2):
                    v.tensor_scalar(dinv2[:, h, :], ident[0:CH, 0:CH], inv2[:, h:h + 1], None, ALU.mult)
                v.tensor_tensor(bias2[:], bn2[:, 2, :], inv2[:], ALU.mult)
                v.scalar_tensor_tensor(sh1[:], bn1[:, 2:3], inv1[:, 0:1], bn1[:, 1:2], ALU.mult, ALU.subtract).then_inc(s_su, 1)
                dve.wait_ge(s_su, 6)
                v.tensor_tensor(bias2[:], bn2[:, 1, :], bias2[:], ALU.subtract).then_inc(s_su, 1)
                v.tensor_tensor(wl[:, PD:PD + 1], wl[:, PD:PD + 1], sh1[:], ALU.subtract).then_inc(s_su, 1)
                v.memset(q3w[:], 0.0)
                v.memset(k3w[:], 0.0)
                v.tensor_copy(v1w[:, PD:PD + 1], par("e48")).then_inc(s_ln, 1)
                dve.wait_ge(s_ln, 3)
                dve.wait_ge(s_su_pe, 2)
                for j in range(3):
                    v.tensor_scalar(q3w[:, 32 * j:32 * j + QK], psB[0:PD + 1, 0:QK], QK ** -0.5, None, ALU.mult)
                    v.tensor_copy(k3w[:, 32 * j:32 * j + QK], psB[0:PD + 1, QK:2 * QK])
                v.tensor_copy(v1w[:, 0:PD], psB[0:PD + 1, 2 * QK:QKV])
                dve.wait_ge(s_su_pe, 3)
                v.tensor_copy(wp2[:], psA[0:CH, 0:2 * C].rearrange("p (k c) -> p k c", k=2)).then_inc(s_su, 1)

            def setup2():
                dve.wait_ge(s_w2, 16)
                dve.wait_ge(s_su_pe, 5)
                v.tensor_copy(wc1[0:CH, :, :], R[0][0:CH, 0:2 * C].rearrange("p (h c) -> p h c", h=2)).then_inc(s_su, 1)
                v.tensor_tensor(bci2[:], R[1][:, 0:1], par("b_ci2c"), ALU.add).then_inc(s_su, 1)
                v.tensor_tensor(wb[:], par("ci2cT").unsqueeze(1).broadcast_to([P, 14, C6]),
                                par("w_ci2b").unsqueeze(2).broadcast_to([P, 14, C6]), ALU.mult).then_inc(s_su, 1)
                v.tensor_scalar(hbias[:], par("half_biases"), 0.5, None, ALU.mult).then_inc(s_su, 1)
                v.tensor_scalar(wph[:], par2("w_pr"), 0.5, None, ALU.mult).then_inc(s_su, 1)
                v.tensor_copy(wc1[CH:CH + 1, 0, :], row("row_dw1_b"))
                v.tensor_copy(wmt[CH:CH + 1, 0, :], row("row_cp_out_b"))
                v.tensor_copy(wmc[CH:CH + 1, 0, :], row("row_cp_in_b")).then_inc(s_su, 1)

            def channel_stats(i, b, src):
                s = gst[i]
                if i == 0:
                    dve.wait_ge(x_in.sem, x_in.at(b, 16))
                for k in range(4):
                    h, n = divmod(k, 2)
                    v.bn_stats(st6[i][:, 2 * k:2 * k + 2, :], src[:, h, n * HB:(n + 1) * HB]).then_inc(s.sem, 1)
                dve.wait_ge(s.sem, s.at(b, 4))
                v.tensor_copy(mv[i][:, 0, :], st6[i][:, :, 1]).then_inc(s.sem, 1)
                v.tensor_tensor(msq[i][:], st6[i][:, :, 1], st6[i][:, :, 1], ALU.mult).then_inc(s.sem, 1)
                dve.wait_ge(s.sem, s.at(b, 6))
                v.scalar_tensor_tensor(mv[i][:, 1, :], st6[i][:, :, 2], 2.0 / HB, msq[i][:],
                                       ALU.mult, ALU.add).then_inc(s.sem, 1)

            def group_stats(i, b, ps):
                s = gmm[i]
                dve.wait_ge(gav[i].sem, gav[i].at(b, 1))
                v.tensor_reduce(gm[i][:], ps[0:CH, 0:16].rearrange("p (s h k) -> p s h k", s=2, h=2),
                                AX_X, ALU.add).then_inc(s.sem, 1)
                dve.wait_ge(s.sem, s.at(b, 1))
                v.tensor_tensor(gsq[i][:], gm[i][:, 0, :], gm[i][:, 0, :], ALU.mult).then_inc(s.sem, 1)
                dve.wait_ge(s.sem, s.at(b, 2))
                v.scalar_tensor_tensor(gvar[i][:], gm[i][:, 1, :], EPS, gsq[i][:], ALU.add, ALU.subtract).then_inc(s.sem, 1)

            def group_shift(i, b):
                s = gmm[i]
                dve.wait_ge(grr[i].sem, grr[i].at(b, 1))
                v.scalar_tensor_tensor(gb[i][:], gm[i][:, 0, :], -1.0, gr[i][:], ALU.mult, ALU.mult).then_inc(s.sem, 1)

            def diagonals(b, k, src):
                v.tensor_tensor(dg[:], ident.unsqueeze(1).broadcast_to([P, NKT, P]),
                                src[:].unsqueeze(2).broadcast_to([P, NKT, P]), ALU.mult).then_inc(dg_s.sem, 1)

            def pixel_var(b):
                dve.wait_ge(var_s.sem, var_s.at(b, 1))
                v.tensor_scalar(pv8[:], psB[:, 0:NKT], EPS, None, ALU.add).then_inc(pv_s.sem, 1)

            def rstd_diagonals(b):
                dve.wait_ge(rT_s.sem, rT_s.at(b, 1))
                diagonals(b, 1, rT)

            def layer_norm(b):
                dve.wait_ge(rb_s.sem, rb_s.at(b, 1))
                v.tensor_tensor(xn[0:PD, :], psA[0:PD, :], rb[:], ALU.mult).then_inc(xn_s.sem, 1)

            def q_low(b):
                dve.wait_ge(qk_s.sem, qk_s.at(b, 1))
                v.tensor_tensor(qs[32:64, :], psB[32:64, :], qs[32:64, :].bitcast(F32), ALU.subtract).then_inc(ql_s.sem, 1)

            def k_low(b):
                dve.wait_ge(qk_s.sem, qk_s.at(b, 2))
                v.tensor_tensor(ks[64:96, :], psA[64:96, :], ks[64:96, :].bitcast(F32), ALU.subtract).then_inc(ql_s.sem, 1)

            def v_copy(b):
                dve.wait_ge(qkp_s.sem, qkp_s.at(b, 3))
                v.tensor_copy(vt[:], psO[:].rearrange("p (t c) -> p t c", c=64)[:, :, 0:PD + 1]).then_inc(vt_s.sem, 1)

            def row_max(b, t):
                dve.wait_ge(mx_s.sem, mx_s.at(b, t + 1))
                v.tensor_reduce(nm[:, t:t + 1], (psA, psB)[t % 2][:], AX_X, ALU.max, negate=True).then_inc(nm_s.sem, 1)

            def split_max(b):
                dve.wait_ge(nm_s.sem, nm_s.at(b, NKT))
                v.tensor_copy(nmr[:, :, 0], nm[:]).then_inc(nm_s.sem, 1)
                dve.wait_ge(nm_s.sem, nm_s.at(b, NKT + 1))
                v.tensor_tensor(nmr[:, :, 1], nm[:], nmr[:, :, 0].bitcast(F32), ALU.subtract).then_inc(nm_s.sem, 1)

            def attn_out(b):
                dve.wait_ge(pvd_s.sem, pvd_s.at(b, NKT))
                v.tensor_copy(osb[:, HB:N], psO[64:64 + PD + 1, :]).then_inc(oc_s.sem, 1)

            def denominator_diagonals(b):
                dve.wait_ge(dn_s.sem, dn_s.at(b, 1))
                v.reciprocal(rT[:], psA[:, 0:NKT]).then_inc(dr_s.sem, 1)
                dve.wait_ge(dr_s.sem, dr_s.at(b, 1))
                diagonals(b, 2, rT)

            def attn_relu(b):
                dve.wait_ge(db_s.sem, db_s.at(b, 1))
                dve.wait_ge(xm_s.sem, xm_s.at(b, 2))
                v.scalar_tensor_tensor(xm[0:PD, 0, :], osb[0:PD, :], 0.0, psB[0:PD, :], ALU.max, ALU.mult).then_inc(xo_s.sem, 1)

            def block1_out(b, h):
                dve.wait_ge(y_s.sem, y_s.at(b, h + 1))
                v.scalar_tensor_tensor(x2[:, h, :], (psA, psB)[h][0:CH, :], bias2[:, h:h + 1], xt[:, h, :],
                                       ALU.add, ALU.add).then_inc(x2_s.sem, 1)

            def normed(c):
                dve.wait_ge(gmm[1].sem, gmm[1].at(c, 4))
                for h in range(2):
                    v.tensor_scalar(X[0:CH, h, :], x2[:, h, :], gr[1][:, h:h + 1], gb[1][:, h:h + 1],
                                    ALU.mult, ALU.add).then_inc(X_s.sem, 1)

            def gram_copy(c):
                dve.wait_ge(gp_s.sem, gp_s.at(c, 1))
                v.tensor_copy(gram[:], R[0][0:CH, 0:2 * C].rearrange("p (h c) -> p h c", h=2)).then_inc(ge_s.sem, 1)

            def times_w(c):
                dve.wait_ge(tue_s.sem, tue_s.at(c, 2))
                v.tensor_tensor(prd[:], tu[:], par2("wqkT"), ALU.mult).then_inc(prd_s.sem, 1)

            def clamp_norms(c):
                dve.wait_ge(kn_s.sem, kn_s.at(c, 1))
                v.tensor_scalar(nrm[:], R[0][0:CH, 0:4], 1e-24, None, ALU.max).then_inc(nrm_s.sem, 1)

            def inverse_norms(c):
                s = sm_s
                dve.wait_ge(rn_s.sem, rn_s.at(c, 1))
                for h in range(2):
                    v.tensor_scalar(dk[:, h, :], ident[0:CH, 0:CH], rn[:, 2 + h:3 + h], None, ALU.mult).then_inc(dk_s.sem, 1)
                v.tensor_tensor(rq[:], rn[:, 0:2], par("temp"), ALU.mult).then_inc(s.sem, 1)

            def scaled_scores(c):
                s = sm_s
                dve.wait_ge(rk_s.sem, rk_s.at(c, 1))
                dve.wait_ge(s.sem, s.at(c, 1))
                dve.wait_ge(sc_s.sem, sc_s.at(c, 1))
                for h in range(2):
                    v.scalar_tensor_tensor(s1[:, h, :], R[1][0:CH, h * CH:(h + 1) * CH], rq[:, h:h + 1],
                                           rk[:, h, :], ALU.mult, ALU.mult).then_inc(s.sem, 1)
                dve.wait_ge(s.sem, s.at(c, 3))
                v.tensor_tensor(s2[:], s1[:], par("mask").unsqueeze(1).broadcast_to([CH, 2, CH]), ALU.add).then_inc(s.sem, 1)
                dve.wait_ge(s.sem, s.at(c, 4))
                v.tensor_reduce(smx[:], s2[:], AX_X, ALU.max, negate=True).then_inc(s.sem, 1)

            def softmax_divide(c):
                s = sm_s
                dve.wait_ge(se_s.sem, se_s.at(c, 2))
                v.reciprocal(srec[:], ssum[:]).then_inc(s.sem, 1)
                dve.wait_ge(s.sem, s.at(c, 6))
                for h in range(2):
                    v.tensor_scalar(attn[:, h, :], se[:, h, :], srec[:, h:h + 1], None, ALU.mult).then_inc(s.sem, 1)

            def copy_wma(c):
                dve.wait_ge(mp_s.sem, mp_s.at(c, 1))
                v.tensor_copy(wma[:], R[1][0:CH, 0:2 * C].rearrange("p (h c) -> p h c", h=2)).then_inc(mae_s.sem, 1)

            def copy_wmc(c):
                dve.wait_ge(mp_s.sem, mp_s.at(c, 3))
                v.tensor_copy(wmc[0:CH, :, :], R[2][0:CH, 0:2 * C6].rearrange("p (h c) -> p h c", h=2)).then_inc(mce_s.sem, 1)

            def pad_t(c):
                dve.wait_ge(t4_s.sem, t4_s.at(c, 1))
                img = tp[:].rearrange("p (y x) -> p y x", x=PW)
                for q in range(4):
                    v.tensor_copy(img[0:C6, 1 + 8 * q:9 + 8 * q, 1:1 + WW],
                                  t4[q * C6:(q + 1) * C6, :].rearrange("p (y x) -> p y x", x=WW)).then_inc(tpc_s.sem, 1)

            def ci1_scale(c):
                dve.wait_ge(cip_s.sem, cip_s.at(c, 1))
                v.tensor_scalar(ci1[:], R[0][:, 0:1], 1.0 / N, par("b_ci1"), ALU.mult, ALU.add).then_inc(ci_s.sem, 1)
                dve.wait_ge(ci_s.sem, ci_s.at(c, 1))
                v.tensor_scalar(wco[:], par("wcoT"), ci1[:, 0:1], None, ALU.mult).then_inc(ci_s.sem, 1)

            def channel_product(c):
                dve.wait_ge(cb_s.sem, cb_s.at(c, 1))
                for q in range(4):
                    p = slice(q * C6, (q + 1) * C6)
                    v.scalar_tensor_tensor(pr4[p, q * QB:(q + 1) * QB], R[0][p, 0:QB], bci2[p, 0:1], t4[p, :],
                                           ALU.add, ALU.mult, accum_out=psm[p, :]).then_inc(pr_s.sem, 1)

            def gate_one(c):
                dve.wait_ge(gt_s.sem, gt_s.at(c, 2))
                v.tensor_scalar(gate2[:], gate[:], 1.0, None, ALU.add).then_inc(g2_s.sem, 1)

            def conv2(c, k):
                tap, h = k // 2 + 1, k % 2
                dy, dx = divmod(tap, 3)
                if tap > 1:
                    dve.wait_ge(cv_s.sem, cv_s.at(c, k - 1))
                else:
                    dve.wait_ge(cf_s.sem, cf_s.at(c, h + 1))
                acc = cx[:, h, :].rearrange("p (y x) -> p y x", x=WW)
                v.scalar_tensor_tensor(acc, cp[:, h, dy:dy + HH, dx:dx + WW], par2("wdw2")[:, h, tap:tap + 1], acc,
                                       ALU.mult, ALU.add).then_inc(cv_s.sem, 1)

            def sp_conv(c, k):
                tap, p = k // 2 + 1, k % 2
                dy, dx = divmod(tap, 3)
                if tap > 1:
                    dve.wait_ge(dv_s.sem, dv_s.at(c, k - 1))
                else:
                    dve.wait_ge(df_s.sem, df_s.at(c, 1))
                acc = dd[:, p * HB:(p + 1) * HB].rearrange("p (y x) -> p y x", x=WW)
                v.scalar_tensor_tensor(acc, spp[:, 16 * p + dy:16 * p + dy + 16, dx:dx + WW],
                                       par("w_spdw")[:, tap:tap + 1], acc, ALU.mult, ALU.add).then_inc(dv_s.sem, 1)

            def gelu_product(c):
                dve.wait_ge(gl_s.sem, gl_s.at(c, 1))
                v.tensor_tensor(gmul[SP2:SPN, :], gl[SP2:SPN, :], dd[SP2:SPN, :], ALU.mult).then_inc(gu_s.sem, 1)

            def gate_attended(c, k):
                n, h = divmod(k, 2)
                dve.wait_ge(ap_s.sem, ap_s.at(c, k + 1))
                dve.wait_ge(th_s.sem, th_s.at(c, k + 1))
                v.scalar_tensor_tensor(uu[:, h, n * HB:(n + 1) * HB], th[:, h, n * HB:(n + 1) * HB], 1.0,
                                       R[k % 3][0:CH, :], ALU.add, ALU.mult).then_inc(uu_s.sem, 1)

            def merge(c, k):
                n, h = divmod(k, 2)
                if k == 0:
                    dve.wait_ge(g2_s.sem, g2_s.at(c, 1))
                dve.wait_ge(uu_s.sem, uu_s.at(c, k + 1))
                v.scalar_tensor_tensor(zz[:, h, n * HB:(n + 1) * HB], cx[:, h, n * HB:(n + 1) * HB], gate2[:, h:h + 1],
                                       uu[:, h, n * HB:(n + 1) * HB], ALU.mult, ALU.add).then_inc(zz_s.sem, 1)

            def result(c, k):
                n, h = divmod(k, 2)
                if k == 0:
                    dve.wait_ge(st_out.sem, st_out.at(c, 0))
                dve.wait_ge(op_s.sem, op_s.at(c, k + 1))
                v.tensor_tensor(oo[:, h, n * HB:(n + 1) * HB], R[(k + 1) % 3][0:CH, :],
                                xr[:, h, n * HB:(n + 1) * HB], ALU.add).then_inc(oo_s.sem, 1)

            def block1(b):
                channel_stats(0, b, xt)
                group_stats(0, b, psB)
                group_shift(0, b)
                pixel_var(b)
                rstd_diagonals(b)
                layer_norm(b)
                q_low(b)
                k_low(b)
                v_copy(b)
                for t in range(8):
                    row_max(b, t)
                split_max(b)
                attn_out(b)
                denominator_diagonals(b)
                attn_relu(b)
                block1_out(b, 0)
                block1_out(b, 1)

            def block2(c):
                channel_stats(1, c, x2)
                group_stats(1, c, R[0])
                group_shift(1, c)
                normed(c)
                for k in range(5):
                    conv2(c, k)
                gram_copy(c)
                conv2(c, 5)
                conv2(c, 6)
                times_w(c)
                conv2(c, 7)
                clamp_norms(c)
                conv2(c, 8)
                conv2(c, 9)
                inverse_norms(c)
                conv2(c, 10)
                scaled_scores(c)
                conv2(c, 11)
                softmax_divide(c)
                conv2(c, 12)
                conv2(c, 13)
                copy_wma(c)
                conv2(c, 14)
                copy_wmc(c)
                conv2(c, 15)
                pad_t(c)
                ci1_scale(c)
                for k in range(13):
                    sp_conv(c, k)
                channel_product(c)
                for k in range(13, 16):
                    sp_conv(c, k)
                gate_one(c)
                gelu_product(c)
                for k in range(4):
                    gate_attended(c, k)
                for k in range(4):
                    merge(c, k)
                for k in range(4):
                    result(c, k)

            def both(c, b):
                channel_stats(1, c, x2)
                channel_stats(0, b, xt)
                group_stats(1, c, R[0])
                group_stats(0, b, psB)
                group_shift(1, c)
                normed(c)
                group_shift(0, b)
                for k in range(5):
                    conv2(c, k)
                pixel_var(b)
                conv2(c, 5)
                conv2(c, 6)
                rstd_diagonals(b)
                conv2(c, 7)
                gram_copy(c)
                conv2(c, 8)
                conv2(c, 9)
                times_w(c)
                conv2(c, 10)
                clamp_norms(c)
                conv2(c, 11)
                conv2(c, 12)
                inverse_norms(c)
                layer_norm(b)
                for k in range(13, 16):
                    conv2(c, k)
                q_low(b)
                scaled_scores(c)
                k_low(b)
                softmax_divide(c)
                v_copy(b)
                row_max(b, 0)
                row_max(b, 1)
                copy_wma(c)
                row_max(b, 2)
                copy_wmc(c)
                row_max(b, 3)
                row_max(b, 4)
                pad_t(c)
                row_max(b, 5)
                row_max(b, 6)
                ci1_scale(c)
                row_max(b, 7)
                split_max(b)
                for k in range(16):
                    sp_conv(c, k)
                gelu_product(c)
                channel_product(c)
                attn_out(b)
                gate_one(c)
                denominator_diagonals(b)
                gate_attended(c, 0)
                gate_attended(c, 1)
                attn_relu(b)
                gate_attended(c, 2)
                gate_attended(c, 3)
                for k in range(4):
                    merge(c, k)
                block1_out(b, 0)
                block1_out(b, 1)
                for k in range(4):
                    result(c, k)

            dve.sem_inc(oo_s.sem, 1)
            dve.sem_inc(st_out.sem, 1)
            setup()
            block1(0)
            setup2()
            dve.wait_ge(s_fill, FILLS)
            with dve.Fori(1, B) as i:
                dve.wait_ge(x2_s.sem, x2_s.at(i, 0))
                dve.wait_ge(oo_s.sem, oo_s.at(i - 1, 0))
                both(i - 1, i)
            dve.wait_ge(x2_s.sem, x2_s.at(B, 0))
            block2(B - 1)

        @block.scalar
        def _(act):
            a = nc.scalar.activation
            ID = ACT.Identity

            def normed1(b):
                act.wait_ge(gmm[0].sem, gmm[0].at(b, 4))
                a(xa[:], xt[0:PD, 0, :], ID, bias=gb[0][0:PD, 0:1], scale=gr[0][0:PD, 0:1]).then_inc(xa_s.sem, 1)

            def squares(b):
                act.wait_ge(xc_s.sem, xc_s.at(b, 1))
                a(sq[:], psA[0:PD, :], ACT.Square).then_inc(sq_s.sem, 1)

            def relu_normed(b, h):
                a(xm[:, h, :], xt[:, h, :], ACT.Relu, bias=gb[0][:, h:h + 1],
                  scale=gr[0][:, h:h + 1]).then_inc(xm_s.sem, 1)

            def rstd_rows(b):
                act.wait_ge(rbp_s.sem, rbp_s.at(b, 1))
                a(rb[:], psB[0:PD, :], ACT.Copy).then_inc(rb_s.sem, 1)

            def q_high(b):
                act.wait_ge(qkp_s.sem, qkp_s.at(b, 1))
                a(qs[0:CH, :], psB[0:CH, :], ACT.Copy).then_inc(qk_s.sem, 1)

            def k_high(b):
                act.wait_ge(qkp_s.sem, qkp_s.at(b, 2))
                a(ks[0:CH, :], psA[0:CH, :], ACT.Copy).then_inc(qk_s.sem, 1)

            def max_copy(b):
                act.wait_ge(tm_s.sem, tm_s.at(b, 1))
                a(qs[CH:CH + 2, :], psB[0:2, :], ACT.Copy).then_inc(qm_s.sem, 1)

            def exps(b, t):
                act.wait_ge(st_s.sem, st_s.at(b, t + 1))
                if t >= 2:
                    act.wait_ge(pvd_s.sem, pvd_s.at(b, t - 1))
                a(pT[t % 2][:], (psA, psB)[t % 2][:], ACT.Exp).then_inc(ex_s.sem, 1)

            def attn_out(b):
                act.wait_ge(pvd_s.sem, pvd_s.at(b, NKT))
                a(osb[:, 0:HB], psO[0:PD + 1, :], ACT.Copy).then_inc(oc_s.sem, 1)

            def residual(c, h):
                a(xr[:, h, :], x2[:, h, :], ID, bias=par("b_pr")[:, h:h + 1]).then_inc(xr_s.sem, 1)

            def pad_conv1(c, k):
                h, n = divmod(k, 2)
                act.wait_ge(c1_s.sem, c1_s.at(c, k + 1))
                a(cp[:, h, 1 + 16 * n:17 + 16 * n, 1:1 + WW],
                  R[(1, 2, 0, 1)[k]][0:CH, :].rearrange("p (y x) -> p y x", x=WW), ACT.Copy).then_inc(ce_s.sem, 1)

            def conv2_first(c, h):
                act.wait_ge(ce_s.sem, ce_s.at(c, 2 * h + 2))
                a(cx[:, h, :].rearrange("p (y x) -> p y x", x=WW), cp[:, h, 0:HH, 0:WW], ID,
                  bias=par("bdw2")[:, h:h + 1], scale=par2("wdw2")[:, h, 0:1]).then_inc(cf_s.sem, 1)

            def copy_xT(c, k):
                act.wait_ge(xtp_s.sem, xtp_s.at(c, k + 1))
                a(xT[:, 2 * k:2 * k + 2, :], R[(2, 0, 1, 2)[k]][:, 0:4 * CH].rearrange("p (t c) -> p t c", t=2),
                  ACT.Copy).then_inc(xte_s.sem, 1)

            def copy_tu(c, jh):
                act.wait_ge(tup_s.sem, tup_s.at(c, jh + 1))
                a(tu[:, jh, :], R[1 + jh][0:CH, 0:2 * C], ACT.Copy).then_inc(tue_s.sem, 1)

            def copy_k_norms(c):
                act.wait_ge(kr_s.sem, kr_s.at(c, 1))
                a(rk[:], R[2][0:CH, 0:2 * CH].rearrange("p (h c) -> p h c", h=2), ACT.Copy).then_inc(rk_s.sem, 1)

            def head_exps(c):
                act.wait_ge(sm_s.sem, sm_s.at(c, 5))
                for h in range(2):
                    a(se[:, h, :], s2[:, h, :], ACT.Exp, bias=smx[:, h:h + 1],
                      accum_out=ssum[:, h:h + 1]).then_inc(se_s.sem, 1)

            def copy_attT(c):
                act.wait_ge(at_s.sem, at_s.at(c, 1))
                a(attT[:], R[2][0:CH, 0:2 * CH].rearrange("p (h c) -> p h c", h=2), ACT.Copy).then_inc(ate_s.sem, 1)

            def copy_wmt(c):
                act.wait_ge(mp_s.sem, mp_s.at(c, 2))
                a(wmt[0:CH, :, :], R[0][0:CH, 0:2 * C].rearrange("p (h c) -> p h c", h=2),
                  ACT.Copy).then_inc(mte_s.sem, 1)

            def copy_t(c):
                act.wait_ge(tt_s.sem, tt_s.at(c, 1))
                a(t4[:], R[0][:, 0:QB], ACT.Copy, accum_out=tsum[:]).then_inc(t4_s.sem, 1)

            def pad_ci2a(c):
                act.wait_ge(ca_s.sem, ca_s.at(c, 1))
                img = up[:].rearrange("p (y x) -> p y x", x=UW)
                for q in range(4):
                    p0 = q * C6
                    a(img[0:C6, 9 + 8 * q:17 + 8 * q, 9:9 + WW],
                      R[0][p0:p0 + C6, 0:QB].rearrange("p (y x) -> p y x", x=WW), ID,
                      bias=par("b_ci2a")[p0:p0 + C6, :]).then_inc(ue_s.sem, 1)

            def channel_gate(c):
                act.wait_ge(cm_s.sem, cm_s.at(c, 1))
                for h in range(2):
                    a(gate[:, h:h + 1], R[0][0:CH, h:h + 1], ACT.Tanh, bias=hbias[:, 2 + h:3 + h],
                      scale=0.5 / N).then_inc(gt_s.sem, 1)

            def pad_sp(c, n):
                act.wait_ge(spi_s.sem, spi_s.at(c, n + 1))
                a(spp[:, 1 + 16 * n:17 + 16 * n, 1:1 + WW],
                  R[1 + n][0:SPN, :].rearrange("p (y x) -> p y x", x=WW), ID,
                  bias=par("b_spi")).then_inc(spe_s.sem, 1)

            def sp_first(c):
                act.wait_ge(spe_s.sem, spe_s.at(c, 2))
                a(dd[:].rearrange("p (y x) -> p y x", x=WW), spp[:, 0:HH, 0:WW], ID, bias=par("b_spdw"),
                  scale=par("w_spdw")[:, 0:1]).then_inc(df_s.sem, 1)

            def gelu(c):
                act.wait_ge(dv_s.sem, dv_s.at(c, 16))
                a(gl[SP2:SPN, :], dd[0:PD, :], ACT.Gelu).then_inc(gl_s.sem, 1)

            def spatial_tanh(c, k):
                n, h = divmod(k, 2)
                act.wait_ge(spo_s.sem, spo_s.at(c, k + 1))
                a(th[:, h, n * HB:(n + 1) * HB], R[1 + h][0:CH, :], ACT.Tanh, scale=0.5,
                  bias=hbias[:, h:h + 1]).then_inc(th_s.sem, 1)

            def block1(b):
                normed1(b)
                squares(b)
                relu_normed(b, 0)
                relu_normed(b, 1)
                rstd_rows(b)
                q_high(b)
                k_high(b)
                max_copy(b)
                for t in range(8):
                    exps(b, t)
                attn_out(b)

            def block2(c):
                residual(c, 0)
                residual(c, 1)
                pad_conv1(c, 0)
                pad_conv1(c, 1)
                conv2_first(c, 0)
                pad_conv1(c, 2)
                pad_conv1(c, 3)
                conv2_first(c, 1)
                for k in range(4):
                    copy_xT(c, k)
                copy_tu(c, 0)
                copy_tu(c, 1)
                copy_k_norms(c)
                head_exps(c)
                copy_attT(c)
                copy_wmt(c)
                copy_t(c)
                pad_sp(c, 0)
                pad_sp(c, 1)
                sp_first(c)
                pad_ci2a(c)
                channel_gate(c)
                gelu(c)
                for k in range(4):
                    spatial_tanh(c, k)

            def both(c, b):
                residual(c, 0)
                residual(c, 1)
                normed1(b)
                for k in range(3):
                    pad_conv1(c, k)
                conv2_first(c, 0)
                pad_conv1(c, 3)
                conv2_first(c, 1)
                squares(b)
                relu_normed(b, 0)
                relu_normed(b, 1)
                for k in range(4):
                    copy_xT(c, k)
                rstd_rows(b)
                copy_tu(c, 0)
                copy_tu(c, 1)
                copy_k_norms(c)
                q_high(b)
                k_high(b)
                head_exps(c)
                copy_attT(c)
                copy_wmt(c)
                copy_t(c)
                pad_sp(c, 0)
                pad_sp(c, 1)
                sp_first(c)
                pad_ci2a(c)
                max_copy(b)
                for t in range(3):
                    exps(b, t)
                gelu(c)
                for t in range(3, 7):
                    exps(b, t)
                spatial_tanh(c, 0)
                exps(b, 7)
                spatial_tanh(c, 1)
                channel_gate(c)
                attn_out(b)
                spatial_tanh(c, 2)
                spatial_tanh(c, 3)

            act.wait_ge(s_w1, 16)
            block1(0)
            act.wait_ge(s_w2, 16)
            act.wait_ge(s_su, 15)
            act.wait_ge(s_fill, FILLS)
            with act.Fori(1, B) as i:
                act.wait_ge(x2_s.sem, x2_s.at(i, 0))
                act.wait_ge(oo_s.sem, oo_s.at(i - 1, 0))
                both(i - 1, i)
            act.wait_ge(x2_s.sem, x2_s.at(B, 0))
            act.wait_ge(oo_s.sem, oo_s.at(B - 1, 0))
            block2(B - 1)

        @block.gpsimd
        def _(pool):
            g = nc.gpsimd

            def rsqrt(dst, src):
                n = src.shape[-1]
                return g.tensor_tensor(dst, src, mhalf[0:src.shape[0], 0:n], ALU.pow)

            def group_rstd(i, b):
                pool.wait_ge(gmm[i].sem, gmm[i].at(b, 3))
                rsqrt(gr[i][:], gvar[i][:]).then_inc(grr[i].sem, 1)

            def pixel_rstd(b):
                pool.wait_ge(pv_s.sem, pv_s.at(b, 1))
                rsqrt(rT[:], pv8[:]).then_inc(rT_s.sem, 1)

            def inverse_norms(c):
                pool.wait_ge(nrm_s.sem, nrm_s.at(c, 1))
                rsqrt(rn[:], nrm[:]).then_inc(rn_s.sem, 1)

            def block1(b):
                group_rstd(0, b)
                pixel_rstd(b)

            def block2(c):
                group_rstd(1, c)
                inverse_norms(c)

            def both(c, b):
                group_rstd(1, c)
                group_rstd(0, b)
                pixel_rstd(b)
                inverse_norms(c)

            g.memset(xn[:], 1.0).then_inc(s_fill, 1)
            g.memset(mhalf[:], -0.5).then_inc(s_fill, 1)
            pool.wait_ge(s_fill, 2)
            pool.wait_ge(s_su, 2)
            rsqrt(isd1[:], var1[:]).then_inc(s_isd, 1)
            rsqrt(isd2[:], var2[:]).then_inc(s_isd, 1)
            block1(0)
            g.memset(tp[:], 0.0).then_inc(s_fill, 1)
            g.memset(up[:], 0.0).then_inc(s_fill, 1)
            g.memset(cp[:, 0, :, :], 0.0).then_inc(s_fill, 1)
            g.memset(cp[:, 1, :, :], 0.0).then_inc(s_fill, 1)
            g.memset(spp[:], 0.0).then_inc(s_fill, 1)
            g.memset(pr4[:], 0.0).then_inc(s_fill, 1)
            pool.wait_ge(s_w2, 16)
            with pool.Fori(1, B) as i:
                pool.wait_ge(x2_s.sem, x2_s.at(i, 0))
                pool.wait_ge(oo_s.sem, oo_s.at(i - 1, 0))
                both(i - 1, i)
            pool.wait_ge(x2_s.sem, x2_s.at(B, 0))
            pool.wait_ge(oo_s.sem, oo_s.at(B - 1, 0))
            block2(B - 1)


def constants():
    k = np.arange(CH)
    same_group = (k[:, None] // GROUP) == (k[None, :] // GROUP)
    same_head = (k[:, None] // HD) == (k[None, :] // HD)
    e48 = np.zeros((PD + 1, 1), np.float32)
    e48[PD] = 1.0
    return {
        "ident": np.eye(P), "gavg": same_group / (4 * GROUP), "center": np.pad(np.eye(PD) - 1.0 / PD, ((0, 0), (0, CH - PD))),
        "mean48": np.full((PD, 1), 1.0 / PD), "ones": np.ones((P, CH)), "e48": e48,
        "mask": np.where(same_head, 0.0, MASKED),
    }


def pack(p):
    f = {k: np.asarray(v) for k, v in p.items()}
    l0 = {k[8:]: v for k, v in f.items() if k.startswith("L0_conv_")}
    l1 = {k[8:]: v for k, v in f.items() if k.startswith("L1_conv_")}

    def halves(m):
        return m.reshape(2, CH, -1).transpose(1, 0, 2).reshape(CH, -1)

    def split_sp(m):
        o = np.zeros(m.shape[:-1] + (SPN,), np.float32)
        o[..., 0:PD], o[..., SP2:SPN] = m[..., 0:PD], m[..., PD:2 * PD]
        return o

    w2a = l1["ci2a_w"][:, 0]
    w_ci2a = np.zeros((3, C6, 3, C6), np.float32)
    for ch in range(C6):
        w_ci2a[:, ch, :, ch] = w2a[ch].T
    w_ci2b = np.zeros((4, C6, 7, 2), np.float32)
    for dx in range(7):
        w_ci2b[dx % 4, :, :, dx // 4] = l1["ci2b_w"][:, 0, :, dx]
    w_spo = np.zeros((SPN, C), np.float32)
    w_spo[SP2:SPN] = l1["sp_out_w"][:, :, 0, 0].T
    ci2cT = l1["ci2c_w"][:, :, 0, 0].T
    blocks = {
        **constants(),
        "ln_w": l0["ln_w"][:, None], "ln_b": l0["ln_b"][:, None], "wqkvT": l0["w_qkv"].T,
        "bn1": np.stack([l0[f"bn1_{k}"] for k in "gbmv"], 1),
        "wproj": halves(l0["w_proj"]),
        "bn2": np.concatenate([halves(l0[f"bn2_{k}"][:, None]) for k in "gbmv"], 1),
        "wqkT": halves(l1["qkv_w"][0:2 * C].T), "wv": halves(l1["qkv_w"][2 * C:]),
        "wdw1T": halves(l1["dw1_w"][:, :, 0, 0].T), "wcpT": halves(l1["cp_in_w"][:, :, 0, 0].T),
        "wdw2": halves(l1["dw2_w"].reshape(C, 9)), "bdw2": halves(l1["dw2_b"][:, None]),
        "temp": halves(np.repeat(l1["temperature"].reshape(-1), HD)[:, None]),
        "w_ci1": np.tile(l1["ci1_w"][:, :, 0, 0].T, (4, 4)), "b_ci1": np.tile(l1["ci1_b"], 4)[:, None],
        "w_ci2a": w_ci2a.reshape(CH, 3 * C6), "b_ci2a": np.tile(l1["ci2a_b"], 4)[:, None],
        "ci2cT": np.tile(ci2cT, (4, 1)), "w_ci2b": w_ci2b.reshape(P, 14),
        "ci2cT_rep": np.tile(ci2cT, (1, 4)), "b_ci2b": l1["ci2b_b"][:, None],
        "b_ci2c": np.tile(l1["ci2c_b"], 4)[:, None], "wcoT": np.tile(l1["cp_out_w"][:, :, 0, 0].T, (4, 1)),
        "half_biases": np.concatenate([halves(l1["sp_out_b"][:, None]), halves(l1["cp_out_b"][:, None])], 1),
        "w_spi": split_sp(halves(l1["sp_in_w"][:, :, 0, 0].T).reshape(CH, 2, 2 * PD)).reshape(CH, -1),
        "b_spi": split_sp(l1["sp_in_b"])[:, None], "w_spdw": split_sp(l1["sp_dw_w"].reshape(2 * PD, 9).T).T,
        "b_spdw": split_sp(l1["sp_dw_b"])[:, None], "w_spo": w_spo,
        "w_pr": halves(l1["proj_w"].T), "b_pr": halves(l1["proj_b"][:, None]),
    }
    out = np.zeros((P, NW), np.float32)
    for name, (parts, off, cols) in AT.items():
        if name.startswith("row_"):
            out[CH, off:off + cols] = l1[name[4:]]
        else:
            out[0:parts, off:off + cols] = blocks[name]
    return out


def kernel(**inputs):
    import concourse.bacc as bacc
    from concourse.bass_utils import run_bass_kernel_spmd

    x = np.ascontiguousarray(np.asarray(inputs["x"]).reshape(B, 2, CH, N))
    params = pack({k: v for k, v in inputs.items() if k != "x"})
    nc = bacc.Bacc("TRN2", target_bir_lowering=False, num_devices=1)
    x_ap = nc.dram_tensor("x_dram", x.shape, F32, kind="ExternalInput").ap()
    p_ap = nc.dram_tensor("params_dram", params.shape, F32, kind="ExternalInput").ap()
    o_ap = nc.dram_tensor("out_dram", x.shape, F32, kind="ExternalOutput").ap()
    build(nc, x_ap, p_ap, o_ap)
    r = run_bass_kernel_spmd(nc, [{"x_dram": x, "params_dram": params}], core_ids=[0])
    return r.results[0]["out_dram"].reshape(B, C, HH, WW)
```

```python
from contextlib import ExitStack

import numpy as np

import concourse.bass as bass
from concourse import mybir

F32 = mybir.dt.float32
F32R = mybir.dt.float32r
ALU = mybir.AluOpType
ACT = mybir.ActivationFunctionType
AX_X = mybir.AxisListType.X

B, C, HH, WW = 4, 192, 32, 32
N = HH * WW
P = 128
CH = C // 2
GROUP = C // 32
PD, QK = 48, 16
QKV = 2 * QK + PD
NKT = N // P
HB = N // 2
QB = N // 4
C6 = C // 6
HD = C // 8
EPS = 1e-5
PW = WW + 2
UW = WW + 18
SP2 = 64
SPN = SP2 + PD
MASKED = -1e30
FILLS = 8

FIRST = {
    "ident": (P, P), "gavg": (CH, CH), "center": (SPN, SPN), "mean_rows": (SPN, 2), "ones": (P, CH),
    "pick_den": (SPN + 1, 2), "pick_one": (SPN + 1, 1), "ln_w": (PD, 1), "ln_b": (PD, 1), "wqkvT": (PD, QKV),
    "bn1": (QKV, 4), "wproj": (CH, 2 * C), "bn2": (CH, 8),
}
SECOND = {
    "wqkT": (CH, 2 * 2 * C), "wv": (CH, 2 * C), "wdw1T": (CH, 2 * C), "wcpT": (CH, 2 * C6),
    "row_dw1_b": (CH + 1, C), "row_cp_in_b": (CH + 1, C6), "row_cp_out_b": (CH + 1, C),
    "wdw2": (CH, 2 * 9), "bdw2": (CH, 2), "temp": (CH, 2), "mask": (CH, CH),
    "w_ci1": (P, P), "b_ci1": (P, 1), "w_ci2a": (CH, 3 * C6), "b_ci2a": (P, 1),
    "ci2cT": (P, C6), "w_ci2b": (P, 14), "ci2cT_rep": (C6, P), "b_ci2b": (C6, 1), "b_ci2c": (P, 1),
    "wcoT": (P, C), "half_biases": (CH, 4), "w_spi": (CH, 2 * SPN), "b_spi": (SPN, 1),
    "w_spdw": (SPN, 9), "b_spdw": (SPN, 1), "w_spo": (SPN, 2 * C), "w_pr": (CH, 2 * C), "b_pr": (CH, 2),
}


def place(blocks, start):
    at = {}
    for name, (parts, cols) in blocks.items():
        at[name] = (parts, start, cols)
        start += cols
    return at, start


AT1, N1 = place(FIRST, 0)
AT2, NW = place(SECOND, N1)
AT = {**AT1, **AT2}


class Signal:

    def __init__(self, sem, per, before=0):
        self.sem, self.per, self.before = sem, per, before

    def at(self, b, k):
        return b * self.per + (k + self.before)


def build(nc, x, params, out):
    with ExitStack() as ctx:
        def sb(name, shape, dt=F32):
            return ctx.enter_context(nc.sbuf_tensor(name, shape, dt))

        def psum(name, shape):
            return ctx.enter_context(nc.psum_tensor(name, shape, F32))

        def sem(name):
            return ctx.enter_context(nc.semaphore(name))

        def sig(name, per, before=0):
            return Signal(sem(name), per, before)

        psA = psum("psA", [P, N])
        psB = psum("psB", [P, N])
        psO = psum("psO", [P, HB])
        R = [psum(f"psR{i}", [P, HB]) for i in range(3)]

        wt = sb("wt", [P, NW])

        def par(name):
            parts, off, cols = AT[name]
            return wt[0:parts, off:off + cols]

        def par2(name):
            return par(name).rearrange("p (h c) -> p h c", h=2)

        ident, ones = par("ident"), par("ones")
        lnmat = sb("lnmat", [PD, PD + 1])
        mhalf = sb("mhalf", [P, NKT])
        var1 = sb("var1", [QKV, 1])
        isd1 = sb("isd1", [QKV, 1])
        inv1 = sb("inv1", [QKV, 1])
        sh1 = sb("sh1", [QKV, 1])
        wl = sb("wl", [QKV, 2, SPN + 1])
        q3w = sb("q3w", [SPN + 1, 2, CH])
        k3w = sb("k3w", [SPN + 1, 2, CH])
        v1w = sb("v1w", [SPN + 1, 2, PD + 1])
        var2 = sb("var2", [CH, 2])
        isd2 = sb("isd2", [CH, 2])
        inv2 = sb("inv2", [CH, 2])
        dinv2 = sb("dinv2", [CH, 2, CH])
        bias2 = sb("bias2", [CH, 2])
        wp2 = sb("wp2", [CH, 2, C])
        wc1 = sb("wc1", [CH + 1, 2, C])
        wb = sb("wb", [P, 14, C6])
        bci2 = sb("bci2", [P, 1])
        hbias = sb("hbias", [CH, 4])
        wph = sb("wph", [CH, 2, C])

        xt = sb("xt", [CH, 2, N])
        st6 = [sb(f"st6_{i}", [CH, 8, 3]) for i in range(2)]
        mv = [sb(f"mv_{i}", [CH, 2, 8]) for i in range(2)]
        msq = [sb(f"msq_{i}", [CH, 8]) for i in range(2)]
        gm = [sb(f"gm_{i}", [CH, 2, 2]) for i in range(2)]
        gsq = [sb(f"gsq_{i}", [CH, 2]) for i in range(2)]
        gvar = [sb(f"gvar_{i}", [CH, 2]) for i in range(2)]
        gr = [sb(f"gr_{i}", [CH, 2]) for i in range(2)]
        gb = [sb(f"gb_{i}", [CH, 2]) for i in range(2)]
        xa = sb("xa", [SPN, HB])
        sq = sb("sq", [SPN, HB])
        pv8 = sb("pv8", [P, NKT])
        rT = sb("rT", [P, NKT])
        dg = sb("dg", [P, NKT, P])
        rb = sb("rb", [SPN, HB])
        xn = sb("xn", [SPN + 1, HB])
        qs = sb("qs", [P, N], F32R)
        ks = sb("ks", [P, N], F32R)
        vt = sb("vt", [P, NKT, SP2])
        nm = sb("nm", [P, NKT])
        nmr = sb("nmr", [P, NKT, 2], F32R)
        pT = [sb(f"pT{i}", [P, N]) for i in range(2)]
        osb = sb("osb", [P, HB])
        xm = sb("xm", [CH, 2, N])
        x2 = sb("x2", [CH, 2, N])

        X = sb("X", [CH + 1, 2, N])
        xr = sb("xr", [CH, 2, N])
        cp = sb("cp", [CH, 2, PW, PW])
        cx = sb("cx", [CH, 2, N])
        xT = sb("xT", [P, NKT, C])
        gram = sb("gram", [CH, 2, C])
        tu = sb("tu", [CH, 2, 2 * C])
        prd = sb("prd", [CH, 2, 2 * C])
        nrm = sb("nrm", [CH, 4])
        rn = sb("rn", [CH, 4])
        dk = sb("dk", [CH, 2, CH])
        rk = sb("rk", [CH, 2, CH])
        rq = sb("rq", [CH, 2])
        s1 = sb("s1", [CH, 2, CH])
        s2 = sb("s2", [CH, 2, CH])
        smx = sb("smx", [CH, 2])
        se = sb("se", [CH, 2, CH])
        ssum = sb("ssum", [CH, 2])
        srec = sb("srec", [CH, 2])
        attn = sb("attn", [CH, 2, CH])
        attT = sb("attT", [CH, 2, CH])
        wmt = sb("wmt", [CH + 1, 2, C])
        wma = sb("wma", [CH, 2, C])
        wmc = sb("wmc", [CH + 1, 2, C6])
        t4 = sb("t4", [P, QB])
        tsum = sb("tsum", [P, 1])
        tp = sb("tp", [CH, PW * PW])
        up = sb("up", [P, UW * UW])
        ci1 = sb("ci1", [P, 1])
        wco = sb("wco", [P, C])
        pr4 = sb("pr4", [P, N])
        psm = sb("psm", [P, 1])
        gate = sb("gate", [CH, 2])
        gate2 = sb("gate2", [CH, 2])
        spp = sb("spp", [SPN, PW, PW])
        dd = sb("dd", [SPN, N])
        gl = sb("gl", [SPN, N])
        gmul = sb("gmul", [SPN, HB])
        th = sb("th", [CH, 2, N])
        uu = sb("uu", [CH, 2, N])
        zz = uu
        oo = sb("oo", [CH, 2, N])

        s_w1, s_w2 = sem("params1_loaded"), sem("params2_loaded")
        s_fill, s_rows = sem("constants_filled"), sem("rows_of_ones")
        s_isd = sem("setup_rsqrt")
        s_ln = sem("lnmat_ready")
        s_su_pe = sem("setup_products")
        s_su = sem("setup_vector_steps")

        x_in = [sig(f"x_in_{h}", 16) for h in range(2)]
        gst = [sig(f"channel_stats_{i}", 7) for i in range(2)]
        gav = [sig(f"group_means_{i}", 1) for i in range(2)]
        gmm = [sig(f"group_steps_{i}", 4) for i in range(2)]
        grr = [sig(f"group_rstd_{i}", 1) for i in range(2)]
        xa_s = sig("attended_normed", 2)
        xm_s = sig("relu_normed", 2)
        xc_s = sig("centered", 1)
        sq_s = sig("squares", 1)
        var_s = sig("pixel_vars", 1)
        pv_s = sig("pixel_vars_copied", 1)
        rT_s = sig("pixel_rstd", 1)
        dg_s = sig("diagonals", 2)
        rbp_s = sig("rstd_rows", 1)
        rb_s = sig("rstd_rows_copied", 1)
        xn_s = sig("layer_normed", 1)
        qkp_s = sig("qkv_products", 3)
        qk_s = sig("qk_high_parts", 2)
        ql_s = sig("qk_low_parts", 2)
        vt_s = sig("vT_copied", 1)
        mx_s = sig("score_rows", NKT)
        nm_s = sig("row_max_steps", NKT + 2)
        tm_s = sig("max_rows", 1)
        qm_s = sig("max_rows_copied", 1)
        st_s = sig("scores_t", NKT)
        ex_s = sig("exps", NKT)
        pvd_s = sig("pv_done", NKT)
        oc_s = sig("attn_out_copied", 1)
        dn_s = sig("denominators", 1)
        dr_s = sig("denominators_inverted", 1)
        db_s = sig("denominator_rows", 1)
        xo_s = sig("attn_relu", 2)
        y_s = sig("proj1", 2)
        x2_s = sig("block1_out", 2)

        X_s = sig("normed2", 2)
        xr_s = sig("residual_biased", 2)
        c1_s = sig("conv1_product", 4)
        ce_s = sig("conv1_padded", 4)
        cf_s = sig("conv2_first_tap", 2)
        cv_s = sig("conv2_taps", 16)
        xtp_s = sig("xT_product", 4)
        xte_s = sig("xT_copied", 4)
        gp_s = sig("gram_product", 1)
        ge_s = sig("gram_copied", 1)
        tup_s = sig("tu_product", 2)
        tue_s = sig("tu_copied", 2)
        prd_s = sig("tu_times_w", 1)
        kn_s = sig("norms_product", 1)
        nrm_s = sig("norms_clamped", 1)
        rn_s = sig("inverse_norms", 1)
        dk_s = sig("k_norm_diagonals", 2)
        kr_s = sig("k_norm_rows", 1)
        rk_s = sig("k_norm_rows_copied", 1)
        sc_s = sig("head_scores", 1)
        sm_s = sig("head_softmax_steps", 8)
        se_s = sig("head_exps", 2)
        at_s = sig("attn_transposed", 1)
        ate_s = sig("attn_transposed_copied", 1)
        mp_s = sig("attn_wv_products", 3)
        mte_s = sig("wmt_copied", 1)
        mae_s = sig("wma_copied", 1)
        mce_s = sig("wmc_copied", 1)
        tt_s = sig("t_product", 1)
        t4_s = sig("t_copied", 1)
        tpc_s = sig("t_padded", 4)
        tpd_s = sig("t_shifted_copies", 32)
        ca_s = sig("ci2a_product", 1)
        ue_s = sig("ci2a_padded", 4)
        ud_s = sig("ci2a_shifted_copies", 48)
        cip_s = sig("ci1_product", 1)
        ci_s = sig("ci1_steps", 2)
        cb_s = sig("ci2_product", 1)
        pr_s = sig("channel_product", 4)
        cm_s = sig("channel_map_mean", 1)
        gt_s = sig("gate_tanh", 2)
        g2_s = sig("gate_plus_one", 1)
        spi_s = sig("sp_in_product", 2)
        spe_s = sig("sp_in_padded", 2)
        df_s = sig("sp_first_tap", 1)
        dv_s = sig("sp_conv", 16)
        gl_s = sig("gelu", 2)
        gu_s = sig("gelu_times_x2", 2)
        spo_s = sig("sp_out_product", 4)
        th_s = sig("spatial_tanh", 4)
        ap_s = sig("attended_product", 4)
        uu_s = sig("attended_gated", 4)
        zz_s = sig("merged", 4)
        op_s = sig("proj2", 4)
        oo_s = sig("out_copied", 4, before=1)
        st_out = sig("out_stored", 64, before=1)

        bn1 = par("bn1")
        bn2 = par("bn2").rearrange("p (f h) -> p f h", f=4)

        def row(name):
            _, off, cols = AT[name]
            return wt[CH:CH + 1, off:off + cols]

        def halves(ps):
            return [ps[:, 0:HB], ps[:, HB:N]]

        block = ctx.enter_context(nc.Block())

        @block.sync
        def _(sp):
            sp.dma_start(wt[:, 0:N1], params[:, 0:N1]).then_inc(s_w1, 16)

            def load_x(b):
                for h in range(2):
                    sp.dma_start(xt[:, h, :], x[b, h]).then_inc(x_in[h].sem, 16)

            def shift_t(c):
                sp.wait_ge(tpc_s.sem, tpc_s.at(c, 4))
                for j in (1, 2):
                    lo, hi = PW, PW * (1 + HH)
                    sp.dma_start(tp[j * C6:(j + 1) * C6, lo - j:hi - j], tp[0:C6, lo:hi]).then_inc(tpd_s.sem, 16)

            def shift_u(c):
                sp.wait_ge(ue_s.sem, ue_s.at(c, 4))
                for j in (1, 2, 3):
                    lo, hi = UW * 9, UW * (9 + HH)
                    sp.dma_start(up[j * C6:(j + 1) * C6, lo - 3 * j:hi - 3 * j],
                                 up[0:C6, lo:hi]).then_inc(ud_s.sem, 16)

            def store(c):
                for k in range(4):
                    n, h = divmod(k, 2)
                    sp.wait_ge(oo_s.sem, oo_s.at(c, k + 1))
                    sp.dma_start(out[c, h, :, n * HB:(n + 1) * HB],
                                 oo[:, h, n * HB:(n + 1) * HB]).then_inc(st_out.sem, 16)

            def block2(c):
                shift_t(c)
                shift_u(c)
                store(c)

            load_x(0)
            sp.dma_start(wt[:, N1:NW], params[:, N1:NW]).then_inc(s_w2, 16)
            with sp.Fori(1, B) as i:
                sp.wait_ge(x2_s.sem, x2_s.at(i, 0))
                load_x(i)
                block2(i - 1)
            block2(B - 1)
            sp.wait_ge(st_out.sem, st_out.at(B - 1, 64))

        @block.tensor
        def _(pe):
            mm = nc.tensor.matmul

            def setup():
                pe.wait_ge(s_w1, 16)
                pe.wait_ge(s_ln, 2)
                mm(psA[0:QKV, 0:PD + 1], par("wqkvT"), lnmat[:], start=True, stop=True).then_inc(s_su_pe, 1)
                pe.wait_ge(s_su, 8)
                for n in range(2):
                    last = mm(psB[0:SPN + 1, n * QKV:(n + 1) * QKV], wl[:, n, :], ident[0:QKV, 0:QKV],
                              start=True, stop=True)
                last.then_inc(s_su_pe, 1)
                wp = par2("wproj")
                for k in range(2):
                    for h in range(2):
                        last = mm(psA[0:CH, k * C + h * CH:k * C + (h + 1) * CH], wp[:, h, k * CH:(k + 1) * CH],
                                  dinv2[:, h, :], start=True, stop=True)
                last.then_inc(s_su_pe, 1)

            def setup2():
                pe.wait_ge(s_w2, 16)
                wv, wd = par2("wv"), par2("wdw1T")
                for jh in range(2):
                    for h in range(2):
                        last = mm(R[0][0:CH, jh * C:(jh + 1) * C], wv[:, h, jh * CH:(jh + 1) * CH],
                                  wd[:, h, :], start=(h == 0), stop=(h == 1))
                last.then_inc(s_su_pe, 1)
                mm(R[1][:, 0:1], par("ci2cT_rep"), par("b_ci2b"), start=True, stop=True).then_inc(s_su_pe, 1)

            def group_means(i, b, ps):
                pe.wait_ge(gst[i].sem, gst[i].at(b, 7))
                mm(ps[0:CH, 0:16], par("gavg"), mv[i][:].rearrange("p s k -> p (s k)"),
                   start=True, stop=True).then_inc(gav[i].sem, 1)

            def center(b):
                pe.wait_ge(xa_s.sem, xa_s.at(b, 2))
                mm(psA[0:SPN, 0:HB], par("center"), xa[:], start=True, stop=True).then_inc(xc_s.sem, 1)

            def pixel_var(b):
                pe.wait_ge(sq_s.sem, sq_s.at(b, 1))
                for t in range(4):
                    last = mm(psB[:, 2 * t:2 * t + 2], sq[:, t * P:(t + 1) * P], par("mean_rows"), start=True, stop=True)
                last.then_inc(var_s.sem, 1)

            def spread(b, k, done):
                pe.wait_ge(dg_s.sem, dg_s.at(b, k))
                for n in range(2):
                    last = mm(psB[n * SP2:(n + 1) * SP2, 0:HB], ones[:, 0:SP2], dg[:, n:NKT:2, :],
                              start=True, stop=True)
                last.then_inc(done.sem, 1)

            def qk_product(b, k):
                pe.wait_ge(xn_s.sem, xn_s.at(b, 1))
                w, ps = ((q3w, psB), (k3w, psA))[k]
                for n in range(2):
                    last = mm(ps[0:CH, n * HB:(n + 1) * HB], w[:, n, :], xn[:], start=True, stop=True)
                last.then_inc(qkp_s.sem, 1)

            def v_product(b):
                w = 2 * (PD + 1)
                for t in range(4):
                    last = mm(psO[:, t * w:(t + 1) * w], xn[:, t * P:(t + 1) * P],
                              v1w[:].rearrange("p n c -> p (n c)"), start=True, stop=True)
                last.then_inc(qkp_s.sem, 1)

            def score_rows(b, t):
                if t == 0:
                    pe.wait_ge(qk_s.sem, qk_s.at(b, 2))
                    pe.wait_ge(ql_s.sem, ql_s.at(b, 2))
                if t >= 2:
                    pe.wait_ge(nm_s.sem, nm_s.at(b, t - 1))
                ps = (psA, psB)[t % 2]
                for n in range(2):
                    last = mm(ps[:, n * HB:(n + 1) * HB], qs[0:CH, t * P:(t + 1) * P],
                              ks[0:CH, n * HB:(n + 1) * HB], start=True, stop=True)
                last.then_inc(mx_s.sem, 1)

            def max_rows(b):
                pe.wait_ge(nm_s.sem, nm_s.at(b, NKT + 2))
                for t in range(NKT):
                    last = nc.tensor.transpose(psB[0:2, t * P:(t + 1) * P], nmr[:, t, :].bitcast(F32), ident)
                last.then_inc(tm_s.sem, 1)

            def scores_t(b, t):
                if t == 0:
                    pe.wait_ge(qm_s.sem, qm_s.at(b, 1))
                if t >= 2:
                    pe.wait_ge(ex_s.sem, ex_s.at(b, t - 1))
                ps = (psA, psB)[t % 2]
                for n in range(2):
                    last = mm(ps[:, n * HB:(n + 1) * HB], ks[0:CH + 2, t * P:(t + 1) * P],
                              qs[0:CH + 2, n * HB:(n + 1) * HB], start=True, stop=True)
                last.then_inc(st_s.sem, 1)

            def pv(b, t):
                if t == 0:
                    pe.wait_ge(vt_s.sem, vt_s.at(b, 1))
                pe.wait_ge(ex_s.sem, ex_s.at(b, t + 1))
                for n in range(2):
                    last = mm(psO[SP2 * n:SP2 * (n + 1), :], vt[:, t, :], pT[t % 2][:, n * HB:(n + 1) * HB],
                              start=(t == 0), stop=(t == NKT - 1))
                last.then_inc(pvd_s.sem, 1)

            def denominators(b):
                pe.wait_ge(oc_s.sem, oc_s.at(b, 1))
                for t in range(4):
                    last = mm(psA[:, 2 * t:2 * t + 2], osb[0:SPN + 1, t * P:(t + 1) * P], par("pick_den"),
                              start=True, stop=True)
                last.then_inc(dn_s.sem, 1)

            def proj1(b, h):
                pe.wait_ge(xo_s.sem, xo_s.at(b, 2))
                ps = (psA, psB)[h]
                for n in range(2):
                    for k in range(2):
                        last = mm(ps[0:CH, n * HB:(n + 1) * HB], wp2[:, k, h * CH:(h + 1) * CH],
                                  xm[:, k, n * HB:(n + 1) * HB], start=(k == 0), stop=(k == 1))
                last.then_inc(y_s.sem, 1)

            def conv1(c, k):
                pe.wait_ge(X_s.sem, X_s.at(c, 2))
                h, n = divmod(k, 2)
                if k == 3:
                    pe.wait_ge(ce_s.sem, ce_s.at(c, 1))
                ps = R[(1, 2, 0, 1)[k]]
                mm(ps[0:CH, :], wc1[0:CH + 1, 0, h * CH:(h + 1) * CH], X[0:CH + 1, 0, n * HB:(n + 1) * HB],
                   start=True, stop=False)
                mm(ps[0:CH, :], wc1[0:CH, 1, h * CH:(h + 1) * CH], X[0:CH, 1, n * HB:(n + 1) * HB],
                   start=False, stop=True).then_inc(c1_s.sem, 1)

            def transpose_x(c, k):
                if k < 3:
                    pe.wait_ge(ce_s.sem, ce_s.at(c, k + 2))
                else:
                    pe.wait_ge(xte_s.sem, xte_s.at(c, 1))
                ps = R[(2, 0, 1, 2)[k]]
                for j in range(4):
                    t, h = 2 * k + j // 2, j % 2
                    last = nc.tensor.transpose(ps[:, j * CH:(j + 1) * CH], X[0:CH, h, t * P:(t + 1) * P],
                                               ident[0:CH, 0:CH])
                last.then_inc(xtp_s.sem, 1)

            def gram_x(c):
                pe.wait_ge(xte_s.sem, xte_s.at(c, 4))
                for h in range(2):
                    for t in range(NKT):
                        last = mm(R[0][0:CH, h * C:(h + 1) * C], xT[:, t, h * CH:(h + 1) * CH], xT[:, t, :],
                                  start=(t == 0), stop=(t == NKT - 1))
                last.then_inc(gp_s.sem, 1)

            def gram_w(c):
                pe.wait_ge(ge_s.sem, ge_s.at(c, 1))
                wqk = par2("wqkT")
                for jh in range(2):
                    for k in range(2):
                        last = mm(R[1 + jh][0:CH, 0:2 * C], gram[:, k, jh * CH:(jh + 1) * CH], wqk[:, k, :],
                                  start=(k == 0), stop=(k == 1))
                    last.then_inc(tup_s.sem, 1)

            def head_scores(c):
                pe.wait_ge(tue_s.sem, tue_s.at(c, 2))
                wqk = par2("wqkT")
                for h in range(2):
                    for jh in range(2):
                        last = mm(R[1][0:CH, h * CH:(h + 1) * CH], tu[:, jh, h * CH:(h + 1) * CH],
                                  wqk[:, jh, C + h * CH:C + (h + 1) * CH], start=(jh == 0), stop=(jh == 1))
                last.then_inc(sc_s.sem, 1)

            def norms(c):
                pe.wait_ge(prd_s.sem, prd_s.at(c, 1))
                for k in range(4):
                    for jh in range(2):
                        last = mm(R[0][0:CH, k:k + 1], prd[:, jh, k * CH:(k + 1) * CH], ones[0:CH, 0:1],
                                  start=(jh == 0), stop=(jh == 1))
                last.then_inc(kn_s.sem, 1)

            def k_norm_rows(c):
                pe.wait_ge(dk_s.sem, dk_s.at(c, 2))
                for h in range(2):
                    last = mm(R[2][0:CH, h * CH:(h + 1) * CH], ones[0:CH, :], dk[:, h, :], start=True, stop=True)
                last.then_inc(kr_s.sem, 1)

            def transpose_attn(c):
                pe.wait_ge(sm_s.sem, sm_s.at(c, 8))
                for h in range(2):
                    last = nc.tensor.transpose(R[2][0:CH, h * CH:(h + 1) * CH], attn[:, h, :], ident[0:CH, 0:CH])
                last.then_inc(at_s.sem, 1)

            def attn_weights(c):
                pe.wait_ge(ate_s.sem, ate_s.at(c, 1))
                wv = par2("wv")
                for h in range(2):
                    last = mm(R[1][0:CH, h * C:(h + 1) * C], attT[:, h, :], wv[:, h, :], start=True, stop=True)
                last.then_inc(mp_s.sem, 1)
                for jh in range(2):
                    for h in range(2):
                        last = mm(R[0][0:CH, jh * C + h * CH:jh * C + (h + 1) * CH],
                                  wv[:, h, jh * CH:(jh + 1) * CH], attT[:, h, :], start=True, stop=True)
                last.then_inc(mp_s.sem, 1)

            def t_weights(c):
                pe.wait_ge(mae_s.sem, mae_s.at(c, 1))
                wcp = par2("wcpT")
                for jh in range(2):
                    for h in range(2):
                        last = mm(R[2][0:CH, jh * C6:(jh + 1) * C6], wma[:, h, jh * CH:(jh + 1) * CH],
                                  wcp[:, h, :], start=(h == 0), stop=(h == 1))
                last.then_inc(mp_s.sem, 1)

            def t_product(c):
                pe.wait_ge(mte_s.sem, mte_s.at(c, 1))
                pe.wait_ge(mce_s.sem, mce_s.at(c, 1))
                for jh in range(2):
                    kk = CH + 1 if jh == 0 else CH
                    for q in range(4):
                        last = mm(R[0][q * C6:(q + 1) * C6, 0:QB], wmc[0:kk, jh, :],
                                  X[0:kk, jh, q * QB:(q + 1) * QB], start=(jh == 0), stop=(jh == 1))
                last.then_inc(tt_s.sem, 1)

            def ci1_product(c):
                pe.wait_ge(t4_s.sem, t4_s.at(c, 1))
                mm(R[0][:, 0:1], par("w_ci1"), tsum[:], start=True, stop=True).then_inc(cip_s.sem, 1)

            def ci2a(c):
                pe.wait_ge(ci_s.sem, ci_s.at(c, 1))
                pe.wait_ge(tpd_s.sem, tpd_s.at(c, 32))
                w = par("w_ci2a").rearrange("p (y o) -> p y o", y=3)
                img = tp[:].rearrange("p (y x) -> p y x", x=PW)
                for dy in range(3):
                    for q in range(4):
                        last = mm(R[0][q * C6:(q + 1) * C6, 0:QB], w[:, dy, :],
                                  img[:, q * 8 + dy:q * 8 + dy + 8, 0:WW], start=(dy == 0), stop=(dy == 2))
                last.then_inc(ca_s.sem, 1)

            def ci2b(c, dy):
                if dy == 0:
                    pe.wait_ge(ud_s.sem, ud_s.at(c, 48))
                img = up[:].rearrange("p (y x) -> p y x", x=UW)
                for second in range(2):
                    g = 2 * dy + second
                    kk = 3 * C6 if second else P
                    for q in range(4):
                        y0 = q * 8 + 3 * dy
                        last = mm(R[0][q * C6:(q + 1) * C6, 0:QB], wb[0:kk, g, :],
                                  img[0:kk, y0:y0 + 8, 12 * second:12 * second + WW],
                                  start=(g == 0), stop=(g == 13))
                if dy == 6:
                    last.then_inc(cb_s.sem, 1)

            def map_mean(c):
                pe.wait_ge(pr_s.sem, pr_s.at(c, 4))
                pe.wait_ge(ci_s.sem, ci_s.at(c, 2))
                for h in range(2):
                    last = mm(R[0][0:CH, h:h + 1], wco[:, h * CH:(h + 1) * CH], psm[:], start=True, stop=True)
                last.then_inc(cm_s.sem, 1)

            def sp_in(c, n):
                pe.wait_ge(cv_s.sem, cv_s.at(c, 16))
                pe.wait_ge(mce_s.sem, mce_s.at(c, 1))
                w = par2("w_spi")
                for k in range(2):
                    last = mm(R[1 + n][0:SPN, :], w[:, k, :], cx[:, k, n * HB:(n + 1) * HB],
                              start=(k == 0), stop=(k == 1))
                last.then_inc(spi_s.sem, 1)

            def sp_out(c, k):
                n, h = divmod(k, 2)
                pe.wait_ge(gu_s.sem, gu_s.at(c, 2))
                if k >= 2:
                    pe.wait_ge(th_s.sem, th_s.at(c, k - 1))
                mm(R[1 + h][0:CH, :], par2("w_spo")[:, n, h * CH:(h + 1) * CH], gmul[:],
                   start=True, stop=True).then_inc(spo_s.sem, 1)

            def attended(c, k):
                n, h = divmod(k, 2)
                if k == 0:
                    pe.wait_ge(mte_s.sem, mte_s.at(c, 1))
                    pe.wait_ge(gt_s.sem, gt_s.at(c, 2))
                elif k < 3:
                    pe.wait_ge(th_s.sem, th_s.at(c, k + 2))
                else:
                    pe.wait_ge(uu_s.sem, uu_s.at(c, 1))
                ps = R[k % 3]
                mm(ps[0:CH, :], wmt[0:CH + 1, 0, h * CH:(h + 1) * CH], X[0:CH + 1, 0, n * HB:(n + 1) * HB],
                   start=True, stop=False)
                mm(ps[0:CH, :], wmt[0:CH, 1, h * CH:(h + 1) * CH], X[0:CH, 1, n * HB:(n + 1) * HB],
                   start=False, stop=False)
                mm(ps[0:CH, :], wco[:, h * CH:(h + 1) * CH], pr4[:, n * HB:(n + 1) * HB],
                   start=False, stop=True).then_inc(ap_s.sem, 1)

            def proj2(c, k):
                n, h = divmod(k, 2)
                pe.wait_ge(zz_s.sem, zz_s.at(c, 2 * n + 2))
                if k == 1:
                    pe.wait_ge(uu_s.sem, uu_s.at(c, 3))
                if k == 3:
                    pe.wait_ge(oo_s.sem, oo_s.at(c, 1))
                for j in range(2):
                    last = mm(R[(k + 1) % 3][0:CH, :], wph[:, j, h * CH:(h + 1) * CH],
                              zz[:, j, n * HB:(n + 1) * HB], start=(j == 0), stop=(j == 1))
                last.then_inc(op_s.sem, 1)

            def block1(b):
                group_means(0, b, psB)
                setup2()
                center(b)
                pixel_var(b)
                spread(b, 1, rbp_s)
                qk_product(b, 0)
                qk_product(b, 1)
                v_product(b)
                for t in range(8):
                    score_rows(b, t)
                max_rows(b)
                scores_t(b, 0)
                scores_t(b, 1)
                pv(b, 0)
                scores_t(b, 2)
                pv(b, 1)
                scores_t(b, 3)
                pv(b, 2)
                scores_t(b, 4)
                pv(b, 3)
                scores_t(b, 5)
                pv(b, 4)
                scores_t(b, 6)
                pv(b, 5)
                scores_t(b, 7)
                pv(b, 6)
                pv(b, 7)
                denominators(b)
                spread(b, 2, db_s)
                proj1(b, 0)
                proj1(b, 1)
                group_means(1, b, psO)

            def block2(c):
                for k in range(4):
                    conv1(c, k)
                for k in range(4):
                    transpose_x(c, k)
                gram_x(c)
                gram_w(c)
                head_scores(c)
                norms(c)
                k_norm_rows(c)
                transpose_attn(c)
                attn_weights(c)
                t_weights(c)
                t_product(c)
                sp_in(c, 0)
                sp_in(c, 1)
                ci1_product(c)
                ci2a(c)
                for k in range(3):
                    ci2b(c, k)
                sp_out(c, 0)
                sp_out(c, 1)
                for k in range(3, 7):
                    ci2b(c, k)
                sp_out(c, 2)
                sp_out(c, 3)
                map_mean(c)
                for k in range(4):
                    attended(c, k)
                for k in range(4):
                    proj2(c, k)

            def both(c, b):
                for k in range(4):
                    conv1(c, k)
                for k in range(3):
                    transpose_x(c, k)
                group_means(0, b, psB)
                transpose_x(c, 3)
                gram_x(c)
                center(b)
                gram_w(c)
                pixel_var(b)
                head_scores(c)
                norms(c)
                spread(b, 1, rbp_s)
                k_norm_rows(c)
                qk_product(b, 0)
                qk_product(b, 1)
                v_product(b)
                transpose_attn(c)
                attn_weights(c)
                score_rows(b, 0)
                t_weights(c)
                score_rows(b, 1)
                score_rows(b, 2)
                t_product(c)
                score_rows(b, 3)
                ci1_product(c)
                sp_in(c, 0)
                score_rows(b, 4)
                score_rows(b, 5)
                sp_in(c, 1)
                score_rows(b, 6)
                score_rows(b, 7)
                ci2a(c)
                max_rows(b)
                scores_t(b, 0)
                scores_t(b, 1)
                pv(b, 0)
                scores_t(b, 2)
                pv(b, 1)
                for k in range(4):
                    ci2b(c, k)
                scores_t(b, 3)
                pv(b, 2)
                scores_t(b, 4)
                for k in range(4, 7):
                    ci2b(c, k)
                pv(b, 3)
                scores_t(b, 5)
                pv(b, 4)
                scores_t(b, 6)
                pv(b, 5)
                map_mean(c)
                sp_out(c, 0)
                attended(c, 0)
                sp_out(c, 1)
                sp_out(c, 2)
                scores_t(b, 7)
                pv(b, 6)
                sp_out(c, 3)
                pv(b, 7)
                attended(c, 1)
                denominators(b)
                attended(c, 2)
                spread(b, 2, db_s)
                attended(c, 3)
                proj1(b, 0)
                proj1(b, 1)
                for k in range(3):
                    proj2(c, k)
                group_means(1, b, psO)
                proj2(c, 3)

            setup()
            pe.wait_ge(s_su, 9)
            block1(0)
            pe.wait_ge(s_su, 15)
            pe.wait_ge(s_fill, FILLS)
            with pe.Fori(1, B) as i:
                pe.wait_ge(x2_s.sem, x2_s.at(i, 0))
                pe.wait_ge(oo_s.sem, oo_s.at(i - 1, 0))
                both(i - 1, i)
            pe.wait_ge(x2_s.sem, x2_s.at(B, 0))
            pe.wait_ge(oo_s.sem, oo_s.at(B - 1, 0))
            block2(B - 1)

        @block.vector
        def _(dve):
            v = nc.vector

            def setup():
                v.memset(ks[CH:CH + 2, :].bitcast(F32), 1.0).then_inc(s_rows, 1)
                v.memset(X[CH:CH + 1, :, :], 1.0).then_inc(s_rows, 1)
                v.memset(wl[:], 0.0).then_inc(s_rows, 1)
                v.memset(xa[:], 0.0).then_inc(s_rows, 1)
                v.memset(gmul[:], 0.0).then_inc(s_rows, 1)
                v.memset(vt[:], 0.0).then_inc(s_rows, 1)
                dve.wait_ge(s_rows, 6)
                dve.wait_ge(s_fill, 1)
                dve.wait_ge(s_w1, 16)
                v.tensor_scalar(lnmat[:, 0:PD], ident[0:PD, 0:PD], par("ln_w"), None, ALU.mult).then_inc(s_ln, 1)
                v.tensor_scalar(var1[:], bn1[:, 3:4], EPS, None, ALU.add).then_inc(s_su, 1)
                v.tensor_scalar(var2[:], bn2[:, 3, :], EPS, None, ALU.add).then_inc(s_su, 1)
                dve.wait_ge(s_isd, 2)
                v.tensor_tensor(inv1[:], bn1[:, 0:1], isd1[:], ALU.mult).then_inc(s_su, 1)
                v.tensor_tensor(inv2[:], bn2[:, 0, :], isd2[:], ALU.mult).then_inc(s_su, 1)
                dve.wait_ge(s_su, 4)
                dve.wait_ge(s_su_pe, 1)
                for n in range(2):
                    v.tensor_scalar(wl[:, n, n * SP2:n * SP2 + PD], psA[0:QKV, 0:PD], inv1[:, 0:1], None, ALU.mult)
                    last = v.tensor_scalar(wl[:, n, SPN:SPN + 1], psA[0:QKV, PD:PD + 1], inv1[:, 0:1], None, ALU.mult)
                last.then_inc(s_su, 1)
                for h in range(2):
                    v.tensor_scalar(dinv2[:, h, :], ident[0:CH, 0:CH], inv2[:, h:h + 1], None, ALU.mult)
                v.tensor_tensor(bias2[:], bn2[:, 2, :], inv2[:], ALU.mult)
                v.scalar_tensor_tensor(sh1[:], bn1[:, 2:3], inv1[:, 0:1], bn1[:, 1:2], ALU.mult, ALU.subtract).then_inc(s_su, 1)
                dve.wait_ge(s_su, 6)
                v.tensor_tensor(bias2[:], bn2[:, 1, :], bias2[:], ALU.subtract).then_inc(s_su, 1)
                v.tensor_tensor(wl[:, :, SPN:SPN + 1], wl[:, :, SPN:SPN + 1],
                                sh1[:].unsqueeze(1).broadcast_to([QKV, 2, 1]), ALU.subtract).then_inc(s_su, 1)
                v.memset(q3w[:], 0.0)
                v.memset(k3w[:], 0.0)
                v.tensor_copy(v1w[:, :, PD:PD + 1],
                              par("pick_one").unsqueeze(1).broadcast_to([SPN + 1, 2, 1])).then_inc(s_ln, 1)
                dve.wait_ge(s_ln, 3)
                dve.wait_ge(s_su_pe, 2)
                wt2 = psB[0:SPN + 1, 0:2 * QKV].rearrange("p (n c) -> p n c", n=2)
                for j in range(3):
                    v.tensor_scalar(q3w[:, :, 32 * j:32 * j + QK], wt2[:, :, 0:QK], QK ** -0.5, None, ALU.mult)
                    v.tensor_copy(k3w[:, :, 32 * j:32 * j + QK], wt2[:, :, QK:2 * QK])
                v.tensor_copy(v1w[:, :, 0:PD], wt2[:, :, 2 * QK:QKV])
                dve.wait_ge(s_su_pe, 3)
                v.tensor_copy(wp2[:], psA[0:CH, 0:2 * C].rearrange("p (k c) -> p k c", k=2)).then_inc(s_su, 1)

            def setup2():
                dve.wait_ge(s_w2, 16)
                dve.wait_ge(s_su_pe, 5)
                v.tensor_copy(wc1[0:CH, :, :], R[0][0:CH, 0:2 * C].rearrange("p (h c) -> p h c", h=2)).then_inc(s_su, 1)
                v.tensor_tensor(bci2[:], R[1][:, 0:1], par("b_ci2c"), ALU.add).then_inc(s_su, 1)
                v.tensor_tensor(wb[:], par("ci2cT").unsqueeze(1).broadcast_to([P, 14, C6]),
                                par("w_ci2b").unsqueeze(2).broadcast_to([P, 14, C6]), ALU.mult).then_inc(s_su, 1)
                v.tensor_scalar(hbias[:], par("half_biases"), 0.5, None, ALU.mult).then_inc(s_su, 1)
                v.tensor_scalar(wph[:], par2("w_pr"), 0.5, None, ALU.mult).then_inc(s_su, 1)
                v.tensor_copy(wc1[CH:CH + 1, 0, :], row("row_dw1_b"))
                v.tensor_copy(wmt[CH:CH + 1, 0, :], row("row_cp_out_b"))
                v.tensor_copy(wmc[CH:CH + 1, 0, :], row("row_cp_in_b")).then_inc(s_su, 1)

            def channel_stats(i, b, h):
                if i == 0:
                    dve.wait_ge(x_in[h].sem, x_in[h].at(b, 16))
                else:
                    dve.wait_ge(x2_s.sem, x2_s.at(b, h + 1))
                for n in range(2):
                    k = 2 * h + n
                    v.bn_stats(st6[i][:, 2 * k:2 * k + 2, :],
                               (xt, x2)[i][:, h, n * HB:(n + 1) * HB]).then_inc(gst[i].sem, 1)

            def moments(i, b):
                s = gst[i]
                dve.wait_ge(s.sem, s.at(b, 4))
                v.tensor_copy(mv[i][:, 0, :], st6[i][:, :, 1]).then_inc(s.sem, 1)
                v.tensor_tensor(msq[i][:], st6[i][:, :, 1], st6[i][:, :, 1], ALU.mult).then_inc(s.sem, 1)
                dve.wait_ge(s.sem, s.at(b, 6))
                v.scalar_tensor_tensor(mv[i][:, 1, :], st6[i][:, :, 2], 2.0 / HB, msq[i][:],
                                       ALU.mult, ALU.add).then_inc(s.sem, 1)

            def group_stats(i, b, ps):
                s = gmm[i]
                dve.wait_ge(gav[i].sem, gav[i].at(b, 1))
                v.tensor_reduce(gm[i][:], ps[0:CH, 0:16].rearrange("p (s h k) -> p s h k", s=2, h=2),
                                AX_X, ALU.add).then_inc(s.sem, 1)
                dve.wait_ge(s.sem, s.at(b, 1))
                v.tensor_tensor(gsq[i][:], gm[i][:, 0, :], gm[i][:, 0, :], ALU.mult).then_inc(s.sem, 1)
                dve.wait_ge(s.sem, s.at(b, 2))
                v.scalar_tensor_tensor(gvar[i][:], gm[i][:, 1, :], EPS, gsq[i][:], ALU.add, ALU.subtract).then_inc(s.sem, 1)

            def group_shift(i, b):
                s = gmm[i]
                dve.wait_ge(grr[i].sem, grr[i].at(b, 1))
                v.scalar_tensor_tensor(gb[i][:], gm[i][:, 0, :], -1.0, gr[i][:], ALU.mult, ALU.mult).then_inc(s.sem, 1)

            def diagonals(b, k, src):
                v.tensor_tensor(dg[:], ident.unsqueeze(1).broadcast_to([P, NKT, P]),
                                src[:].unsqueeze(2).broadcast_to([P, NKT, P]), ALU.mult).then_inc(dg_s.sem, 1)

            def pixel_var(b):
                dve.wait_ge(var_s.sem, var_s.at(b, 1))
                v.tensor_scalar(pv8[:], psB[:, 0:NKT], EPS, None, ALU.add).then_inc(pv_s.sem, 1)

            def rstd_diagonals(b):
                dve.wait_ge(rT_s.sem, rT_s.at(b, 1))
                diagonals(b, 1, rT)

            def layer_norm(b):
                dve.wait_ge(rb_s.sem, rb_s.at(b, 1))
                v.tensor_tensor(xn[0:SPN, :], psA[0:SPN, 0:HB], rb[:], ALU.mult).then_inc(xn_s.sem, 1)

            def q_low(b):
                dve.wait_ge(qk_s.sem, qk_s.at(b, 1))
                v.tensor_tensor(qs[32:64, :], psB[32:64, :], qs[32:64, :].bitcast(F32), ALU.subtract).then_inc(ql_s.sem, 1)

            def k_low(b):
                dve.wait_ge(qk_s.sem, qk_s.at(b, 2))
                v.tensor_tensor(ks[64:96, :], psA[64:96, :], ks[64:96, :].bitcast(F32), ALU.subtract).then_inc(ql_s.sem, 1)

            def v_copy(b):
                dve.wait_ge(qkp_s.sem, qkp_s.at(b, 3))
                v.tensor_copy(vt[:, :, 0:PD + 1].rearrange("p (n t) c -> p t n c", n=2),
                              psO[:, 0:NKT * (PD + 1)].rearrange("p (t n c) -> p t n c", t=4, n=2)).then_inc(vt_s.sem, 1)

            def row_max(b, t):
                dve.wait_ge(mx_s.sem, mx_s.at(b, t + 1))
                v.tensor_reduce(nm[:, t:t + 1], (psA, psB)[t % 2][:], AX_X, ALU.max, negate=True).then_inc(nm_s.sem, 1)

            def split_max(b):
                dve.wait_ge(nm_s.sem, nm_s.at(b, NKT))
                v.tensor_copy(nmr[:, :, 0], nm[:]).then_inc(nm_s.sem, 1)
                dve.wait_ge(nm_s.sem, nm_s.at(b, NKT + 1))
                v.tensor_tensor(nmr[:, :, 1], nm[:], nmr[:, :, 0].bitcast(F32), ALU.subtract).then_inc(nm_s.sem, 1)



            def denominator_diagonals(b):
                dve.wait_ge(dn_s.sem, dn_s.at(b, 1))
                v.reciprocal(rT[:], psA[:, 0:NKT]).then_inc(dr_s.sem, 1)
                dve.wait_ge(dr_s.sem, dr_s.at(b, 1))
                diagonals(b, 2, rT)

            def attn_relu(b):
                dve.wait_ge(db_s.sem, db_s.at(b, 1))
                dve.wait_ge(xm_s.sem, xm_s.at(b, 2))
                for n in range(2):
                    p = slice(n * SP2, n * SP2 + PD)
                    v.scalar_tensor_tensor(xm[0:PD, 0, n * HB:(n + 1) * HB], osb[p, :], 0.0, psB[p, 0:HB],
                                           ALU.max, ALU.mult).then_inc(xo_s.sem, 1)

            def block1_out(b, h):
                dve.wait_ge(y_s.sem, y_s.at(b, h + 1))
                v.scalar_tensor_tensor(x2[:, h, :], (psA, psB)[h][0:CH, :], bias2[:, h:h + 1], xt[:, h, :],
                                       ALU.add, ALU.add).then_inc(x2_s.sem, 1)

            def normed(c):
                dve.wait_ge(gmm[1].sem, gmm[1].at(c, 4))
                v.tensor_scalar(X[0:CH, 0, :], x2[:, 0, :], gr[1][:, 0:1], gb[1][:, 0:1],
                                ALU.mult, ALU.add).then_inc(X_s.sem, 1)

            def gram_copy(c):
                dve.wait_ge(gp_s.sem, gp_s.at(c, 1))
                v.tensor_copy(gram[:], R[0][0:CH, 0:2 * C].rearrange("p (h c) -> p h c", h=2)).then_inc(ge_s.sem, 1)

            def times_w(c):
                dve.wait_ge(tue_s.sem, tue_s.at(c, 2))
                v.tensor_tensor(prd[:], tu[:], par2("wqkT"), ALU.mult).then_inc(prd_s.sem, 1)

            def clamp_norms(c):
                dve.wait_ge(kn_s.sem, kn_s.at(c, 1))
                v.tensor_scalar(nrm[:], R[0][0:CH, 0:4], 1e-24, None, ALU.max).then_inc(nrm_s.sem, 1)

            def inverse_norms(c):
                s = sm_s
                dve.wait_ge(rn_s.sem, rn_s.at(c, 1))
                for h in range(2):
                    v.tensor_scalar(dk[:, h, :], ident[0:CH, 0:CH], rn[:, 2 + h:3 + h], None, ALU.mult).then_inc(dk_s.sem, 1)
                v.tensor_tensor(rq[:], rn[:, 0:2], par("temp"), ALU.mult).then_inc(s.sem, 1)

            def scaled_scores(c):
                s = sm_s
                dve.wait_ge(rk_s.sem, rk_s.at(c, 1))
                dve.wait_ge(s.sem, s.at(c, 1))
                dve.wait_ge(sc_s.sem, sc_s.at(c, 1))
                for h in range(2):
                    v.scalar_tensor_tensor(s1[:, h, :], R[1][0:CH, h * CH:(h + 1) * CH], rq[:, h:h + 1],
                                           rk[:, h, :], ALU.mult, ALU.mult).then_inc(s.sem, 1)
                dve.wait_ge(s.sem, s.at(c, 3))
                v.tensor_tensor(s2[:], s1[:], par("mask").unsqueeze(1).broadcast_to([CH, 2, CH]), ALU.add).then_inc(s.sem, 1)
                dve.wait_ge(s.sem, s.at(c, 4))
                v.tensor_reduce(smx[:], s2[:], AX_X, ALU.max, negate=True).then_inc(s.sem, 1)

            def softmax_divide(c):
                s = sm_s
                dve.wait_ge(se_s.sem, se_s.at(c, 2))
                v.reciprocal(srec[:], ssum[:]).then_inc(s.sem, 1)
                dve.wait_ge(s.sem, s.at(c, 6))
                for h in range(2):
                    v.tensor_scalar(attn[:, h, :], se[:, h, :], srec[:, h:h + 1], None, ALU.mult).then_inc(s.sem, 1)

            def copy_wma(c):
                dve.wait_ge(mp_s.sem, mp_s.at(c, 1))
                v.tensor_copy(wma[:], R[1][0:CH, 0:2 * C].rearrange("p (h c) -> p h c", h=2)).then_inc(mae_s.sem, 1)

            def copy_wmc(c):
                dve.wait_ge(mp_s.sem, mp_s.at(c, 3))
                v.tensor_copy(wmc[0:CH, :, :], R[2][0:CH, 0:2 * C6].rearrange("p (h c) -> p h c", h=2)).then_inc(mce_s.sem, 1)

            def pad_t(c):
                dve.wait_ge(t4_s.sem, t4_s.at(c, 1))
                img = tp[:].rearrange("p (y x) -> p y x", x=PW)
                for q in range(4):
                    v.tensor_copy(img[0:C6, 1 + 8 * q:9 + 8 * q, 1:1 + WW],
                                  t4[q * C6:(q + 1) * C6, :].rearrange("p (y x) -> p y x", x=WW)).then_inc(tpc_s.sem, 1)

            def ci1_scale(c):
                dve.wait_ge(cip_s.sem, cip_s.at(c, 1))
                v.tensor_scalar(ci1[:], R[0][:, 0:1], 1.0 / N, par("b_ci1"), ALU.mult, ALU.add).then_inc(ci_s.sem, 1)
                dve.wait_ge(ci_s.sem, ci_s.at(c, 1))
                v.tensor_scalar(wco[:], par("wcoT"), ci1[:, 0:1], None, ALU.mult).then_inc(ci_s.sem, 1)

            def channel_product(c):
                dve.wait_ge(cb_s.sem, cb_s.at(c, 1))
                for q in range(4):
                    p = slice(q * C6, (q + 1) * C6)
                    v.scalar_tensor_tensor(pr4[p, q * QB:(q + 1) * QB], R[0][p, 0:QB], bci2[p, 0:1], t4[p, :],
                                           ALU.add, ALU.mult, accum_out=psm[p, :]).then_inc(pr_s.sem, 1)

            def gate_one(c):
                dve.wait_ge(gt_s.sem, gt_s.at(c, 2))
                v.tensor_scalar(gate2[:], gate[:], 1.0, None, ALU.add).then_inc(g2_s.sem, 1)

            def conv2(c, k):
                tap, h = k // 2 + 1, k % 2
                dy, dx = divmod(tap, 3)
                if tap > 1:
                    dve.wait_ge(cv_s.sem, cv_s.at(c, k - 1))
                else:
                    dve.wait_ge(cf_s.sem, cf_s.at(c, h + 1))
                acc = cx[:, h, :].rearrange("p (y x) -> p y x", x=WW)
                v.scalar_tensor_tensor(acc, cp[:, h, dy:dy + HH, dx:dx + WW], par2("wdw2")[:, h, tap:tap + 1], acc,
                                       ALU.mult, ALU.add).then_inc(cv_s.sem, 1)

            def sp_conv(c, k):
                tap, p = k // 2 + 1, k % 2
                dy, dx = divmod(tap, 3)
                if tap > 1:
                    dve.wait_ge(dv_s.sem, dv_s.at(c, k - 1))
                else:
                    dve.wait_ge(df_s.sem, df_s.at(c, 1))
                acc = dd[:, p * HB:(p + 1) * HB].rearrange("p (y x) -> p y x", x=WW)
                v.scalar_tensor_tensor(acc, spp[:, 16 * p + dy:16 * p + dy + 16, dx:dx + WW],
                                       par("w_spdw")[:, tap:tap + 1], acc, ALU.mult, ALU.add).then_inc(dv_s.sem, 1)

            def gelu_product(c, n):
                dve.wait_ge(gl_s.sem, gl_s.at(c, n + 1))
                px = slice(n * HB, (n + 1) * HB)
                v.tensor_tensor(gmul[n * SP2:n * SP2 + PD, :], gl[SP2:SPN, px], dd[SP2:SPN, px],
                                ALU.mult).then_inc(gu_s.sem, 1)

            def gate_attended(c, k):
                n, h = divmod(k, 2)
                dve.wait_ge(ap_s.sem, ap_s.at(c, k + 1))
                dve.wait_ge(th_s.sem, th_s.at(c, k + 1))
                v.scalar_tensor_tensor(uu[:, h, n * HB:(n + 1) * HB], th[:, h, n * HB:(n + 1) * HB], 1.0,
                                       R[k % 3][0:CH, :], ALU.add, ALU.mult).then_inc(uu_s.sem, 1)

            def merge(c, k):
                n, h = divmod(k, 2)
                if k == 0:
                    dve.wait_ge(g2_s.sem, g2_s.at(c, 1))
                dve.wait_ge(uu_s.sem, uu_s.at(c, k + 1))
                v.scalar_tensor_tensor(zz[:, h, n * HB:(n + 1) * HB], cx[:, h, n * HB:(n + 1) * HB], gate2[:, h:h + 1],
                                       uu[:, h, n * HB:(n + 1) * HB], ALU.mult, ALU.add).then_inc(zz_s.sem, 1)

            def result(c, k):
                n, h = divmod(k, 2)
                if k == 0:
                    dve.wait_ge(st_out.sem, st_out.at(c, 0))
                dve.wait_ge(op_s.sem, op_s.at(c, k + 1))
                v.tensor_tensor(oo[:, h, n * HB:(n + 1) * HB], R[(k + 1) % 3][0:CH, :],
                                xr[:, h, n * HB:(n + 1) * HB], ALU.add).then_inc(oo_s.sem, 1)

            def block1(b):
                channel_stats(0, b, 0)
                channel_stats(0, b, 1)
                moments(0, b)
                group_stats(0, b, psB)
                group_shift(0, b)
                setup2()
                pixel_var(b)
                rstd_diagonals(b)
                layer_norm(b)
                q_low(b)
                k_low(b)
                v_copy(b)
                for t in range(8):
                    row_max(b, t)
                split_max(b)
                denominator_diagonals(b)
                attn_relu(b)
                block1_out(b, 0)
                channel_stats(1, b, 0)
                block1_out(b, 1)
                channel_stats(1, b, 1)
                moments(1, b)
                group_stats(1, b, psO)
                group_shift(1, b)

            def block2(c):
                normed(c)
                for k in range(5):
                    conv2(c, k)
                gram_copy(c)
                for k in range(5, 8):
                    conv2(c, k)
                times_w(c)
                conv2(c, 8)
                clamp_norms(c)
                conv2(c, 9)
                inverse_norms(c)
                conv2(c, 10)
                scaled_scores(c)
                conv2(c, 11)
                softmax_divide(c)
                conv2(c, 12)
                conv2(c, 13)
                copy_wma(c)
                conv2(c, 14)
                copy_wmc(c)
                conv2(c, 15)
                pad_t(c)
                ci1_scale(c)
                for k in range(16):
                    sp_conv(c, k)
                gelu_product(c, 0)
                gelu_product(c, 1)
                channel_product(c)
                gate_one(c)
                for k in range(4):
                    gate_attended(c, k)
                for k in range(4):
                    merge(c, k)
                for k in range(4):
                    result(c, k)

            def both(c, b):
                normed(c)
                channel_stats(0, b, 0)
                channel_stats(0, b, 1)
                moments(0, b)
                conv2(c, 0)
                group_stats(0, b, psB)
                conv2(c, 1)
                group_shift(0, b)
                for k in range(2, 7):
                    conv2(c, k)
                gram_copy(c)
                for k in range(7, 10):
                    conv2(c, k)
                pixel_var(b)
                times_w(c)
                conv2(c, 10)
                rstd_diagonals(b)
                clamp_norms(c)
                conv2(c, 11)
                inverse_norms(c)
                conv2(c, 12)
                layer_norm(b)
                scaled_scores(c)
                conv2(c, 13)
                softmax_divide(c)
                conv2(c, 14)
                conv2(c, 15)
                q_low(b)
                k_low(b)
                v_copy(b)
                copy_wma(c)
                row_max(b, 0)
                copy_wmc(c)
                row_max(b, 1)
                row_max(b, 2)
                pad_t(c)
                row_max(b, 3)
                ci1_scale(c)
                for t in range(4, 8):
                    row_max(b, t)
                split_max(b)
                for k in range(16):
                    sp_conv(c, k)
                gelu_product(c, 0)
                gelu_product(c, 1)
                channel_product(c)
                gate_one(c)
                gate_attended(c, 0)
                denominator_diagonals(b)
                gate_attended(c, 1)
                gate_attended(c, 2)
                attn_relu(b)
                gate_attended(c, 3)
                for k in range(4):
                    merge(c, k)
                block1_out(b, 0)
                channel_stats(1, b, 0)
                block1_out(b, 1)
                channel_stats(1, b, 1)
                moments(1, b)
                for k in range(3):
                    result(c, k)
                group_stats(1, b, psO)
                result(c, 3)
                group_shift(1, b)

            dve.sem_inc(oo_s.sem, 1)
            dve.sem_inc(st_out.sem, 1)
            setup()
            block1(0)
            dve.wait_ge(s_fill, FILLS)
            with dve.Fori(1, B) as i:
                dve.wait_ge(x2_s.sem, x2_s.at(i, 0))
                dve.wait_ge(oo_s.sem, oo_s.at(i - 1, 0))
                both(i - 1, i)
            dve.wait_ge(x2_s.sem, x2_s.at(B, 0))
            block2(B - 1)

        @block.scalar
        def _(act):
            a = nc.scalar.activation
            ID = ACT.Identity

            def normed1(b):
                act.wait_ge(gmm[0].sem, gmm[0].at(b, 4))
                for n in range(2):
                    a(xa[n * SP2:n * SP2 + PD, :], xt[0:PD, 0, n * HB:(n + 1) * HB], ID, bias=gb[0][0:PD, 0:1],
                      scale=gr[0][0:PD, 0:1]).then_inc(xa_s.sem, 1)

            def squares(b):
                act.wait_ge(xc_s.sem, xc_s.at(b, 1))
                a(sq[:], psA[0:SPN, 0:HB], ACT.Square).then_inc(sq_s.sem, 1)

            def relu_normed(b, h):
                a(xm[:, h, :], xt[:, h, :], ACT.Relu, bias=gb[0][:, h:h + 1],
                  scale=gr[0][:, h:h + 1]).then_inc(xm_s.sem, 1)

            def rstd_rows(b):
                act.wait_ge(rbp_s.sem, rbp_s.at(b, 1))
                a(rb[:], psB[0:SPN, 0:HB], ACT.Copy).then_inc(rb_s.sem, 1)

            def q_high(b):
                act.wait_ge(qkp_s.sem, qkp_s.at(b, 1))
                a(qs[0:CH, :], psB[0:CH, :], ACT.Copy).then_inc(qk_s.sem, 1)

            def k_high(b):
                act.wait_ge(qkp_s.sem, qkp_s.at(b, 2))
                a(ks[0:CH, :], psA[0:CH, :], ACT.Copy).then_inc(qk_s.sem, 1)

            def max_copy(b):
                act.wait_ge(tm_s.sem, tm_s.at(b, 1))
                a(qs[CH:CH + 2, :], psB[0:2, :], ACT.Copy).then_inc(qm_s.sem, 1)

            def exps(b, t):
                act.wait_ge(st_s.sem, st_s.at(b, t + 1))
                if t >= 2:
                    act.wait_ge(pvd_s.sem, pvd_s.at(b, t - 1))
                a(pT[t % 2][:], (psA, psB)[t % 2][:], ACT.Exp).then_inc(ex_s.sem, 1)

            def attn_out(b):
                act.wait_ge(pvd_s.sem, pvd_s.at(b, NKT))
                a(osb[:], psO[:], ACT.Copy).then_inc(oc_s.sem, 1)

            def normed2(c):
                act.wait_ge(gmm[1].sem, gmm[1].at(c, 4))
                a(X[0:CH, 1, :], x2[:, 1, :], ID, bias=gb[1][:, 1:2], scale=gr[1][:, 1:2]).then_inc(X_s.sem, 1)

            def residual(c, h):
                a(xr[:, h, :], x2[:, h, :], ID, bias=par("b_pr")[:, h:h + 1]).then_inc(xr_s.sem, 1)

            def pad_conv1(c, k):
                h, n = divmod(k, 2)
                act.wait_ge(c1_s.sem, c1_s.at(c, k + 1))
                a(cp[:, h, 1 + 16 * n:17 + 16 * n, 1:1 + WW],
                  R[(1, 2, 0, 1)[k]][0:CH, :].rearrange("p (y x) -> p y x", x=WW), ACT.Copy).then_inc(ce_s.sem, 1)

            def conv2_first(c, h):
                act.wait_ge(ce_s.sem, ce_s.at(c, 2 * h + 2))
                a(cx[:, h, :].rearrange("p (y x) -> p y x", x=WW), cp[:, h, 0:HH, 0:WW], ID,
                  bias=par("bdw2")[:, h:h + 1], scale=par2("wdw2")[:, h, 0:1]).then_inc(cf_s.sem, 1)

            def copy_xT(c, k):
                act.wait_ge(xtp_s.sem, xtp_s.at(c, k + 1))
                a(xT[:, 2 * k:2 * k + 2, :], R[(2, 0, 1, 2)[k]][:, 0:4 * CH].rearrange("p (t c) -> p t c", t=2),
                  ACT.Copy).then_inc(xte_s.sem, 1)

            def copy_tu(c, jh):
                act.wait_ge(tup_s.sem, tup_s.at(c, jh + 1))
                a(tu[:, jh, :], R[1 + jh][0:CH, 0:2 * C], ACT.Copy).then_inc(tue_s.sem, 1)

            def copy_k_norms(c):
                act.wait_ge(kr_s.sem, kr_s.at(c, 1))
                a(rk[:], R[2][0:CH, 0:2 * CH].rearrange("p (h c) -> p h c", h=2), ACT.Copy).then_inc(rk_s.sem, 1)

            def head_exps(c):
                act.wait_ge(sm_s.sem, sm_s.at(c, 5))
                for h in range(2):
                    a(se[:, h, :], s2[:, h, :], ACT.Exp, bias=smx[:, h:h + 1],
                      accum_out=ssum[:, h:h + 1]).then_inc(se_s.sem, 1)

            def copy_attT(c):
                act.wait_ge(at_s.sem, at_s.at(c, 1))
                a(attT[:], R[2][0:CH, 0:2 * CH].rearrange("p (h c) -> p h c", h=2), ACT.Copy).then_inc(ate_s.sem, 1)

            def copy_wmt(c):
                act.wait_ge(mp_s.sem, mp_s.at(c, 2))
                a(wmt[0:CH, :, :], R[0][0:CH, 0:2 * C].rearrange("p (h c) -> p h c", h=2),
                  ACT.Copy).then_inc(mte_s.sem, 1)

            def copy_t(c):
                act.wait_ge(tt_s.sem, tt_s.at(c, 1))
                a(t4[:], R[0][:, 0:QB], ACT.Copy, accum_out=tsum[:]).then_inc(t4_s.sem, 1)

            def pad_ci2a(c):
                act.wait_ge(ca_s.sem, ca_s.at(c, 1))
                img = up[:].rearrange("p (y x) -> p y x", x=UW)
                for q in range(4):
                    p0 = q * C6
                    a(img[0:C6, 9 + 8 * q:17 + 8 * q, 9:9 + WW],
                      R[0][p0:p0 + C6, 0:QB].rearrange("p (y x) -> p y x", x=WW), ID,
                      bias=par("b_ci2a")[p0:p0 + C6, :]).then_inc(ue_s.sem, 1)

            def channel_gate(c):
                act.wait_ge(cm_s.sem, cm_s.at(c, 1))
                for h in range(2):
                    a(gate[:, h:h + 1], R[0][0:CH, h:h + 1], ACT.Tanh, bias=hbias[:, 2 + h:3 + h],
                      scale=0.5 / N).then_inc(gt_s.sem, 1)

            def pad_sp(c, n):
                act.wait_ge(spi_s.sem, spi_s.at(c, n + 1))
                a(spp[:, 1 + 16 * n:17 + 16 * n, 1:1 + WW],
                  R[1 + n][0:SPN, :].rearrange("p (y x) -> p y x", x=WW), ID,
                  bias=par("b_spi")).then_inc(spe_s.sem, 1)

            def sp_first(c):
                act.wait_ge(spe_s.sem, spe_s.at(c, 2))
                a(dd[:].rearrange("p (y x) -> p y x", x=WW), spp[:, 0:HH, 0:WW], ID, bias=par("b_spdw"),
                  scale=par("w_spdw")[:, 0:1]).then_inc(df_s.sem, 1)

            def gelu(c, n):
                act.wait_ge(dv_s.sem, dv_s.at(c, 15 + n))
                a(gl[SP2:SPN, n * HB:(n + 1) * HB], dd[0:PD, n * HB:(n + 1) * HB], ACT.Gelu).then_inc(gl_s.sem, 1)

            def spatial_tanh(c, k):
                n, h = divmod(k, 2)
                act.wait_ge(spo_s.sem, spo_s.at(c, k + 1))
                a(th[:, h, n * HB:(n + 1) * HB], R[1 + h][0:CH, :], ACT.Tanh, scale=0.5,
                  bias=hbias[:, h:h + 1]).then_inc(th_s.sem, 1)

            def block1(b):
                normed1(b)
                squares(b)
                relu_normed(b, 0)
                relu_normed(b, 1)
                rstd_rows(b)
                q_high(b)
                k_high(b)
                max_copy(b)
                for t in range(8):
                    exps(b, t)
                attn_out(b)

            def block2(c):
                normed2(c)
                residual(c, 0)
                residual(c, 1)
                pad_conv1(c, 0)
                pad_conv1(c, 1)
                conv2_first(c, 0)
                pad_conv1(c, 2)
                pad_conv1(c, 3)
                for k in range(4):
                    copy_xT(c, k)
                conv2_first(c, 1)
                copy_tu(c, 0)
                copy_tu(c, 1)
                copy_k_norms(c)
                head_exps(c)
                copy_attT(c)
                copy_wmt(c)
                copy_t(c)
                pad_sp(c, 0)
                pad_sp(c, 1)
                sp_first(c)
                pad_ci2a(c)
                gelu(c, 0)
                gelu(c, 1)
                for k in range(3):
                    spatial_tanh(c, k)
                channel_gate(c)
                spatial_tanh(c, 3)

            def both(c, b):
                normed2(c)
                residual(c, 0)
                residual(c, 1)
                pad_conv1(c, 0)
                pad_conv1(c, 1)
                conv2_first(c, 0)
                pad_conv1(c, 2)
                pad_conv1(c, 3)
                conv2_first(c, 1)
                for k in range(4):
                    copy_xT(c, k)
                normed1(b)
                squares(b)
                relu_normed(b, 0)
                copy_tu(c, 0)
                relu_normed(b, 1)
                copy_tu(c, 1)
                rstd_rows(b)
                copy_k_norms(c)
                head_exps(c)
                q_high(b)
                k_high(b)
                copy_attT(c)
                copy_wmt(c)
                copy_t(c)
                pad_sp(c, 0)
                pad_sp(c, 1)
                sp_first(c)
                pad_ci2a(c)
                max_copy(b)
                for t in range(3):
                    exps(b, t)
                gelu(c, 0)
                gelu(c, 1)
                for t in range(3, 7):
                    exps(b, t)
                channel_gate(c)
                for k in range(3):
                    spatial_tanh(c, k)
                exps(b, 7)
                spatial_tanh(c, 3)
                attn_out(b)

            act.wait_ge(s_w1, 16)
            a(lnmat[:, PD:PD + 1], par("ln_b"), ID).then_inc(s_ln, 1)
            block1(0)
            act.wait_ge(s_w2, 16)
            act.wait_ge(s_su, 15)
            act.wait_ge(s_fill, FILLS)
            with act.Fori(1, B) as i:
                act.wait_ge(x2_s.sem, x2_s.at(i, 0))
                act.wait_ge(oo_s.sem, oo_s.at(i - 1, 0))
                both(i - 1, i)
            act.wait_ge(x2_s.sem, x2_s.at(B, 0))
            act.wait_ge(oo_s.sem, oo_s.at(B - 1, 0))
            block2(B - 1)

        @block.gpsimd
        def _(pool):
            g = nc.gpsimd

            def rsqrt(dst, src):
                n = src.shape[-1]
                return g.tensor_tensor(dst, src, mhalf[0:src.shape[0], 0:n], ALU.pow)

            def group_rstd(i, b):
                pool.wait_ge(gmm[i].sem, gmm[i].at(b, 3))
                rsqrt(gr[i][:], gvar[i][:]).then_inc(grr[i].sem, 1)

            def pixel_rstd(b):
                pool.wait_ge(pv_s.sem, pv_s.at(b, 1))
                rsqrt(rT[:], pv8[:]).then_inc(rT_s.sem, 1)

            def inverse_norms(c):
                pool.wait_ge(nrm_s.sem, nrm_s.at(c, 1))
                rsqrt(rn[:], nrm[:]).then_inc(rn_s.sem, 1)

            def block1(b):
                group_rstd(0, b)
                pixel_rstd(b)
                group_rstd(1, b)

            def block2(c):
                inverse_norms(c)

            def both(c, b):
                group_rstd(0, b)
                pixel_rstd(b)
                inverse_norms(c)
                group_rstd(1, b)

            g.memset(xn[:], 1.0).then_inc(s_fill, 1)
            g.memset(mhalf[:], -0.5).then_inc(s_fill, 1)
            pool.wait_ge(s_fill, 2)
            pool.wait_ge(s_su, 2)
            rsqrt(isd1[:], var1[:]).then_inc(s_isd, 1)
            rsqrt(isd2[:], var2[:]).then_inc(s_isd, 1)
            block1(0)
            g.memset(tp[:], 0.0).then_inc(s_fill, 1)
            g.memset(up[:], 0.0).then_inc(s_fill, 1)
            g.memset(cp[:, 0, :, :], 0.0).then_inc(s_fill, 1)
            g.memset(cp[:, 1, :, :], 0.0).then_inc(s_fill, 1)
            g.memset(spp[:], 0.0).then_inc(s_fill, 1)
            g.memset(pr4[:], 0.0).then_inc(s_fill, 1)
            pool.wait_ge(s_w2, 16)
            with pool.Fori(1, B) as i:
                pool.wait_ge(x2_s.sem, x2_s.at(i, 0))
                pool.wait_ge(oo_s.sem, oo_s.at(i - 1, 0))
                both(i - 1, i)
            pool.wait_ge(x2_s.sem, x2_s.at(B, 0))
            pool.wait_ge(oo_s.sem, oo_s.at(B - 1, 0))
            block2(B - 1)


def constants():
    k = np.arange(CH)
    same_group = (k[:, None] // GROUP) == (k[None, :] // GROUP)
    same_head = (k[:, None] // HD) == (k[None, :] // HD)
    center, mean_rows = np.zeros((SPN, SPN)), np.zeros((SPN, 2))
    pick_den, pick_one = np.zeros((SPN + 1, 2)), np.zeros((SPN + 1, 1))
    pick_one[SPN] = 1.0
    for n in range(2):
        rows = slice(n * SP2, n * SP2 + PD)
        center[rows, rows] = np.eye(PD) - 1.0 / PD
        mean_rows[rows, n] = 1.0 / PD
        pick_den[n * SP2 + PD, n] = 1.0
    return {
        "ident": np.eye(P), "gavg": same_group / (4 * GROUP), "center": center,
        "mean_rows": mean_rows, "ones": np.ones((P, CH)), "pick_den": pick_den, "pick_one": pick_one,
        "mask": np.where(same_head, 0.0, MASKED),
    }


def pack(p):
    f = {k: np.asarray(v) for k, v in p.items()}
    l0 = {k[8:]: v for k, v in f.items() if k.startswith("L0_conv_")}
    l1 = {k[8:]: v for k, v in f.items() if k.startswith("L1_conv_")}

    def halves(m):
        return m.reshape(2, CH, -1).transpose(1, 0, 2).reshape(CH, -1)

    def split_sp(m):
        o = np.zeros(m.shape[:-1] + (SPN,), np.float32)
        o[..., 0:PD], o[..., SP2:SPN] = m[..., 0:PD], m[..., PD:2 * PD]
        return o

    w2a = l1["ci2a_w"][:, 0]
    w_ci2a = np.zeros((3, C6, 3, C6), np.float32)
    for ch in range(C6):
        w_ci2a[:, ch, :, ch] = w2a[ch].T
    w_ci2b = np.zeros((4, C6, 7, 2), np.float32)
    for dx in range(7):
        w_ci2b[dx % 4, :, :, dx // 4] = l1["ci2b_w"][:, 0, :, dx]
    w_spo = np.zeros((SPN, 2, C), np.float32)
    for n in range(2):
        w_spo[n * SP2:n * SP2 + PD, n] = l1["sp_out_w"][:, :, 0, 0].T
    ci2cT = l1["ci2c_w"][:, :, 0, 0].T
    blocks = {
        **constants(),
        "ln_w": l0["ln_w"][:, None], "ln_b": l0["ln_b"][:, None], "wqkvT": l0["w_qkv"].T,
        "bn1": np.stack([l0[f"bn1_{k}"] for k in "gbmv"], 1),
        "wproj": halves(l0["w_proj"]),
        "bn2": np.concatenate([halves(l0[f"bn2_{k}"][:, None]) for k in "gbmv"], 1),
        "wqkT": halves(l1["qkv_w"][0:2 * C].T), "wv": halves(l1["qkv_w"][2 * C:]),
        "wdw1T": halves(l1["dw1_w"][:, :, 0, 0].T), "wcpT": halves(l1["cp_in_w"][:, :, 0, 0].T),
        "wdw2": halves(l1["dw2_w"].reshape(C, 9)), "bdw2": halves(l1["dw2_b"][:, None]),
        "temp": halves(np.repeat(l1["temperature"].reshape(-1), HD)[:, None]),
        "w_ci1": np.tile(l1["ci1_w"][:, :, 0, 0].T, (4, 4)), "b_ci1": np.tile(l1["ci1_b"], 4)[:, None],
        "w_ci2a": w_ci2a.reshape(CH, 3 * C6), "b_ci2a": np.tile(l1["ci2a_b"], 4)[:, None],
        "ci2cT": np.tile(ci2cT, (4, 1)), "w_ci2b": w_ci2b.reshape(P, 14),
        "ci2cT_rep": np.tile(ci2cT, (1, 4)), "b_ci2b": l1["ci2b_b"][:, None],
        "b_ci2c": np.tile(l1["ci2c_b"], 4)[:, None], "wcoT": np.tile(l1["cp_out_w"][:, :, 0, 0].T, (4, 1)),
        "half_biases": np.concatenate([halves(l1["sp_out_b"][:, None]), halves(l1["cp_out_b"][:, None])], 1),
        "w_spi": split_sp(halves(l1["sp_in_w"][:, :, 0, 0].T).reshape(CH, 2, 2 * PD)).reshape(CH, -1),
        "b_spi": split_sp(l1["sp_in_b"])[:, None], "w_spdw": split_sp(l1["sp_dw_w"].reshape(2 * PD, 9).T).T,
        "b_spdw": split_sp(l1["sp_dw_b"])[:, None], "w_spo": w_spo.reshape(SPN, 2 * C),
        "w_pr": halves(l1["proj_w"].T), "b_pr": halves(l1["proj_b"][:, None]),
    }
    out = np.zeros((P, NW), np.float32)
    for name, (parts, off, cols) in AT.items():
        if name.startswith("row_"):
            out[CH, off:off + cols] = l1[name[4:]]
        else:
            out[0:parts, off:off + cols] = blocks[name]
    return out


def kernel(**inputs):
    import concourse.bacc as bacc
    from concourse.bass_utils import run_bass_kernel_spmd

    x = np.ascontiguousarray(np.asarray(inputs["x"]).reshape(B, 2, CH, N))
    params = pack({k: v for k, v in inputs.items() if k != "x"})
    nc = bacc.Bacc("TRN2", target_bir_lowering=False, num_devices=1)
    x_ap = nc.dram_tensor("x_dram", x.shape, F32, kind="ExternalInput").ap()
    p_ap = nc.dram_tensor("params_dram", params.shape, F32, kind="ExternalInput").ap()
    o_ap = nc.dram_tensor("out_dram", x.shape, F32, kind="ExternalOutput").ap()
    build(nc, x_ap, p_ap, o_ap)
    r = run_bass_kernel_spmd(nc, [{"x_dram": x, "params_dram": params}], core_ids=[0])
    return r.results[0]["out_dram"].reshape(B, C, HH, WW)
```
